# Optimizing a Trainium2 kernel written in Bass

```python
import numpy as np
import jax
import jax.numpy as jnp

def _softmax(x, axis=-1):
    return jax.nn.softmax(x, axis=axis)

def _gelu(x):
    return jax.nn.gelu(x, approximate=True)

def _silu(x):
    return jax.nn.silu(x)

def _sigmoid(x):
    return jax.nn.sigmoid(x)

def _layernorm(x, axis=-1, eps=1e-05):
    m = jnp.mean(x, axis=axis, keepdims=True)
    v = jnp.var(x, axis=axis, keepdims=True)
    return (x - m) / jnp.sqrt(v + eps)

def _scatter_add(tgt, idx, src, axis=0):
    return tgt.at[idx].add(src)

def _segment_sum(src, seg, n):
    return jax.ops.segment_sum(src, seg, n)
kernel_name = 'mk_adaln_d2_jaxref_r8_ff32f7'

def setup_inputs(seed: int=0):
    np.random.seed(seed)
    _w = jnp.asarray

    def _L0_attn_setup():
        import math
        import jax, jax.numpy as jnp
        import numpy as np
        B, T, E = (2, 256, 512)
        H, HKV = (32, 8)
        DH = E // H
        G = H // HKV
        ROPE_THETA = 500000.0
        ROPE_FACTOR = 32.0
        HI_FREQ_FACTOR = 4.0
        LO_FREQ_FACTOR = 1.0
        ORIG_CTX = 1024

        def _rope_cos_sin(t_len):
            inv_freq = 1.0 / ROPE_THETA ** (jnp.arange(0, DH, 2, dtype=jnp.float32) / DH)
            wavelen = 2.0 * math.pi / inv_freq
            cut_lo = ORIG_CTX / HI_FREQ_FACTOR
            cut_hi = ORIG_CTX / LO_FREQ_FACTOR
            inv_freq = jnp.where(wavelen > cut_hi, inv_freq / ROPE_FACTOR, inv_freq)
            smooth = (ORIG_CTX / wavelen - LO_FREQ_FACTOR) / (HI_FREQ_FACTOR - LO_FREQ_FACTOR)
            smoothed = (1.0 - smooth) * inv_freq / ROPE_FACTOR + smooth * inv_freq
            is_medium = ~(wavelen < cut_hi) & ~(wavelen > cut_lo)
            inv_freq = jnp.where(is_medium, smoothed, inv_freq)
            pos = jnp.arange(t_len, dtype=jnp.float32)
            freqs = pos[:, None] * inv_freq[None, :]
            emb = jnp.concatenate([freqs, freqs], axis=-1)
            return (jnp.cos(emb), jnp.sin(emb))

        def _rotate_half(x):
            x1, x2 = jnp.split(x, 2, axis=-1)
            return jnp.concatenate([-x2, x1], axis=-1)
        key = jax.random.key(seed)
        kx, kq, kk, kv, ko = jax.random.split(key, 5)
        w = lambda k, shape: jax.random.normal(k, shape, jnp.float32) * 0.02
        return {'x': jax.random.normal(kx, (B, T, E), jnp.float32), 'Wq': w(kq, (E, E)), 'Wk': w(kk, (HKV * DH, E)), 'Wv': w(kv, (HKV * DH, E)), 'Wo': w(ko, (E, E))}
    _L0_attn_in = _L0_attn_setup()

    def _L0_ffn_setup():
        import jax, jax.numpy as jnp
        import numpy as np
        HID, INT, LAT, NE, K = (512, 1024, 256, 8, 2)
        LN_EPS = 1e-05

        def _layernorm(x, gamma, beta):
            mu = jnp.mean(x, axis=-1, keepdims=True)
            var = jnp.var(x, axis=-1, keepdims=True)
            return (x - mu) * jax.lax.rsqrt(var + LN_EPS) * gamma + beta
        key = jax.random.key(seed)
        ks = jax.random.split(key, 8)
        s = lambda d: 1.0 / np.sqrt(d)
        return {'hidden_states': jax.random.normal(ks[0], (4, 256, HID), jnp.float32), 'gate_w': jax.random.normal(ks[1], (HID, NE), jnp.float32) * s(HID), 'up_w': jax.random.normal(ks[2], (HID, INT), jnp.float32) * s(HID), 'down_w': jax.random.normal(ks[3], (INT, HID), jnp.float32) * s(INT), 'fc1_w': jax.random.normal(ks[4], (HID, LAT), jnp.float32) * s(HID), 'fc2_w': jax.random.normal(ks[5], (LAT, HID), jnp.float32) * s(LAT), 'expert_w': jax.random.normal(ks[6], (LAT, LAT), jnp.float32), 'ln_gamma': jnp.ones((HID,), jnp.float32), 'ln_beta': jnp.zeros((HID,), jnp.float32)}
    _L0_ffn_in = _L0_ffn_setup()
    _L0_c = _w((lambda *s: np.random.randn(*s).astype(np.float32) * 0.05)(1, 512))
    _L0_wmod = _w((lambda *s: np.random.randn(*s).astype(np.float32) * 0.05)(512, 6 * 512) * 512 ** (-0.5))

    def _L1_attn_setup():
        import jax, jax.numpy as jnp
        import numpy as np
        HID = 512
        DM = 128
        DIN = 2 * DM
        DST = 16
        HD = 64
        NH = DIN // HD
        DCONV = 7
        CONV_DIM = DIN + 2 * DST
        DIN_PROJ = 2 * DIN + 2 * DST + 2 * NH
        SEQ, BATCH = (256, 4)

        def _causal_conv(x, w, b):
            y = jax.lax.conv_general_dilated(jnp.transpose(x, (0, 2, 1)), w, (1,), [(DCONV - 1, 0)], feature_group_count=CONV_DIM, dimension_numbers=('NCH', 'OIH', 'NCH'))
            return jnp.transpose(y, (0, 2, 1)) + b

        def _ssm_scan(x, dt, A, B, C):
            dA = jnp.exp(dt * A)
            dBx = dt[..., None] * x

            def step(h, t):
                dA_t, dBx_t, B_t, C_t = t
                h = dA_t[:, :, None, None] * h + dBx_t[..., None] * B_t[:, None, None, :]
                y = jnp.einsum('bhpn,bn->bhp', h, C_t)
                return (h, y)
            h0 = jnp.zeros((x.shape[0], NH, HD, DST), x.dtype)
            _, ys = jax.lax.scan(step, h0, (jnp.moveaxis(dA, 1, 0), jnp.moveaxis(dBx, 1, 0), jnp.moveaxis(B, 1, 0), jnp.moveaxis(C, 1, 0)))
            return jnp.moveaxis(ys, 0, 1)

        def _hydra(u, in_w, conv_w, conv_b, dt_bias, A_log, D, fcD_w, norm_w, out_w):
            b, l, _ = u.shape
            zxbcdt = u @ in_w.T
            z = zxbcdt[..., :DIN]
            xBC = zxbcdt[..., DIN:DIN + CONV_DIM]
            dt2 = zxbcdt[..., DIN + CONV_DIM:]
            dt_fw = jax.nn.softplus(dt2[..., :NH] + dt_bias)
            dt_bw = jax.nn.softplus(jnp.flip(dt2[..., NH:], 1) + dt_bias)
            xBC = jax.nn.silu(_causal_conv(xBC, conv_w, conv_b))
            xs = xBC[..., :DIN]
            Bm = xBC[..., DIN:DIN + DST]
            Cm = xBC[..., DIN + DST:]
            A = -jnp.exp(A_log)
            x4 = xs.reshape(b, l, NH, HD)
            y_fw = _ssm_scan(x4, dt_fw, A, Bm, Cm).reshape(b, l, DIN)
            y_bw = jnp.flip(_ssm_scan(jnp.flip(x4, 1), dt_bw, A, jnp.flip(Bm, 1), jnp.flip(Cm, 1)).reshape(b, l, DIN), 1)
            zero = jnp.zeros((b, 1, DIN), u.dtype)
            y = jnp.concatenate([zero, y_fw[:, :-1]], 1) + jnp.concatenate([y_bw[:, 1:], zero], 1)
            y = y + xs * jnp.repeat(xs @ fcD_w.T + D, HD, axis=-1)
            yz = y * jax.nn.silu(z)
            y = yz * jax.lax.rsqrt(jnp.mean(jnp.square(yz), -1, keepdims=True) + 1e-05) * norm_w
            return y @ out_w.T
        key = jax.random.key(seed)
        ks = jax.random.split(key, 12)
        rn = lambda k, shape, s=0.02: jax.random.normal(k, shape, jnp.float32) * s
        dt = jnp.exp(jax.random.uniform(ks[5], (NH,), jnp.float32, np.log(0.001), np.log(0.1)))
        return dict(x=jax.random.normal(ks[0], (SEQ, BATCH, HID), jnp.float32), w_down=rn(ks[1], (DM, HID)), b_down=jnp.zeros((DM,), jnp.float32), w_up=rn(ks[2], (HID, DM)), b_up=jnp.zeros((HID,), jnp.float32), gate1=jnp.asarray(0.6, jnp.float32), hy_in_w=rn(ks[3], (DIN_PROJ, DM)), hy_conv_w=rn(ks[4], (CONV_DIM, 1, DCONV), 0.2), hy_conv_b=jnp.zeros((CONV_DIM,), jnp.float32), hy_dt_bias=jnp.log(jnp.expm1(dt)), hy_A_log=jnp.log(jax.random.uniform(ks[6], (NH,), jnp.float32, 1.0, 16.0)), hy_D=jnp.ones((NH,), jnp.float32), hy_fcD_w=rn(ks[7], (NH, DIN)), hy_norm_w=jnp.ones((DIN,), jnp.float32), hy_out_w=rn(ks[8], (DM, DIN)))
    _L1_attn_in = _L1_attn_setup()

    def _L1_ffn_setup():
        import jax, jax.numpy as jnp
        import numpy as np
        DIM = 512
        HID = 1376
        R = 16
        SCALING = 32.0 / 16.0

        def _lora_linear(x, w, a, b):
            base = jnp.einsum('bsd,od->bso', x, w)
            low = jnp.einsum('bsr,or->bso', jnp.einsum('bsd,rd->bsr', x, a), b)
            return base + low * SCALING
        key = jax.random.key(seed)
        ks = jax.random.split(key, 10)
        s_in = 1.0 / np.sqrt(DIM)
        s_hid = 1.0 / np.sqrt(HID)
        return {'x': jax.random.normal(ks[0], (4, 256, DIM), jnp.float32), 'w1': jax.random.normal(ks[1], (HID, DIM), jnp.float32) * s_in, 'w3': jax.random.normal(ks[2], (HID, DIM), jnp.float32) * s_in, 'w2': jax.random.normal(ks[3], (DIM, HID), jnp.float32) * s_hid, 'lora_A1': jax.random.normal(ks[4], (R, DIM), jnp.float32) * s_in, 'lora_B1': jax.random.normal(ks[5], (HID, R), jnp.float32) * 0.02, 'lora_A3': jax.random.normal(ks[6], (R, DIM), jnp.float32) * s_in, 'lora_B3': jax.random.normal(ks[7], (HID, R), jnp.float32) * 0.02, 'lora_A2': jax.random.normal(ks[8], (R, HID), jnp.float32) * s_hid, 'lora_B2': jax.random.normal(ks[9], (DIM, R), jnp.float32) * 0.02}
    _L1_ffn_in = _L1_ffn_setup()
    _L1_c = _w((lambda *s: np.random.randn(*s).astype(np.float32) * 0.05)(1, 512))
    _L1_wmod = _w((lambda *s: np.random.randn(*s).astype(np.float32) * 0.05)(512, 6 * 512) * 512 ** (-0.5))
    _d = {'L0_attn_x': _L0_attn_in['x'], 'L0_attn_Wq': _L0_attn_in['Wq'], 'L0_attn_Wk': _L0_attn_in['Wk'], 'L0_attn_Wv': _L0_attn_in['Wv'], 'L0_attn_Wo': _L0_attn_in['Wo'], 'L0_ffn_gate_w': _L0_ffn_in['gate_w'], 'L0_ffn_up_w': _L0_ffn_in['up_w'], 'L0_ffn_down_w': _L0_ffn_in['down_w'], 'L0_ffn_fc1_w': _L0_ffn_in['fc1_w'], 'L0_ffn_fc2_w': _L0_ffn_in['fc2_w'], 'L0_ffn_expert_w': _L0_ffn_in['expert_w'], 'L0_ffn_ln_gamma': _L0_ffn_in['ln_gamma'], 'L0_ffn_ln_beta': _L0_ffn_in['ln_beta'], 'L0_c': _L0_c, 'L0_wmod': _L0_wmod, 'L1_attn_w_down': _L1_attn_in['w_down'], 'L1_attn_b_down': _L1_attn_in['b_down'], 'L1_attn_w_up': _L1_attn_in['w_up'], 'L1_attn_b_up': _L1_attn_in['b_up'], 'L1_attn_gate1': _L1_attn_in['gate1'], 'L1_attn_hy_in_w': _L1_attn_in['hy_in_w'], 'L1_attn_hy_conv_w': _L1_attn_in['hy_conv_w'], 'L1_attn_hy_conv_b': _L1_attn_in['hy_conv_b'], 'L1_attn_hy_dt_bias': _L1_attn_in['hy_dt_bias'], 'L1_attn_hy_A_log': _L1_attn_in['hy_A_log'], 'L1_attn_hy_D': _L1_attn_in['hy_D'], 'L1_attn_hy_fcD_w': _L1_attn_in['hy_fcD_w'], 'L1_attn_hy_norm_w': _L1_attn_in['hy_norm_w'], 'L1_attn_hy_out_w': _L1_attn_in['hy_out_w'], 'L1_ffn_w1': _L1_ffn_in['w1'], 'L1_ffn_w3': _L1_ffn_in['w3'], 'L1_ffn_w2': _L1_ffn_in['w2'], 'L1_ffn_lora_A1': _L1_ffn_in['lora_A1'], 'L1_ffn_lora_B1': _L1_ffn_in['lora_B1'], 'L1_ffn_lora_A3': _L1_ffn_in['lora_A3'], 'L1_ffn_lora_B3': _L1_ffn_in['lora_B3'], 'L1_ffn_lora_A2': _L1_ffn_in['lora_A2'], 'L1_ffn_lora_B2': _L1_ffn_in['lora_B2'], 'L1_c': _L1_c, 'L1_wmod': _L1_wmod}
    _x0 = _d['L0_attn_x']
    _d['L0_attn_x'] = jax.random.normal(jax.random.fold_in(jax.random.key(seed), 1), (1, 1024, 512), dtype=_x0.dtype)
    del _x0
    return _d

def reference(L0_attn_x, L0_attn_Wq, L0_attn_Wk, L0_attn_Wv, L0_attn_Wo, L0_ffn_gate_w, L0_ffn_up_w, L0_ffn_down_w, L0_ffn_fc1_w, L0_ffn_fc2_w, L0_ffn_expert_w, L0_ffn_ln_gamma, L0_ffn_ln_beta, L0_c, L0_wmod, L1_attn_w_down, L1_attn_b_down, L1_attn_w_up, L1_attn_b_up, L1_attn_gate1, L1_attn_hy_in_w, L1_attn_hy_conv_w, L1_attn_hy_conv_b, L1_attn_hy_dt_bias, L1_attn_hy_A_log, L1_attn_hy_D, L1_attn_hy_fcD_w, L1_attn_hy_norm_w, L1_attn_hy_out_w, L1_ffn_w1, L1_ffn_w3, L1_ffn_w2, L1_ffn_lora_A1, L1_ffn_lora_B1, L1_ffn_lora_A3, L1_ffn_lora_B3, L1_ffn_lora_A2, L1_ffn_lora_B2, L1_c, L1_wmod):

    def _L0_attn_ref(x, Wq, Wk, Wv, Wo):
        import math
        import jax, jax.numpy as jnp
        import numpy as np
        B, T, E = (2, 256, 512)
        H, HKV = (32, 8)
        DH = E // H
        G = H // HKV
        ROPE_THETA = 500000.0
        ROPE_FACTOR = 32.0
        HI_FREQ_FACTOR = 4.0
        LO_FREQ_FACTOR = 1.0
        ORIG_CTX = 1024

        def _rope_cos_sin(t_len):
            inv_freq = 1.0 / ROPE_THETA ** (jnp.arange(0, DH, 2, dtype=jnp.float32) / DH)
            wavelen = 2.0 * math.pi / inv_freq
            cut_lo = ORIG_CTX / HI_FREQ_FACTOR
            cut_hi = ORIG_CTX / LO_FREQ_FACTOR
            inv_freq = jnp.where(wavelen > cut_hi, inv_freq / ROPE_FACTOR, inv_freq)
            smooth = (ORIG_CTX / wavelen - LO_FREQ_FACTOR) / (HI_FREQ_FACTOR - LO_FREQ_FACTOR)
            smoothed = (1.0 - smooth) * inv_freq / ROPE_FACTOR + smooth * inv_freq
            is_medium = ~(wavelen < cut_hi) & ~(wavelen > cut_lo)
            inv_freq = jnp.where(is_medium, smoothed, inv_freq)
            pos = jnp.arange(t_len, dtype=jnp.float32)
            freqs = pos[:, None] * inv_freq[None, :]
            emb = jnp.concatenate([freqs, freqs], axis=-1)
            return (jnp.cos(emb), jnp.sin(emb))

        def _rotate_half(x):
            x1, x2 = jnp.split(x, 2, axis=-1)
            return jnp.concatenate([-x2, x1], axis=-1)
        b, t, _ = x.shape
        q = (x @ Wq.T).reshape(b, t, H, DH).transpose(0, 2, 1, 3)
        k = (x @ Wk.T).reshape(b, t, HKV, DH).transpose(0, 2, 1, 3)
        v = (x @ Wv.T).reshape(b, t, HKV, DH).transpose(0, 2, 1, 3)
        cos, sin = _rope_cos_sin(t)
        cos = cos.astype(x.dtype)[None, None]
        sin = sin.astype(x.dtype)[None, None]
        q = q * cos + _rotate_half(q) * sin
        k = k * cos + _rotate_half(k) * sin
        qg = q.reshape(b, HKV, G, t, DH)
        scores = jnp.einsum('bhgtd,bhkd->bhgtk', qg.astype(jnp.float32), k.astype(jnp.float32)) / math.sqrt(DH)
        causal = jnp.tril(jnp.ones((t, t), dtype=bool))
        scores = jnp.where(causal[None, None, None], scores, jnp.finfo(jnp.float32).min)
        attn = jax.nn.softmax(scores, axis=-1).astype(x.dtype)
        ctx = jnp.einsum('bhgtk,bhkd->bhgtd', attn, v)
        out = ctx.reshape(b, H, t, DH).transpose(0, 2, 1, 3).reshape(b, t, E)
        return out @ Wo.T

    def _L0_ffn_ref(hidden_states, gate_w, up_w, down_w, fc1_w, fc2_w, expert_w, ln_gamma, ln_beta):
        import jax, jax.numpy as jnp
        import numpy as np
        HID, INT, LAT, NE, K = (512, 1024, 256, 8, 2)
        LN_EPS = 1e-05

        def _layernorm(x, gamma, beta):
            mu = jnp.mean(x, axis=-1, keepdims=True)
            var = jnp.var(x, axis=-1, keepdims=True)
            return (x - mu) * jax.lax.rsqrt(var + LN_EPS) * gamma + beta
        logits = jnp.einsum('bsh,he->bse', hidden_states, gate_w)
        routing_weights, selected_experts = jax.lax.top_k(logits, K)
        h = jax.nn.relu(jnp.einsum('bsh,hi->bsi', hidden_states, up_w)) ** 2
        shared_out = jnp.einsum('bsi,ih->bsh', h, down_w)
        x_latent = jnp.einsum('bsh,hl->bsl', hidden_states, fc1_w)
        expert_out = jnp.einsum('bsl,lm->bsm', x_latent, expert_w)
        moe_out = expert_out * jnp.sum(routing_weights, axis=-1, keepdims=True)
        routed_out = jnp.einsum('bsl,lh->bsh', moe_out, fc2_w)
        return _layernorm(shared_out + routed_out, ln_gamma, ln_beta)

    def _L1_attn_ref(x, w_down, b_down, w_up, b_up, gate1, hy_in_w, hy_conv_w, hy_conv_b, hy_dt_bias, hy_A_log, hy_D, hy_fcD_w, hy_norm_w, hy_out_w):
        import jax, jax.numpy as jnp
        import numpy as np
        HID = 512
        DM = 128
        DIN = 2 * DM
        DST = 16
        HD = 64
        NH = DIN // HD
        DCONV = 7
        CONV_DIM = DIN + 2 * DST
        DIN_PROJ = 2 * DIN + 2 * DST + 2 * NH
        SEQ, BATCH = (256, 4)

        def _causal_conv(x, w, b):
            y = jax.lax.conv_general_dilated(jnp.transpose(x, (0, 2, 1)), w, (1,), [(DCONV - 1, 0)], feature_group_count=CONV_DIM, dimension_numbers=('NCH', 'OIH', 'NCH'))
            return jnp.transpose(y, (0, 2, 1)) + b

        def _ssm_scan(x, dt, A, B, C):
            dA = jnp.exp(dt * A)
            dBx = dt[..., None] * x

            def step(h, t):
                dA_t, dBx_t, B_t, C_t = t
                h = dA_t[:, :, None, None] * h + dBx_t[..., None] * B_t[:, None, None, :]
                y = jnp.einsum('bhpn,bn->bhp', h, C_t)
                return (h, y)
            h0 = jnp.zeros((x.shape[0], NH, HD, DST), x.dtype)
            _, ys = jax.lax.scan(step, h0, (jnp.moveaxis(dA, 1, 0), jnp.moveaxis(dBx, 1, 0), jnp.moveaxis(B, 1, 0), jnp.moveaxis(C, 1, 0)))
            return jnp.moveaxis(ys, 0, 1)

        def _hydra(u, in_w, conv_w, conv_b, dt_bias, A_log, D, fcD_w, norm_w, out_w):
            b, l, _ = u.shape
            zxbcdt = u @ in_w.T
            z = zxbcdt[..., :DIN]
            xBC = zxbcdt[..., DIN:DIN + CONV_DIM]
            dt2 = zxbcdt[..., DIN + CONV_DIM:]
            dt_fw = jax.nn.softplus(dt2[..., :NH] + dt_bias)
            dt_bw = jax.nn.softplus(jnp.flip(dt2[..., NH:], 1) + dt_bias)
            xBC = jax.nn.silu(_causal_conv(xBC, conv_w, conv_b))
            xs = xBC[..., :DIN]
            Bm = xBC[..., DIN:DIN + DST]
            Cm = xBC[..., DIN + DST:]
            A = -jnp.exp(A_log)
            x4 = xs.reshape(b, l, NH, HD)
            y_fw = _ssm_scan(x4, dt_fw, A, Bm, Cm).reshape(b, l, DIN)
            y_bw = jnp.flip(_ssm_scan(jnp.flip(x4, 1), dt_bw, A, jnp.flip(Bm, 1), jnp.flip(Cm, 1)).reshape(b, l, DIN), 1)
            zero = jnp.zeros((b, 1, DIN), u.dtype)
            y = jnp.concatenate([zero, y_fw[:, :-1]], 1) + jnp.concatenate([y_bw[:, 1:], zero], 1)
            y = y + xs * jnp.repeat(xs @ fcD_w.T + D, HD, axis=-1)
            yz = y * jax.nn.silu(z)
            y = yz * jax.lax.rsqrt(jnp.mean(jnp.square(yz), -1, keepdims=True) + 1e-05) * norm_w
            return y @ out_w.T
        x_init = x
        h = x @ w_down.T + b_down
        h = jnp.transpose(h, (1, 0, 2))
        h = jax.nn.gelu(h, approximate=False)
        xmid = h
        hp = (hy_in_w, hy_conv_w, hy_conv_b, hy_dt_bias, hy_A_log, hy_D, hy_fcD_w, hy_norm_w, hy_out_w)
        h = _hydra(h, *hp)
        h = _hydra(h, *hp)
        alpha = jax.nn.sigmoid(gate1)
        h = alpha * xmid + (1.0 - alpha) * h
        h = xmid + h
        h = h @ w_up.T + b_up
        return x_init + jnp.transpose(h, (1, 0, 2))

    def _L1_ffn_ref(x, w1, w3, w2, lora_A1, lora_B1, lora_A3, lora_B3, lora_A2, lora_B2):
        import jax, jax.numpy as jnp
        import numpy as np
        DIM = 512
        HID = 1376
        R = 16
        SCALING = 32.0 / 16.0

        def _lora_linear(x, w, a, b):
            base = jnp.einsum('bsd,od->bso', x, w)
            low = jnp.einsum('bsr,or->bso', jnp.einsum('bsd,rd->bsr', x, a), b)
            return base + low * SCALING
        h1 = _lora_linear(x, w1, lora_A1, lora_B1)
        h3 = _lora_linear(x, w3, lora_A3, lora_B3)
        g = jax.nn.silu(h1) * h3
        return _lora_linear(g, w2, lora_A2, lora_B2)
    x = L0_attn_x
    mod = (_silu(L0_c) @ L0_wmod).reshape(L0_c.shape[0], 6, 1, -1)
    sa, ca, ga, sb, cb, gb = (mod[:, 0], mod[:, 1], mod[:, 2], mod[:, 3], mod[:, 4], mod[:, 5])
    ga = (2 * (ga >= 0) - 1) * jnp.maximum(jnp.abs(ga), 0.25)
    gb = (2 * (gb >= 0) - 1) * jnp.maximum(jnp.abs(gb), 0.25)
    h = _layernorm(x, axis=-1) * (1 + ca) + sa
    x = x + ga * _L0_attn_ref(h, L0_attn_Wq, L0_attn_Wk, L0_attn_Wv, L0_attn_Wo)
    h = _layernorm(x, axis=-1) * (1 + cb) + sb
    x = x + gb * _L0_ffn_ref(h, L0_ffn_gate_w, L0_ffn_up_w, L0_ffn_down_w, L0_ffn_fc1_w, L0_ffn_fc2_w, L0_ffn_expert_w, L0_ffn_ln_gamma, L0_ffn_ln_beta)
    mod = (_silu(L1_c) @ L1_wmod).reshape(L1_c.shape[0], 6, 1, -1)
    sa, ca, ga, sb, cb, gb = (mod[:, 0], mod[:, 1], mod[:, 2], mod[:, 3], mod[:, 4], mod[:, 5])
    ga = (2 * (ga >= 0) - 1) * jnp.maximum(jnp.abs(ga), 0.25)
    gb = (2 * (gb >= 0) - 1) * jnp.maximum(jnp.abs(gb), 0.25)
    h = _layernorm(x, axis=-1) * (1 + ca) + sa
    x = x + ga * _L1_attn_ref(h, L1_attn_w_down, L1_attn_b_down, L1_attn_w_up, L1_attn_b_up, L1_attn_gate1, L1_attn_hy_in_w, L1_attn_hy_conv_w, L1_attn_hy_conv_b, L1_attn_hy_dt_bias, L1_attn_hy_A_log, L1_attn_hy_D, L1_attn_hy_fcD_w, L1_attn_hy_norm_w, L1_attn_hy_out_w)
    h = _layernorm(x, axis=-1) * (1 + cb) + sb
    x = x + gb * _L1_ffn_ref(h, L1_ffn_w1, L1_ffn_w3, L1_ffn_w2, L1_ffn_lora_A1, L1_ffn_lora_B1, L1_ffn_lora_A3, L1_ffn_lora_B3, L1_ffn_lora_A2, L1_ffn_lora_B2)
    return x

_drawn_inputs = setup_inputs


def setup_inputs(seed=0):
    import zlib

    import numpy as np

    out = dict(_drawn_inputs(seed))
    spreads = {'L0_ffn_ln_gamma': (1.0, 0.6),
     'L0_ffn_ln_beta': (0.0, 0.961),
     'L1_attn_b_down': (0.0, 0.8),
     'L1_attn_b_up': (0.0, 0.976),
     'L1_attn_hy_conv_b': (0.0, 2.0),
     'L1_attn_hy_D': (1.0, 0.6),
     'L1_attn_hy_norm_w': (1.0, 0.6)}
    factors = {'L0_attn_Wq': 8.0,
     'L0_attn_Wk': 8.0,
     'L0_attn_Wv': 8.0,
     'L0_attn_Wo': 8.0,
     'L1_attn_hy_in_w': 8.0,
     'L1_attn_hy_conv_w': 8.0,
     'L1_attn_hy_fcD_w': 8.0,
     'L1_attn_hy_out_w': 8.0,
     'L0_ffn_gate_w': 14.587,
     'L0_ffn_up_w': 8.0,
     'L0_ffn_down_w': 8.0,
     'L1_ffn_lora_A1': 6.839,
     'L1_ffn_lora_B1': 6.852,
     'L1_ffn_lora_A3': 6.721,
     'L1_ffn_lora_B3': 6.791,
     'L1_ffn_lora_A2': 6.817,
     'L1_ffn_lora_B2': 6.784}
    for name, (base, spread) in spreads.items():
        noise = np.random.default_rng([zlib.crc32(name.encode()), seed]).standard_normal(out[name].shape)
        drawn = base * np.exp(spread * noise) if base else spread * noise
        out[name] = jnp.asarray(drawn.astype(out[name].dtype))
    for name, factor in factors.items():
        out[name] = (out[name] * factor).astype(out[name].dtype)
    return out
```

```python
from contextlib import ExitStack

import concourse.bass as bass
from concourse import mybir

F32 = mybir.dt.float32
F32R = mybir.dt.float32r
BF16 = mybir.dt.bfloat16
ALU = mybir.AluOpType
ACT = mybir.ActivationFunctionType
AXX = mybir.AxisListType.X

P = 128
T = 1024
D = 512
NT = T // P
KC = D // P
HALF = T // 2
NKV, G, DH = 8, 4, 16
KROWS = 6 * DH
EPS = 1e-5
NEG = -3.0e38
HID0, LAT, NE = 1024, 256, 8
HC0 = HID0 // P
HID1 = 1376
HC1 = (HID1 + P - 1) // P
R = 16
LROWS = 6 * R
MODW = 640
DIN = 256

SB0 = 16512
AR_WORDS = 43008
HT_W, ACT_W, WR_W = 0, 8192, 8192 + 22528
X_B = SB0 + 4 * AR_WORDS
XN_B = X_B + 16384
RAW_B = XN_B + 8192
FULL_B = RAW_B + 8192
MISC_B = FULL_B + 4096
HT_B = SB0
ACT_B = SB0 + 4 * ACT_W
WR_B = SB0 + 4 * WR_W


class Order:

    def __init__(self):
        self.n = 0
        self.at = {}

    def add(self, name):
        assert name not in self.at, name
        self.at[name] = (self.n, 0)
        self.n += 1

    def loop(self, names, turns):
        for k, name in enumerate(names):
            self.at[name] = (self.n + k, len(names))
        self.n += turns * len(names)

    def before(self, name, turn=0):
        base, per = self.at[name]
        return base + turn * per if per else base


class Banks:

    def __init__(self):
        self.count = [0] * 8
        self.at = {}
        self.next = 0

    def add(self, name, bank=None):
        assert name not in self.at, name
        if bank is None:
            bank = self.next
            self.next = (self.next + 1) % 8
        self.at[name] = (bank, self.count[bank], 0)
        self.count[bank] += 1

    def loop(self, names, turns):
        start = list(self.count)
        mine = []
        for name in names:
            self.add(name)
            mine.append((name, *self.at[name][:2]))
        per = [self.count[b] - start[b] for b in range(8)]
        for name, b, c in mine:
            self.at[name] = (b, c, per[b])
        for b in range(8):
            self.count[b] = start[b] + turns * per[b]

    def get(self, name, turn=0):
        b, c, per = self.at[name]
        return b, (c + turn * per if per else c)


def plan():
    banks, pieces, prods = Banks(), Order(), Order()
    banks.add("mod0")
    banks.add("mod0T")
    for hf in range(2):
        for c in range(KC):
            banks.add(("ln", 0, hf, c))
    for hf in range(2):
        for m in range(6):
            banks.add(("qkv", hf, m))
        banks.add(("vT", hf))
    banks.attn = list(banks.count)
    banks.add("modT")
    for hf in range(2):
        for c in range(KC):
            banks.add(("aT", hf, c))
    for t in range(NT):
        banks.add(("wo", t))
        if t == 5:
            for c in range(KC):
                banks.add(("ln", 1, 0, c))
    for c in range(KC):
        banks.add(("ln", 1, 1, c))
    for hf in range(2):
        banks.add(("gate", hf))
        for m in range(2):
            banks.add(("fc1", hf, m))
    banks.add("gateT")
    banks.loop([("up", j, hf) for j in range(2) for hf in range(2)], HC0 // 2)
    for hf in range(2):
        for m in range(2):
            banks.add(("eo", hf, m))
    for t in range(NT):
        banks.add(("shared", t))
        banks.add(("routed", t))
        if t == 6:
            for c in range(KC):
                banks.add(("ln", 2, 0, c))
    for c in range(KC):
        banks.add(("ln", 2, 1, c))
    for hf in range(2):
        banks.add(("mid", hf))
    for y in range(2):
        for hf in range(2):
            for m in range(2):
                banks.add(("xs", y, hf, m))
            for m in range(2):
                banks.add(("z", y, hf, m))
        for hf in range(2):
            for m in range(2):
                banks.add(("fd", y, hf, m))
        for hf in range(2):
            banks.add(("ssq", y, hf))
            banks.add(("hout", y, hf))
            banks.add(("rbc", y, hf))
    for t in range(NT):
        banks.add(("wup", t))
        if t == 5:
            for c in range(KC):
                banks.add(("ln", 3, 0, c))
    for c in range(KC):
        banks.add(("ln", 3, 1, c))
    banks.add(("lora", 0))
    banks.add(("lora3", 0))
    banks.loop([x for j in range(2) for x in
                [("lora", "L", j), ("lora3", "L", j), ("h1", "L", j, 0), ("h3", "L", j, 0),
                 ("h1", "L", j, 1), ("h3", "L", j, 1)]], HC1 // 2)
    for hf in range(2):
        banks.add(("h1", "E", 0, hf))
        banks.add(("h3", "E", 0, hf))
    for q in range(2):
        for t in range(4):
            banks.add(("down", q, t), bank=4 * q + t)
        for c in range(HC1):
            banks.add(("lora2", q, c), bank=4 * (1 - q) + c % 4)
    for k in range(3):
        pieces.add(("wqkv", k))
    for k in range(2):
        pieces.add(("wo", k))
    pieces.add("fc1")
    pieces.add("gate")
    pieces.add("expert")
    pieces.add("fc2")
    pieces.loop([("up", 0), ("down", 0), ("up", 1), ("down", 1)], HC0 // 2)
    pieces.add("wdown")
    pieces.add("hin")
    pieces.add("fcd")
    pieces.add("hout")
    pieces.add("wup")
    pieces.add(("w13", 0))
    pieces.loop([("w13", 1), ("w13", 2)], HC1 // 2)
    base = pieces.at[("w13", 0)][0]
    pieces.at[("w13", "even")] = (base, 2)
    pieces.at[("w13", "last")] = (base + HC1 - 1, 0)
    for q in range(2):
        for c in range(HC1):
            pieces.add(("w2", q, c))
    prods.loop([("up", j, hf) for j in range(2) for hf in range(2)], HC0 // 2)
    prods.loop([("g", "L", j, hf) for j in range(2) for hf in range(2)], HC1 // 2)
    for hf in range(2):
        prods.add(("g", "E", 0, hf))
    return banks, pieces, prods


SUNITS = [(i, gp, kh) for i in range(NT) for gp in range(2) for kh in range(1 if i < 4 else 2)]
NS = len(SUNITS)
NSE = NS + 2
TUNITS = [(j, i) for j in range(NT) for i in range(j, NT)]
NTU = len(TUNITS)
AHEAD = 10
LAG = 3
PRING = 6
assert NTU % PRING == 0 and NTU % 2 == 0


def adaln_two_blocks(nc, a, out):
    banks, pieces, prods = plan()
    with ExitStack() as ctx:
        cursor = [MISC_B]

        def at(name, shape, dt, offset=None):
            if offset is None:
                offset = cursor[0]
                size = 4 if dt in (F32, F32R) else 2
                for n in shape[1:]:
                    size *= n
                cursor[0] += (size + 31) // 32 * 32
            return nc.alloc_sbuf_tensor_at(name, shape, dt, offset=offset)

        def sem(name):
            return ctx.enter_context(nc.semaphore(name))

        AR = at("arena", [P, AR_WORDS], F32R, SB0)

        def ar(word, *dims):
            n = 1
            for d in dims:
                n *= d
            v = AR[:, word:word + n]
            if len(dims) == 2:
                v = v.rearrange("p (a b) -> p a b", b=dims[1])
            if len(dims) == 3:
                v = v.rearrange("p (a b c) -> p a b c", b=dims[1], c=dims[2])
            return v

        K = 256
        hT = [ar(HT_W, KC, T), ar(HT_W + KC * T, KC, T)]
        x = at("x", [P, NT, D], F32, X_B)
        xnb = at("xnb", [P, 4, D], F32, XN_B)
        raw = at("raw", [P, 2, 1024], F32, RAW_B)
        full = at("full", [P, 2, D], F32, FULL_B)
        Qst = at("Qst", [99, NKV, G, T], BF16, ACT_B)
        Kst = at("Kst", [99, NKV, T], BF16, ACT_B + 65536)
        vtok = at("vtok", [P, NT, P], F32, ACT_B + 81920)
        vr = at("vr", [P, NT, 32], F32, ACT_B + 81920 + 4096)
        mt = at("mt", [32, 2, P], F32, ACT_B + 81920 + 5120)
        mparts = at("mparts", [32, 3, P], BF16, ACT_B + 81920 + 6144)
        maskb = at("maskb", [P, 2, P], BF16, ACT_B + 81920 + 7168)
        Wqkv = [ar(WR_W, KC, 768), ar(WR_W + 3072, KC, 768)]
        cosb = at("cosb", [P, T], F32, WR_B + 24 * 1024)
        sinb = at("sinb", [P, T], F32, WR_B + 28 * 1024)
        rsw = at("rsw", [P, 2, HALF], F32, WR_B + 32 * 1024)
        rq = at("rq", [P, 2, HALF], F32, WR_B + 36 * 1024)
        parts = at("parts", [P, 2, 3, HALF], BF16, WR_B + 40 * 1024)
        wm0 = at("wm0", [P, KC, 1024], F32, ACT_B)
        wmr = at("wmr", [P, KC, MODW], F32, WR_B)
        att = at("att", [P, NT, D], F32, HT_B)
        pr = at("pr", [P, PRING, D], F32, HT_B + 16384)
        ot = at("ot", [P, 2, D], F32, HT_B + 16384 + PRING * 2048)
        gabc = at("gabc", [P, D], F32, WR_B + 12 * 1024)
        gtmp = at("gtmp", [P, D], F32, WR_B + 14 * 1024)
        Wo = [ar(WR_W + 24 * K, KC, D), ar(WR_W + 32 * K, KC, D)]
        lraw = at("lraw", [P, 720], F32, XN_B)
        lpart = at("lpart", [P, 3, 720], BF16, XN_B + 2912)
        aTr = [ar(ACT_W, KC, T), ar(ACT_W + 16 * K, KC, T)]
        u = [ar(ACT_W, HC0, T), ar(ACT_W + 32 * K, HC0, T)]
        lat = [ar(ACT_W + 64 * K, 2, T), ar(ACT_W + 72 * K, 2, T)]
        gg = at("gg", [P, D], F32, ACT_B + 80 * 1024)
        bb = at("bb", [P, D], F32, ACT_B + 82 * 1024)
        Wex = [ar(ACT_W + 84 * K, 2, LAT), ar(ACT_W + 86 * K, 2, LAT)]
        yb = at("yb", [P, 2, D], F32, ACT_B + 84 * 1024)
        gb0 = at("gb0", [P, D], F32, ACT_B + 40 * 1024)
        gb0t = at("gb0t", [P, D], F32, ACT_B + 42 * 1024)
        Wg = [ar(ACT_W + 60 * K, KC, NE), ar(ACT_W + 60 * K + 32, KC, NE)]
        lg = at("lg", [NE, T], F32, ACT_B + 56 * 1024)
        eo = [ar(HT_W, 2, T), ar(HT_W + 2048, 2, T)]
        Wd0 = [ar(WR_W, HC0, D), ar(WR_W + 16 * K, HC0, D)]
        Wf2 = [ar(WR_W + 32 * K, 2, D), ar(WR_W + 36 * K, 2, D)]
        Wf1 = [ar(WR_W + 40 * K, 2, KC, P), ar(WR_W + 44 * K, 2, KC, P)]
        Wup = [[ar(WR_W + (40 + 4 * s) * K, KC, P), ar(WR_W + (42 + 4 * s) * K, KC, P)] for s in range(2)]
        midf = at("midf", [P, T], F32, ACT_B)
        mid = [ar(ACT_W + 4 * K, T), ar(ACT_W + 8 * K, T)]
        xs = at("xs", [P, 2, T], F32, ACT_B + 12 * 1024)
        xsr = [ar(ACT_W + 20 * K, 2, T), ar(ACT_W + 28 * K, 2, T)]
        sz = at("sz", [P, 2, T], F32, ACT_B + 36 * 1024)
        yzr = [ar(ACT_W + 44 * K, 2, T), ar(ACT_W + 52 * K, 2, T)]
        sq = at("sq", [P, 2, T], F32, ACT_B + 60 * 1024)
        hob = [ar(ACT_W + 68 * K, T), ar(ACT_W + 72 * K, T)]
        hof = at("hof", [P, T], F32, ACT_B + 76 * 1024)
        yz = at("yz", [P, 2, T], F32, ACT_B + 80 * 1024)
        dg = at("dg", [P, 4, P], F32, WR_B + 10 * 1024)
        rb = at("rb", [P, HALF], F32, WR_B + 12 * 1024)
        Wdn = [ar(WR_W + 40 * K, KC, P), ar(WR_W + 42 * K, KC, P)]
        Whi = [ar(WR_W + 44 * K, 4, P), ar(WR_W + 46 * K, 4, P)]
        Wfd = [ar(WR_W, 2, 2, P), ar(WR_W + 2 * K, 2, 2, P)]
        Who = [ar(WR_W + 4 * K, 2, P), ar(WR_W + 5 * K, 2, P)]
        Wuo = [ar(WR_W + 6 * K, D), ar(WR_W + 8 * K, D)]
        rt = at("rt", [P, NT, D], F32, WR_B + 16 * 1024)
        Abc = at("Abc", [P, D], F32, WR_B + 32 * 1024)
        Bbc = at("Bbc", [P, D], F32, WR_B + 34 * 1024)
        t36 = at("t36", [P, D], F32, WR_B + 36 * 1024)
        t38 = at("t38", [P, D], F32, WR_B + 38 * 1024)
        gT = [ar(ACT_W, HC1, T), ar(ACT_W + 44 * K, HC1, T)]
        W13 = [[ar(WR_W + 16 * K * 0 + (8 * s) * K, 2, KC, P), ar(WR_W + (8 * s + 4) * K, 2, KC, P)] for s in range(2)]
        W2 = [[ar(WR_W + (16 + 4 * s) * K, D), ar(WR_W + (18 + 4 * s) * K, D)] for s in range(2)]
        Ast = at("Ast", [LROWS, 2432], BF16, WR_B + 36 * 1024)
        Bst = at("Bst", [LROWS, 3328], BF16, WR_B + 36 * 1024 + 4864)
        gb1 = at("gb1", [P, D], F32, WR_B + 34 * 1024)
        gb1t = at("gb1t", [P, D], F32, WR_B + 32 * 1024)
        ident = at("ident", [P, P], F32)
        identb = at("identb", [P, P], BF16)
        sc32 = at("sc32", [P, KC, 2, 16], F32)
        cols = at("cols", [P, 18], F32)
        modc = at("modc", [P, 40], F32)
        mod0c = at("mod0c", [P, 8], F32)
        st = at("st", [P, 4, 6], F32)
        mv = at("mv", [P, 2, 4, 2], F32)
        ve = at("ve", [P, 4], F32)
        rs = at("rs", [P, 2, 4], F32)
        mh = at("mh", [P, 4], F32)
        hms = at("hms", [P, 4], F32)
        hrs = at("hrs", [P, 4], F32)
        yst = at("yst", [P, 2, 6], F32)
        ymv = at("ymv", [P, 2, 2], F32)
        yve = at("yve", [P, 2, 1], F32)
        yrs = at("yrs", [P, 2, 1], F32)
        sce = at("sce", [P, 9], F32)
        alf = at("alf", [P, 2], F32)
        mxp = at("mxp", [P, 2, G, NT], F32)
        nm = at("nm", [P, G * NT], F32)
        rec = at("rec", [P, 2, G, 4], F32)
        top = at("top", [P, NT, 8], F32)
        s2 = at("s2", [P, NT], F32)
        ones = at("ones", [P, P], F32)
        assert cursor[0] <= 229344, cursor[0]
        C_C, C_G, C_BD, C_CW, C_CB, C_D, C_NW = 0, 8, 9, 10, 12, 14, 16

        ps = ctx.enter_context(nc.psum_tensor("ps", [P, 8, 512], F32))

        qscr = nc.dram_tensor("q_parts", (3, DH, NKV, G, T), BF16, kind="Internal").ap()
        kscr = nc.dram_tensor("k_parts", (3, DH, NKV, T), BF16, kind="Internal").ap()
        lscr = nc.dram_tensor("lora_parts", (3, R * 5760), BF16, kind="Internal").ap()
        mscr = nc.dram_tensor("mod_rows", (2, 8 * MODW), F32, kind="Internal").ap()

        full_b = [sem(f"bank{b}_full") for b in range(8)]
        read_b = [sem(f"bank{b}_read") for b in range(8)]
        raw_in = [sem(f"raw{s}_loaded") for s in range(2)]
        piece_done, piece_scaled = sem("piece_split"), sem("piece_scaled")
        x_in = [sem(f"x_half{h}_loaded") for h in range(2)]
        c_in, ident_in, mask_in, trig_in, wm0_in = (sem(n) for n in
                                                    ("cols_loaded", "ident_loaded", "mask_loaded", "trig_loaded", "wm0_loaded"))
        consts = sem("consts_ready")
        c_exp, c_silu, maxp_init = sem("exp_c_ready"), sem("silu_c_ready"), sem("maxima_initialised")
        ln_var, ln_rstd, ln_xn = sem("ln_variance_ready"), sem("ln_rstd_ready"), sem("ln_tile_normalised")
        ln_hi, ln_lo = sem("ln_hi_ready"), sem("ln_lo_ready")
        rope_sw, rope_sin, rope_q = sem("rope_swapped"), sem("rope_sin_applied"), sem("rope_done")
        part_h, part_r, part_m, part_l = (sem(f"part_{n}_ready") for n in "hrml")
        part_out = [sem(f"parts{s}_stored") for s in range(2)]
        v_ones = sem("v_ones_ready")
        stack_in = [sem(f"stacks_of_heads{k}_loaded") for k in range(2)]
        k_ones = sem("k_ones_ready")
        s_full, s_read = sem("score_unit_ready"), sem("score_unit_read")
        nm_ready, mt_parts, mrow_in = sem("row_maxima_ready"), sem("max_parts_ready"), sem("max_rows_loaded")
        modrow_out, wmr_in = sem("mod_piece_stored"), sem("mod_weights_loaded")
        t_full, exp_done, pv_done = sem("scoresT_ready"), sem("exp_done"), sem("pv_done")
        vr_ready, o_copied, o_turned, o_read = (sem("v_of_head_ready"), sem("ctx_copied"), sem("ctx_turned"),
                                                sem("ctx_normalised"))
        lraw_in, lpart_ready, lpart_out, lst_in = (sem("lora_loaded"), sem("lora_parts_ready"),
                                                   sem("lora_parts_stored"), sem("lora_stacks_loaded"))
        ga_in, ga_ready = sem("gate_row_loaded"), sem("gate_of_attn_ready")
        modc_in = sem("mod_chunks_loaded")
        sp_hi = sem("evac_hi_ready")
        ffbc_in, gg_ready, bb_added = sem("mlp_rows_loaded"), sem("mlp_gamma_ready"), sem("mlp_beta_added")
        s_top = sem("top2_sum_ready")
        pr_first, pr_hi, pr_lo = sem("factor_ready"), sem("product_hi_ready"), sem("product_lo_ready")
        y_var, y_rstd, x_mlp = sem("mlp_variance_ready"), sem("mlp_rstd_ready"), sem("x_after_mlp_ready")
        ab_in, ab_ready, rn_ready, r_ready = (sem("mixer_rows_loaded"), sem("mixer_rows_ready"),
                                              sem("mixer_rest_normalised"), sem("mixer_rest_ready"))
        mid_lo, xs_lo, yz_ready, sq_ready, yz_lo = (sem("mid_lo_ready"), sem("xs_lo_ready"), sem("yz_ready"),
                                                    sem("yz_squared"), sem("yz_lo_ready"))
        mr_ready, dg_ready, ho_lo = sem("inverse_rms_ready"), sem("inverse_rms_diagonal_ready"), sem("hydra_out_lo_ready")
        dn_hi = sem("down_hi_ready")
        w_hi, w2_scaled, down_c = sem("merged_weights_hi_ready"), sem("w2_scaled"), sem("down_chunk_done")
        gb1_in, gb1_ready = sem("gate_mlp_loaded"), sem("gate_mlp_ready")
        out_done = sem("out_stored")
        dve_c, act_c, pool_c = sem("vector_chain"), sem("scalar_chain"), sem("gpsimd_chain")

        def filled(eng, job, turn=0):
            b, n = banks.get(job, turn)
            eng.wait_ge(full_b[b], n + 1)
            return b

        def evacuated(eng, job, turn=0):
            b, n = banks.get(job, turn)
            eng.wait_ge(read_b[b], n + 1)

        def bank_of(eng, job, turn=0):
            b, n = banks.get(job, turn)
            if not (isinstance(n, int) and n == 0):
                eng.wait_ge(read_b[b], n)
            return b

        def piece_slot(name):
            return pieces.at[name][0] % 2

        def raw_loaded(eng, name, turn=0):
            base, per = pieces.at[name]
            eng.wait_ge(raw_in[base % 2], 16 * (base // 2 + 1) + (8 * per * turn if per else 0))
            return base % 2

        def weights(eng, name, turn=0):
            eng.wait_ge(piece_done, pieces.before(name, turn) + 1)

        def w13_free(eng, piece, turn=0):
            if piece == ("w13", 0):
                filled(eng, ("wup", NT - 1))
            elif piece == ("w13", 1):
                filled(eng, ("h3", "L", 1, 1), turn - 1)
            else:
                filled(eng, ("h3", "L", 0, 1), turn)

        def w2_free(eng, k):
            if k < 2:
                evacuated(eng, ("wup", NT - 1))
            else:
                q, c = divmod(k - 2, HC1)
                if c < HC1 - 1:
                    eng.wait_ge(down_c, q * (HC1 - 1) + c + 1)
                else:
                    filled(eng, ("down", q, 3))

        class Chain:

            def __init__(self, eng, s):
                self.eng, self.s, self.n, self.turn = eng, s, 0, None

            def link(self, ins):
                ins.then_inc(self.s, 1)
                self.n += 1
                if self.turn is None:
                    self.eng.wait_ge(self.s, self.n)
                else:
                    self.eng.wait_ge(self.s, self.turn * self.per + self.n)

            def tick(self, ins):
                ins.then_inc(self.s, 1)
                self.n += 1

            def enter(self, turn, per):
                self.turn, self.per, self.at = turn, per, self.n

            def leave(self, turns):
                assert self.n - self.at == self.per, (self.n - self.at, self.per)
                self.n = self.at + turns * self.per
                self.turn = None

        block = ctx.enter_context(nc.Block())

        @block.sync
        def _(sp):
            def load_piece(name, src, cols_, turn=0):
                n = pieces.before(name, turn)
                s = piece_slot(name)
                if not (isinstance(n, int) and n < 2):
                    sp.wait_ge(piece_done, n - 1)
                sp.dma_start(raw[:, s, 0:cols_], src).then_inc(raw_in[s], 16)

            sp.dma_start(cols[:, 0:18], a["cols"]).then_inc(c_in, 16)
            for t in range(4):
                sp.dma_start(x[:, t, :], a["x"][t * P:(t + 1) * P, :]).then_inc(x_in[0], 16)
            sp.dma_start(wm0[:, :, :].rearrange("p c n -> p (c n)"), a["wm0"]).then_inc(wm0_in, 16)
            sp.dma_start(ident[:, :], a["ident"]).then_inc(ident_in, 16)
            for k in range(2):
                load_piece(("wqkv", k), a["wqkv"][:, 1024 * k:1024 * (k + 1)], 1024)
            for t in range(4, 8):
                sp.dma_start(x[:, t, :], a["x"][t * P:(t + 1) * P, :]).then_inc(x_in[1], 16)
            sp.dma_start(cosb[:, :], a["cos"]).then_inc(trig_in, 16)
            sp.dma_start(sinb[:, :], a["sin"]).then_inc(trig_in, 16)
            load_piece(("wqkv", 2), a["wqkv"][:, 2048:3072], 1024)
            sp.dma_start(rq[:, 0, 0:2 * P], a["mask"]).then_inc(mask_in, 16)

            for n in range(10):
                hf, m = divmod(n, 5)
                sp.wait_ge(part_l, n + 1)
                tok = slice(hf * HALF, (hf + 1) * HALF)
                for q in range(3):
                    src = parts[:, n % 2, q, :]
                    if m < 4:
                        dst = qscr[q, :, :, m, tok].rearrange("d n t -> n d t")
                    else:
                        dst = kscr[q, :, :, tok].rearrange("d n t -> n d t")
                    sp.dma_start(dst, src).then_inc(part_out[n % 2], 16)
            for s in range(2):
                sp.wait_ge(part_out[s], 16 * 15)
            QP, KP = (0, 0, 1, 0, 2, 1), (0, 1, 0, 2, 0, 1)
            for k, (n0, n1) in enumerate(((0, 2), (2, NKV))):
                for r in range(6):
                    rows = slice(DH * r, DH * (r + 1))
                    sp.dma_start(Kst[rows, n0:n1, :], kscr[KP[r], :, n0:n1, :]).then_inc(stack_in[k], 16)
                    sp.dma_start(Qst[rows, n0:n1, :, :].rearrange("p n g t -> p (n g) t"),
                                 qscr[QP[r], :, n0:n1, :, :].rearrange("d n g t -> d (n g) t")).then_inc(stack_in[k], 16)
            sp.dma_start(lraw[:, :], a["lora"]).then_inc(lraw_in, 16)

            b, n = banks.get(("qkv", 1, 5))
            sp.wait_ge(full_b[b], n + 1)
            sp.dma_start(wmr[:, :, :].rearrange("p c n -> p (c n)"), a["wmr"][0]).then_inc(wmr_in, 16)

            def head_dmas(h, more):
                sp.wait_ge(mt_parts, h + 1)
                for q in range(3):
                    sp.dma_start(Qst[KROWS + q:KROWS + q + 1, bass.ds(h, 1), :, :].rearrange("p n g t -> p (n g t)"),
                                 mparts[:, q, :]).then_inc(mrow_in, 16)
                sp.wait_ge(s_read, h * NSE + NSE)
                for blk in range(2):
                    sp.dma_start(mscr[blk, bass.ds(h * MODW, MODW)].rearrange("(q n) -> q n", n=MODW // 4),
                                 full[16 * blk:16 * blk + 97:32, 0, 0:MODW // 4]).then_inc(modrow_out, 16)
                if more:
                    sp.wait_ge(s_full, h * NSE + NSE)
                    sp.dma_start(wmr[:, :, :].rearrange("p c n -> p (c n)"),
                                 a["wmr"][bass.ds(h + 1, 1)].rearrange("o p n -> (o p) n")).then_inc(wmr_in, 16)

            with sp.Fori(0, NKV - 1) as h:
                head_dmas(h, True)
            head_dmas(NKV - 1, False)
            sp.wait_ge(modrow_out, 32 * NKV)

            def row(k):
                return mscr[0 if k < 4 else 1, k * D:(k + 1) * D].rearrange("(o n) -> o n", o=1).to_broadcast([P, D])

            def rowin(name):
                return a[name].rearrange("(o n) -> o n", o=1).to_broadcast([P, D])

            sp.dma_start(gabc[:, :], row(0)).then_inc(ga_in, 16)
            for blk, (k0, k1) in enumerate(((0, 16), (16, 40))):
                sp.dma_start(full[k0:k1, 1, 0:P], mscr[blk, k0 * P:k1 * P].rearrange("(k n) -> k n", n=P))\
                    .then_inc(modc_in, 16)
            for q in range(3):
                sp.wait_ge(lpart_ready, 1)
                sp.dma_start(lscr[q].rearrange("(p n) -> p n", p=P), lpart[:, q, :]).then_inc(lpart_out, 16)
            for k in range(2):
                load_piece(("wo", k), a["wo"][:, 1024 * k:1024 * (k + 1)], 1024)
            load_piece("fc1", a["fc1"], 1024)
            load_piece("gate", a["gate"], KC * NE)
            load_piece("expert", a["expert"], 2 * LAT)
            sp.wait_ge(o_read, 2 * NKV)
            sp.dma_start(gg[:, :], rowin("gamma")).then_inc(ffbc_in, 16)
            sp.dma_start(bb[:, :], rowin("beta")).then_inc(ffbc_in, 16)
            sp.dma_start(gb0[:, :], row(3)).then_inc(ffbc_in, 16)
            load_piece("fc2", a["fc2"], 1024)
            with sp.Fori(0, HC0 // 2) as i:
                for j in range(2):
                    for kind in ("up", "down"):
                        load_piece((kind, j), a[kind][bass.ds(2 * i + j, 1)].rearrange("o p n -> (o p) n"), D, i)
            load_piece("wdown", a["wdown"], D)
            load_piece("hin", a["hin"], D)
            load_piece("fcd", a["fcd"], D)
            load_piece("hout", a["hout"], 2 * P)
            load_piece("wup", a["wup"], D)
            b, n = banks.get(("routed", NT - 1))
            sp.wait_ge(full_b[b], n + 1)
            sp.dma_start(Abc[:, :], row(5)).then_inc(ab_in, 16)
            sp.dma_start(Bbc[:, :], row(4)).then_inc(ab_in, 16)
            sp.dma_start(t36[:, :], row(6)).then_inc(ab_in, 16)
            sp.dma_start(t38[:, :], rowin("bup")).then_inc(ab_in, 16)
            sp.wait_ge(lpart_out, 48)
            b, n = banks.get(("z", 1, 1, 1))
            sp.wait_ge(full_b[b], n + 1)
            sp.wait_ge(r_ready, NT)
            sp.wait_ge(piece_done, pieces.before("wup") + 1)
            for r in range(6):
                rows = slice(DH * r, DH * (r + 1))
                lv = [lscr[q].rearrange("(r n) -> r n", r=R) for q in (QP[r], KP[r])]
                sp.dma_start(Ast[rows, :], lv[0][:, 0:2432]).then_inc(lst_in, 16)
                sp.dma_start(Bst[rows, :], lv[1][:, 2432:5760]).then_inc(lst_in, 16)
            sp.dma_start(gb1[:, :], row(9)).then_inc(gb1_in, 16)
            load_piece(("w13", 0), a["w13"][0], 1024)
            with sp.Fori(0, HC1 // 2) as i:
                for j in (1, 2):
                    load_piece(("w13", j), a["w13"][bass.ds(2 * i + j, 1)].rearrange("o p n -> (o p) n"), 1024, i)
            for q in range(2):
                for c in range(HC1):
                    load_piece(("w2", q, c), a["w2"][c], D)
            for t in range(NT):
                evacuated(sp, ("down", t // 4, t % 4))
                sp.dma_start(out[t * P:(t + 1) * P, :], x[:, t, :]).then_inc(out_done, 16)
            sp.wait_ge(out_done, 16 * NT)

        @block.tensor
        def _(pe):
            def mm(outp, lhs, rhs, start, stop):
                return nc.tensor.matmul(outp, lhs, rhs, start=start, stop=stop, skip_group_check=True)

            def mm3(outp, lhs, rhs, start, stop):
                mm(outp, lhs[0], rhs[0], start, False)
                mm(outp, lhs[0], rhs[1], False, False)
                return mm(outp, lhs[1], rhs[0], False, stop)

            def hilo(pair, f):
                return f(pair[0]), f(pair[1])

            def ln_turn(L, hf):
                pe.wait_ge(ln_xn, 8 * L + 4 * hf + 4)
                for c in range(KC):
                    b = bank_of(pe, ("ln", L, hf, c))
                    for t in range(4):
                        last = nc.tensor.transpose(ps[:, b, t * P:(t + 1) * P], xnb[:, t, c * P:(c + 1) * P],
                                                   ident[:, :])
                    last.then_inc(full_b[b], 1)

            tok = [slice(0, HALF), slice(HALF, T)]

            def tl(t):
                return slice(t * P, (t + 1) * P)

            pe.wait_ge(c_silu, 1)
            pe.wait_ge(wm0_in, 16)
            b = bank_of(pe, "mod0")
            for kc in range(KC):
                for q in range(4):
                    last = mm(ps[32 * q:32 * q + 32, b, 0:256], sc32[:, kc, :, :].rearrange("p l m -> p (l m)"), wm0[:, kc, 256 * q:256 * q + 256],
                              kc == 0, kc == KC - 1)
            last.then_inc(full_b[b], 1)
            evacuated(pe, "mod0")
            pe.wait_ge(ident_in, 16)
            b = bank_of(pe, "mod0T")
            for k in range(2):
                last = nc.tensor.transpose(ps[:, b, k * P:(k + 1) * P], full[:, 0, k * P:(k + 1) * P], ident[:, :])
            last.then_inc(full_b[b], 1)
            for hf in range(2):
                ln_turn(0, hf)
            for hf in range(2):
                pe.wait_ge(ln_lo, 4 * hf + 4)
                for m in range(6):
                    if hf == 0 and m == 0:
                        weights(pe, ("wqkv", 2))
                    b = bank_of(pe, ("qkv", hf, m))
                    for kc in range(KC):
                        last = mm3(ps[:, b, :], hilo(Wqkv, lambda w: w[:, kc, m * P:(m + 1) * P]),
                                   hilo(hT, lambda h: h[:, kc, tok[hf]]), kc == 0, kc == KC - 1)
                    last.then_inc(full_b[b], 1)
                evacuated(pe, ("qkv", hf, 5))
                b = bank_of(pe, ("vT", hf))
                for t in range(4):
                    last = nc.tensor.transpose(ps[:, b, tl(t)], full[:, hf, tl(t)], ident[:, :])
                last.then_inc(full_b[b], 1)

            def s_unit(h, s):
                slot = s % 2
                i, gp, kh = SUNITS[s]
                if s >= 2:
                    pe.wait_ge(s_read, h * NSE + s - 1)
                elif not (isinstance(h, int) and h == 0):
                    pe.wait_ge(s_read, h * NSE - 1 + s)
                w = min(P * (i + 1), 512) if kh == 0 else P * (i - 3)
                diag = kh == (0 if i < 4 else 1)
                for e in range(2):
                    o = ps[:, 2 * slot + e, :]
                    last = mm(o[:, 0:w], Qst[0:KROWS, bass.ds(h, 1), 2 * gp + e, i * P:(i + 1) * P]
                              .rearrange("p n t -> p (n t)"),
                              Kst[0:KROWS, bass.ds(h, 1), 512 * kh:512 * kh + w].rearrange("p n t -> p (n t)"),
                              True, not diag)
                    if diag:
                        last = mm(o[:, w - P:w], identb[:, :], maskb[:, 0, :], False, True)
                last.then_inc(s_full, 1)

            def max_turn(h):
                pe.wait_ge(s_read, h * NSE + NS - 1)
                pe.wait_ge(nm_ready, h + 1)
                nc.tensor.transpose(ps[0:32, 0, 0:P], nm[:, :], ident[:, :]).then_inc(s_full, 1)

            def mod_step(h):
                pe.wait_ge(s_read, h * NSE + NS)
                pe.wait_ge(wmr_in, 16 * h + 16)
                w = MODW // 4
                for kc in range(KC):
                    for q in range(4):
                        last = mm(ps[32 * q:32 * q + 32, 2, 0:w], sc32[:, kc, :, :].rearrange("p l m -> p (l m)"),
                                  wmr[:, kc, w * q:w * q + w], kc == 0, kc == KC - 1)
                last.then_inc(s_full, 1)

            def t_unit(n, k):
                j, i = TUNITS[k]
                if k == 0:
                    pe.wait_ge(mrow_in, 48 * n + 48)
                if k >= 2:
                    pe.wait_ge(exp_done, n * NTU + k - 1)
                o = ps[:, 4 + k % 2, :].rearrange("p (g t) -> p g t", g=G)
                last = mm(o, Kst[:, bass.ds(n, 1), j * P:(j + 1) * P].rearrange("p n t -> p (n t)"),
                          Qst[:, bass.ds(n, 1), :, i * P:(i + 1) * P].rearrange("p n g t -> p (n g) t"),
                          True, i > j)
                if i == j:
                    last = mm(o, identb[:, :], maskb[:, 1, :].unsqueeze(1).to_broadcast([P, G, P]), False, True)
                last.then_inc(t_full, 1)

            def pv(n, k):
                j, i = TUNITS[k]
                if k == 0:
                    pe.wait_ge(vr_ready, n + 1)
                    if not (isinstance(n, int) and n == 0):
                        pe.wait_ge(o_read, 2 * n)
                pe.wait_ge(exp_done, n * NTU + k + 1)
                q = 32 * (i % 4)
                mm(ps[q:q + 32, 6 + i // 4, :], vr[:, j, :], pr[:, k % PRING, :], j == 0, j == i).then_inc(pv_done, 1)

            def ctx_turn(n):
                for b in range(2):
                    pe.wait_ge(o_copied, 2 * n + b + 1)
                    for g in range(G):
                        last = nc.tensor.transpose(ps[:, 6 + b, tl(g)], ot[:, b, tl(g)], ident[:, :])
                    last.then_inc(o_turned, 1)

            def head_body(n, nxt, nxt2):
                todo = []
                if nxt:
                    todo += [(k * 22 // (NS - AHEAD), s_unit, n + 1, AHEAD + k) for k in range(NS - AHEAD)]
                    todo += [(24, max_turn, n + 1, None), (25, mod_step, n + 1, None)]
                if nxt2:
                    todo += [(26 + k if k < AHEAD - 1 else NTU, s_unit, n + 2, k) for k in range(AHEAD)]
                for k in range(NTU + LAG):
                    if k < NTU:
                        t_unit(n, k)
                    while todo and todo[0][0] <= k:
                        _, f, h, s = todo.pop(0)
                        f(h) if s is None else f(h, s)
                    if k >= LAG:
                        pv(n, k - LAG)
                assert not todo
                ctx_turn(n)

            for b in range(8):
                if banks.attn[b]:
                    pe.wait_ge(read_b[b], banks.attn[b])
            pe.wait_ge(k_ones, 2)
            pe.wait_ge(stack_in[0], 16 * 12)
            for s in range(NS):
                s_unit(0, s)
            max_turn(0)
            mod_step(0)
            for s in range(AHEAD):
                s_unit(1, s)
            pe.wait_ge(stack_in[1], 16 * 12)
            with pe.Fori(0, NKV - 2) as n:
                head_body(n, True, True)
            head_body(NKV - 2, True, False)
            head_body(NKV - 1, False, False)

            pe.wait_ge(o_read, 2 * NKV)
            pe.wait_ge(s_read, NKV * NSE)
            pe.wait_ge(modc_in, 32)
            b = bank_of(pe, "modT")
            nc.tensor.transpose(ps[:, b, 0:40], full[0:40, 1, 0:P], ident[0:40, 0:40]).then_inc(full_b[b], 1)
            for hf in range(2):
                for c in range(KC):
                    b = bank_of(pe, ("aT", hf, c))
                    for t in range(4):
                        last = nc.tensor.transpose(ps[:, b, tl(t)], att[:, 4 * hf + t, c * P:(c + 1) * P], ident[:, :])
                    last.then_inc(full_b[b], 1)
            weights(pe, ("wo", 1))
            for t in range(NT):
                if t % 4 == 0:
                    for c in range(KC):
                        evacuated(pe, ("aT", t // 4, c))
                b = bank_of(pe, ("wo", t))
                for kc in range(KC):
                    last = mm3(ps[:, b, :], hilo(aTr, lambda h: h[:, kc, tl(t)]), hilo(Wo, lambda w: w[:, kc, :]),
                               kc == 0, kc == KC - 1)
                last.then_inc(full_b[b], 1)
                if t == 5:
                    ln_turn(1, 0)
            ln_turn(1, 1)

            for hf in range(2):
                pe.wait_ge(ln_lo, 8 + 4 * hf + 4)
                weights(pe, "gate")
                b = bank_of(pe, ("gate", hf))
                for kc in range(KC):
                    last = mm3(ps[0:NE, b, :], hilo(Wg, lambda w: w[:, kc, :]), hilo(hT, lambda h: h[:, kc, tok[hf]]),
                               kc == 0, kc == KC - 1)
                last.then_inc(full_b[b], 1)
                for m in range(2):
                    b = bank_of(pe, ("fc1", hf, m))
                    for kc in range(KC):
                        last = mm3(ps[:, b, :], hilo(Wf1, lambda w: w[:, m, kc, :]),
                                   hilo(hT, lambda h: h[:, kc, tok[hf]]), kc == 0, kc == KC - 1)
                    last.then_inc(full_b[b], 1)
            evacuated(pe, ("gate", 0))
            evacuated(pe, ("gate", 1))
            b = bank_of(pe, "gateT")
            for t in range(NT):
                last = nc.tensor.transpose(ps[:, b, NE * t:NE * t + NE], lg[:, tl(t)], ident[0:NE, 0:NE])
            last.then_inc(full_b[b], 1)
            with pe.Fori(0, HC0 // 2) as i:
                for j in range(2):
                    weights(pe, ("up", j), i)
                    for hf in range(2):
                        b = bank_of(pe, ("up", j, hf), i)
                        for kc in range(KC):
                            last = mm3(ps[:, b, :], hilo(Wup[j], lambda w: w[:, kc, :]),
                                       hilo(hT, lambda h: h[:, kc, tok[hf]]), kc == 0, kc == KC - 1)
                        last.then_inc(full_b[b], 1)
            weights(pe, "expert")
            for hf in range(2):
                for m in range(2):
                    evacuated(pe, ("fc1", hf, m))
                for m in range(2):
                    b = bank_of(pe, ("eo", hf, m))
                    for kc in range(2):
                        last = mm3(ps[:, b, :], hilo(Wex, lambda w: w[:, kc, m * P:(m + 1) * P]),
                                   hilo(lat, lambda h: h[:, kc, tok[hf]]), kc == 0, kc == 1)
                    last.then_inc(full_b[b], 1)
            pe.wait_ge(pr_lo, 2 * HC0)
            for t in range(NT):
                if t == 0:
                    weights(pe, ("down", 1), HC0 // 2 - 1)
                b = bank_of(pe, ("shared", t))
                for kc in range(HC0):
                    last = mm3(ps[:, b, :], hilo(u, lambda h: h[:, kc, tl(t)]), hilo(Wd0, lambda w: w[:, kc, :]),
                               kc == 0, kc == HC0 - 1)
                last.then_inc(full_b[b], 1)
                if t % 4 == 0:
                    for m in range(2):
                        evacuated(pe, ("eo", t // 4, m))
                b = bank_of(pe, ("routed", t))
                for kc in range(2):
                    last = mm3(ps[:, b, :], hilo(eo, lambda h: h[:, kc, tl(t)]), hilo(Wf2, lambda w: w[:, kc, :]),
                               kc == 0, kc == 1)
                last.then_inc(full_b[b], 1)
                if t == 6:
                    ln_turn(2, 0)
            ln_turn(2, 1)

            weights(pe, "wdown")
            for hf in range(2):
                pe.wait_ge(ln_lo, 16 + 4 * hf + 4)
                b = bank_of(pe, ("mid", hf))
                for kc in range(KC):
                    last = mm3(ps[:, b, :], hilo(Wdn, lambda w: w[:, kc, :]), hilo(hT, lambda h: h[:, kc, tok[hf]]),
                               kc == 0, kc == KC - 1)
                last.then_inc(full_b[b], 1)
            weights(pe, "hin")
            for y in range(2):
                src = mid if y == 0 else hob
                for hf in range(2):
                    pe.wait_ge(mid_lo if y == 0 else ho_lo, hf + 1)
                    for kind, m0 in (("xs", 2), ("z", 0)):
                        for m in range(2):
                            b = bank_of(pe, (kind, y, hf, m))
                            mm3(ps[:, b, :], hilo(Whi, lambda w: w[:, m0 + m, :]), hilo(src, lambda h: h[:, tok[hf]]),
                                True, True).then_inc(full_b[b], 1)
                weights(pe, "hout")
                for hf in range(2):
                    pe.wait_ge(xs_lo, 4 * y + 2 * hf + 2)
                    for m in range(2):
                        b = bank_of(pe, ("fd", y, hf, m))
                        for kc in range(2):
                            last = mm3(ps[:, b, :], hilo(Wfd, lambda w: w[:, kc, m, :]),
                                       hilo(xsr, lambda h: h[:, kc, tok[hf]]), kc == 0, kc == 1)
                        last.then_inc(full_b[b], 1)
                for hf in range(2):
                    pe.wait_ge(sq_ready, 4 * y + 2 * hf + 2)
                    b = bank_of(pe, ("ssq", y, hf))
                    for t in range(4):
                        for kc in range(2):
                            last = mm(ps[:, b, t:t + 1], sq[:, kc, tl(4 * hf + t)], ones[:, 0:1], kc == 0, kc == 1)
                    last.then_inc(full_b[b], 1)
                    pe.wait_ge(yz_lo, 4 * y + 2 * hf + 2)
                    b = bank_of(pe, ("hout", y, hf))
                    for kc in range(2):
                        last = mm3(ps[:, b, :], hilo(Who, lambda w: w[:, kc, :]), hilo(yzr, lambda h: h[:, kc, tok[hf]]),
                                   kc == 0, kc == 1)
                    last.then_inc(full_b[b], 1)
                    pe.wait_ge(dg_ready, 2 * y + hf + 1)
                    b = bank_of(pe, ("rbc", y, hf))
                    mm(ps[:, b, :], ones[:, :], dg[:, :, :].rearrange("p t n -> p (t n)"), True, True)\
                        .then_inc(full_b[b], 1)
            weights(pe, "wup")
            for t in range(NT):
                if t % 4 == 0:
                    pe.wait_ge(ho_lo, 2 + t // 4 + 1)
                b = bank_of(pe, ("wup", t))
                mm3(ps[:, b, :], hilo(hob, lambda h: h[:, tl(t)]), Wuo, True, True).then_inc(full_b[b], 1)
                if t == 5:
                    ln_turn(3, 0)
            ln_turn(3, 1)

            def lora(name, c, turn=0):
                for which, (kind, o) in enumerate((("lora", 0), ("lora3", HC1 * P))):
                    b = bank_of(pe, (kind, *name), turn)
                    for kc in range(KC):
                        last = mm(ps[:, b, kc * P:(kc + 1) * P],
                                  Ast[:, 512 * which + kc * P:512 * which + (kc + 1) * P],
                                  Bst[:, bass.ds(o + c * P, P)], True, True)
                    last.then_inc(full_b[b], 1)

            def gated(name, piece, slot, turn=0):
                weights(pe, piece, turn)
                for hf in range(2):
                    if name == ("E", 0) or name == ("L", 0):
                        pe.wait_ge(ln_lo, 24 + 4 * hf + 4)
                    for which, kind in enumerate(("h1", "h3")):
                        b = bank_of(pe, (kind, *name, hf), turn)
                        for kc in range(KC):
                            last = mm3(ps[:, b, :], hilo(W13[slot], lambda w: w[:, which, kc, :]),
                                       hilo(hT, lambda h: h[:, kc, tok[hf]]), kc == 0, kc == KC - 1)
                        last.then_inc(full_b[b], 1)

            pe.wait_ge(lst_in, 16 * 12)
            lora((0,), 0)
            with pe.Fori(0, HC1 // 2) as i:
                lora(("L", 0), 2 * i + 1, i)
                gated(("L", 0), ("w13", "even"), 0, i)
                lora(("L", 1), 2 * i + 2, i)
                gated(("L", 1), ("w13", 1), 1, i)
            gated(("E", 0), ("w13", "last"), 0)

            def lora2(q, c):
                b = bank_of(pe, ("lora2", q, c))
                mm(ps[:, b, :], Ast[:, 1024 + c * P:1024 + (c + 1) * P], Bst[:, 2 * HC1 * P:2 * HC1 * P + D], True, True)\
                    .then_inc(full_b[b], 1)

            steps = [(q, c) for q in range(2) for c in range(HC1)]
            for k, (q, c) in enumerate(steps):
                if c == 0:
                    lora2(q, 0)
                if c + 1 < HC1:
                    lora2(q, c + 1)
                if k == 0:
                    pe.wait_ge(pr_lo, 2 * HC0 + 2 * HC1)
                weights(pe, ("w2", q, c))
                for t in range(4):
                    b = bank_of(pe, ("down", q, t)) if c == 0 else banks.get(("down", q, t))[0]
                    last = mm3(ps[:, b, :], hilo(gT, lambda h: h[:, c, tl(4 * q + t)]), W2[k % 2], c == 0, c == HC1 - 1)
                    if c == HC1 - 1:
                        last.then_inc(full_b[b], 1)
                if c < HC1 - 1:
                    last.then_inc(down_c, 1)

        @block.scalar
        def _(act):
            A = nc.scalar.activation
            chain = Chain(act, act_c)

            def ln_full(L, hf, c, scale, bias):
                n = 8 * L + 4 * hf + c
                b = filled(act, ("ln", L, hf, c))
                if n >= 2:
                    act.wait_ge(ln_lo, n - 1)
                A(full[:, n % 2, :], ps[:, b, :], ACT.Identity, scale=scale, bias=bias).then_inc(read_b[b], 1)

            def split_hi(job, dst):
                b = filled(act, job)
                A(dst, ps[:, b, :], ACT.Copy).then_inc(sp_hi, 1)

            tok = [slice(0, HALF), slice(HALF, T)]

            act.wait_ge(c_in, 16)
            A(sce[:, :], cols[:, 0:9], ACT.Exp, scale=-1.0).then_inc(c_exp, 1)
            b = filled(act, "mod0")
            A(full[:, 0, 0:256], ps[:, b, 0:256], ACT.Copy).then_inc(read_b[b], 1)
            evacuated(act, "mod0T")
            for hf in range(2):
                for c in range(KC):
                    ln_full(0, hf, c, mod0c[:, 4 + c:5 + c], mod0c[:, c:c + 1])
            for hf in range(2):
                for m in range(5):
                    n = 5 * hf + m
                    act.wait_ge(rope_q, n + 1)
                    if n >= 2:
                        act.wait_ge(part_out[n % 2], 48 * (n // 2))
                    A(parts[:, n % 2, 0, :], rq[:, n % 2, :], ACT.Copy).then_inc(part_h, 1)
                    act.wait_ge(part_r, n + 1)
                    A(parts[:, n % 2, 1, :], rq[:, n % 2, :], ACT.Copy).then_inc(part_m, 1)
                b = filled(act, ("qkv", hf, 5))
                if hf == 0:
                    act.wait_ge(ln_lo, 8)
                A(full[:, hf, :], ps[:, b, :], ACT.Copy).then_inc(read_b[b], 1)
                b = filled(act, ("vT", hf))
                A(vtok[:, 4 * hf:4 * hf + 4, :].rearrange("p t n -> p (t n)"), ps[:, b, :], ACT.Copy)\
                    .then_inc(read_b[b], 1)

            def head_body(n):
                for k in range(NTU):
                    act.wait_ge(t_full, n * NTU + k + 1)
                    if k >= PRING:
                        act.wait_ge(pv_done, n * NTU + k - PRING + 1)
                    elif k == 0 and not (isinstance(n, int) and n == 0):
                        act.wait_ge(pv_done, n * NTU)
                    A(pr[:, k % PRING, :], ps[:, 4 + k % 2, :], ACT.Exp, scale=float(DH) ** -0.5).then_inc(exp_done, 1)
                act.wait_ge(pv_done, n * NTU + NTU)
                for b in range(2):
                    A(ot[:, b, :], ps[:, 6 + b, :], ACT.Copy).then_inc(o_copied, 1)

            with act.Fori(0, NKV) as n:
                head_body(n)
            for hf in range(2):
                for c in range(KC):
                    split_hi(("aT", hf, c), aTr[0][:, c, tok[hf]])
            evacuated(act, "modT")
            for hf in range(2):
                for c in range(KC):
                    ln_full(1, hf, c, modc[:, 8 + c:9 + c], modc[:, 4 + c:5 + c])

            for hf in range(2):
                b = filled(act, ("gate", hf))
                A(lg[:, tok[hf]], ps[0:NE, b, :], ACT.Copy).then_inc(read_b[b], 1)
                for m in range(2):
                    split_hi(("fc1", hf, m), lat[0][:, m, tok[hf]])

            def relu_unit(i, j, hf):
                name = ("up", j, hf)
                s = prods.at[name][0] % 2
                b = filled(act, name, i)
                A(full[:, s, :], ps[:, b, :], ACT.Relu).then_inc(pr_first, 1)
                evacuated(act, name, i)
                A(u[0][:, bass.ds(2 * i + j, 1), tok[hf]].rearrange("p o n -> p (o n)"), xnb[:, s, :], ACT.Copy)\
                    .then_inc(pr_hi, 1)

            act.wait_ge(ln_lo, 16)
            with act.Fori(0, HC0 // 2) as i:
                for j in range(2):
                    s = raw_loaded(act, ("down", j), i)
                    A(Wd0[0][:, bass.ds(2 * i + j, 1), :].rearrange("p o n -> p (o n)"), raw[:, s, 0:D], ACT.Copy)\
                        .then_inc(dn_hi, 1)
                    for hf in range(2):
                        relu_unit(i, j, hf)
            for hf in range(2):
                for m in range(2):
                    split_hi(("eo", hf, m), eo[0][:, m, tok[hf]])
            act.wait_ge(s_top, 1)
            for t in range(NT):
                b = filled(act, ("routed", t))
                if t >= 2:
                    act.wait_ge(y_var, t - 1)
                A(full[:, t % 2, :], ps[:, b, :], ACT.Copy, scale=s2[:, t:t + 1]).then_inc(read_b[b], 1)
                if t == 7:
                    act.wait_ge(y_var, 8)
                    for c in range(KC):
                        ln_full(2, 0, c, modc[:, 20 + c:21 + c], modc[:, 16 + c:17 + c])
            for c in range(KC):
                ln_full(2, 1, c, modc[:, 20 + c:21 + c], modc[:, 16 + c:17 + c])

            for hf in range(2):
                b = filled(act, ("mid", hf))
                A(midf[:, tok[hf]], ps[:, b, :], ACT.Gelu, bias=cols[:, C_BD:C_BD + 1]).then_inc(read_b[b], 1)
            for y in range(2):
                for hf in range(2):
                    for m in range(2):
                        b = filled(act, ("xs", y, hf, m))
                        if y == 1:
                            act.wait_ge(yz_ready, 2 * hf + m + 1)
                        A(xs[:, m, tok[hf]], ps[:, b, :], ACT.Silu, scale=cols[:, C_CW + m:C_CW + m + 1],
                          bias=cols[:, C_CB + m:C_CB + m + 1]).then_inc(read_b[b], 1)
                    for m in range(2):
                        b = filled(act, ("z", y, hf, m))
                        A(sz[:, m, tok[hf]], ps[:, b, :], ACT.Silu).then_inc(read_b[b], 1)
                for hf in range(2):
                    for m in range(2):
                        act.wait_ge(yz_ready, 4 * y + 2 * hf + m + 1)
                        A(sq[:, m, tok[hf]], yz[:, m, tok[hf]], ACT.Square).then_inc(sq_ready, 1)
                for hf in range(2):
                    b = filled(act, ("rbc", y, hf))
                    if 2 * y + hf >= 1:
                        evacuated(act, ("hout", y if hf else 0, 1 - hf))
                    A(rb[:, :], ps[:, b, :], ACT.Copy).then_inc(read_b[b], 1)
            for hf in range(2):
                for c in range(KC):
                    ln_full(3, hf, c, modc[:, 32 + c:33 + c], modc[:, 28 + c:29 + c])

            def w13_hi(piece, slot, job, turn=0):
                evacuated(act, job, turn)
                w13_free(act, piece, turn)
                A(W13[slot][0][:, :, :, :].rearrange("p a c n -> p (a c n)"), raw[:, piece_slot(piece), :], ACT.Copy)\
                    .then_inc(w_hi, 1)

            def gate_unit(i, name, c):
                for hf in range(2):
                    pn = ("g", *name, hf)
                    s = prods.at[pn][0] % 2
                    b = filled(act, ("h1", *name, hf), i)
                    A(full[:, s, :], ps[:, b, :], ACT.Silu).then_inc(read_b[b], 1)
                    evacuated(act, ("h3", *name, hf), i)
                    A(gT[0][:, bass.ds(c, 1), tok[hf]].rearrange("p o n -> p (o n)"), xnb[:, s, :], ACT.Copy)\
                        .then_inc(pr_hi, 1)

            act.wait_ge(ln_lo, 32)
            w13_hi(("w13", 0), 0, ("lora3", 0))
            with act.Fori(0, HC1 // 2) as i:
                w13_hi(("w13", 1), 1, ("lora3", "L", 0), i)
                gate_unit(i, ("L", 0), 2 * i)
                w13_hi(("w13", 2), 0, ("lora3", "L", 1), i)
                gate_unit(i, ("L", 1), 2 * i + 1)
            gate_unit(0, ("E", 0), HC1 - 1)
            for q in range(2):
                for c in range(HC1):
                    k = q * HC1 + c
                    act.wait_ge(w2_scaled, k + 1)
                    w2_free(act, k)
                    A(W2[k % 2][0], raw[:, piece_slot(("w2", q, c)), 0:D], ACT.Copy).then_inc(w_hi, 1)

        @block.vector
        def _(dve):
            V = nc.vector
            chain = Chain(dve, dve_c)
            link = chain.link
            tok = [slice(0, HALF), slice(HALF, T)]

            def ln_stats(L, hf):
                for t in range(4):
                    ins = V.bn_stats(st[:, t, :], x[:, 4 * hf + t, :])
                    if t < 3:
                        chain.tick(ins)
                link(ins)
                for t in range(4):
                    ins = V.bn_aggr(mv[:, hf, t, :], st[:, t, :])
                    if t < 3:
                        chain.tick(ins)
                link(ins)
                V.tensor_scalar(ve[:, :], mv[:, hf, :, 1], EPS, None, ALU.add).then_inc(ln_var, 1)

            def ln_norm(L, hf):
                dve.wait_ge(ln_rstd, 2 * L + hf + 1)
                if hf:
                    filled(dve, ("ln", L, 0, KC - 1))
                for t in range(4):
                    V.tensor_scalar(xnb[:, t, :], x[:, 4 * hf + t, :], mv[:, hf, t, 0:1], rs[:, hf, t:t + 1],
                                    ALU.subtract, ALU.mult).then_inc(ln_xn, 1)

            def ln_hi_(L, hf):
                for c in range(KC):
                    n = 8 * L + 4 * hf + c
                    evacuated(dve, ("ln", L, hf, c))
                    V.tensor_copy(hT[0][:, c, tok[hf]], full[:, n % 2, :]).then_inc(ln_hi, 1)

            def split_lo(order_n, job, hi, dst):
                dve.wait_ge(sp_hi, order_n + 1)
                b = banks.get(job)[0]
                V.tensor_tensor(dst, ps[:, b, :], hi.bitcast(F32), ALU.subtract).then_inc(read_b[b], 1)

            def floor_gate(v, tmp):
                link(V.tensor_scalar(tmp, v, 0.0, 2.0, ALU.is_ge, ALU.mult))
                link(V.scalar_tensor_tensor(out=v, in0=v, scalar=-1.0, in1=v, op0=ALU.mult, op1=ALU.max))
                link(V.tensor_scalar(v, v, 0.25, None, ALU.max))
                return V.scalar_tensor_tensor(out=v, in0=tmp, scalar=-1.0, in1=v, op0=ALU.add, op1=ALU.mult)

            V.memset(ones[:, :], 1.0).then_inc(consts, 1)
            V.memset(mh[:, :], -0.5).then_inc(consts, 1)
            V.memset(mxp[:, :, :, :], NEG).then_inc(maxp_init, 1)
            dve.wait_ge(c_exp, 1)
            link(V.tensor_scalar(sce[:, :], sce[:, :], 1.0, None, ALU.add))
            link(V.reciprocal(sce[:, :], sce[:, :]))
            V.tensor_tensor(sc32[:, :, :, :].rearrange("p k l m -> p l k m"),
                            cols[:, 0:8].rearrange("p (l k) -> p l k", l=2).unsqueeze(3).to_broadcast([P, 2, KC, 16]),
                            sce[:, 0:8].rearrange("p (l k) -> p l k", l=2).unsqueeze(3).to_broadcast([P, 2, KC, 16]),
                            ALU.mult).then_inc(c_silu, 1)
            V.tensor_scalar(alf[:, 0:1], sce[:, 8:9], 1.0, None, ALU.add).then_inc(consts, 1)
            V.tensor_scalar(alf[:, 1:2], sce[:, 8:9], -1.0, 1.0, ALU.mult, ALU.add).then_inc(consts, 1)
            dve.wait_ge(consts, 4)
            for hf in range(2):
                dve.wait_ge(x_in[hf], 64)
                ln_stats(0, hf)
                if hf == 0:
                    ln_norm(0, 0)
            dve.wait_ge(ident_in, 16)
            V.tensor_copy(identb[:, :], ident[:, :]).then_inc(k_ones, 1)
            b = filled(dve, "mod0T")
            cview = ps[:, b, 0:256].rearrange("p (k q m) -> p q k m", k=2, m=32)[:, :, :, 0]
            link(V.tensor_copy(mod0c[:, 0:4].rearrange("p (q k) -> p q k", k=2), cview[:, 0:2, :]))
            V.tensor_scalar(mod0c[:, 4:8].rearrange("p (q k) -> p q k", k=2), cview[:, 2:4, :], 1.0, None, ALU.add)\
                .then_inc(read_b[b], 1)
            dve.wait_ge(mask_in, 16)
            link(V.tensor_copy(maskb[:, :, :].rearrange("p a b -> p (a b)"), rq[:, 0, 0:2 * P]))
            ln_norm(0, 1)
            for hf in range(2):
                ln_hi_(0, hf)
            V.memset(vr[:, :, 16:32], 1.0).then_inc(v_ones, 1)
            V.memset(Kst[KROWS:KROWS + 3, :, :], 1.0).then_inc(k_ones, 1)

            dve.wait_ge(trig_in, 32)
            swap = [p ^ 8 for p in range(32)]
            for hf in range(2):
                for m in range(5):
                    n = 5 * hf + m
                    s = n % 2
                    b = filled(dve, ("qkv", hf, m))
                    if n >= 2:
                        dve.wait_ge(part_l, n - 1)
                    V.stream_shuffle(rsw[:, s, :], ps[:, b, :], swap).then_inc(rope_sw, 1)
                    V.tensor_tensor(rq[:, s, :], ps[:, b, :], cosb[:, tok[hf]], ALU.mult).then_inc(read_b[b], 1)
                    dve.wait_ge(rope_sin, n + 1)
                    evacuated(dve, ("qkv", hf, m))
                    V.tensor_tensor(rq[:, s, :], rq[:, s, :], rsw[:, s, :], ALU.add).then_inc(rope_q, 1)
                    dve.wait_ge(part_h, n + 1)
                    V.tensor_tensor(rq[:, s, :], rq[:, s, :], parts[:, s, 0, :], ALU.subtract).then_inc(part_r, 1)
                    dve.wait_ge(part_m, n + 1)
                    V.tensor_tensor(parts[:, s, 2, :], rq[:, s, :], parts[:, s, 1, :], ALU.subtract).then_inc(part_l, 1)

            def s_unit(h, s):
                i, gp, kh = SUNITS[s]
                slot = s % 2
                w = min(P * (i + 1), 512) if kh == 0 else P * (i - 3)
                dve.wait_ge(s_full, h * NSE + s + 1)
                V.tensor_reduce(mxp[:, kh, 2 * gp:2 * gp + 2, i], ps[:, 2 * slot:2 * slot + 2, 0:w], AXX, ALU.max)\
                    .then_inc(s_read, 1)

            def maxima(h, mod):
                dve.wait_ge(s_read, h * NSE + NS)
                V.tensor_tensor(nm[:, :], mxp[:, 0, :, :].rearrange("p g i -> p (g i)"),
                                mxp[:, 1, :, :].rearrange("p g i -> p (g i)"), ALU.max).then_inc(nm_ready, 1)
                dve.wait_ge(s_full, h * NSE + NS + 1)
                if not (isinstance(h, int) and h == 0):
                    dve.wait_ge(mrow_in, 48 * h)
                V.tensor_scalar(mt[:, 0, :], ps[0:32, 0, 0:P], -1.0, None, ALU.mult).then_inc(s_read, 1)
                dve.wait_ge(s_read, h * NSE + NS + 1)
                link(V.tensor_copy(mparts[:, 0, :], mt[:, 0, :]))
                link(V.tensor_tensor(mt[:, 1, :], mt[:, 0, :], mparts[:, 0, :], ALU.subtract))
                link(V.tensor_copy(mparts[:, 1, :], mt[:, 1, :]))
                V.tensor_tensor(mparts[:, 2, :], mt[:, 1, :], mparts[:, 1, :], ALU.subtract).then_inc(mt_parts, 1)
                dve.wait_ge(s_full, h * NSE + NSE)
                if not (isinstance(h, int) and h == 0):
                    dve.wait_ge(modrow_out, 32 * h)
                V.tensor_copy(full[:, 0, 0:MODW // 4], ps[:, 2, 0:MODW // 4]).then_inc(s_read, 1)

            def ctx_norm(n):
                for b in range(2):
                    v = ps[:, 6 + b, :].rearrange("p (g i c) -> p g i c", g=G, c=32)
                    dve.wait_ge(o_turned, 2 * n + b + 1)
                    link(V.reciprocal(rec[:, b, :, :], v[:, :, :, 16]))
                    V.tensor_tensor(att[:, 4 * b:4 * b + 4, bass.ds(n * G * DH, G * DH)]
                                    .rearrange("p i (g d) -> p g i d", g=G),
                                    v[:, :, :, 0:DH], rec[:, b, :, :].unsqueeze(3).to_broadcast([P, G, 4, DH]),
                                    ALU.mult).then_inc(o_read, 1)

            def head_body(n, nxt, nxt2):
                if nxt:
                    for s in range(AHEAD, NS):
                        s_unit(n + 1, s)
                    maxima(n + 1, True)
                if nxt2:
                    for s in range(AHEAD):
                        s_unit(n + 2, s)
                ctx_norm(n)

            evacuated(dve, ("vT", 1))
            dve.wait_ge(maxp_init, 1)
            for s in range(NS):
                s_unit(0, s)
            maxima(0, True)
            for s in range(AHEAD):
                s_unit(1, s)
            with dve.Fori(0, NKV - 2) as n:
                chain.enter(n, 5)
                head_body(n, True, True)
            chain.leave(NKV - 2)
            head_body(NKV - 2, True, False)
            dve.wait_ge(ga_in, 16)
            floor_gate(gabc[:, :], gtmp[:, :]).then_inc(ga_ready, 1)
            head_body(NKV - 1, False, False)
            b = filled(dve, "modT")
            link(V.tensor_copy(modc[:, :], ps[:, b, 0:40]))
            for c0 in (8, 20):
                link(V.tensor_scalar(modc[:, c0:c0 + 4], modc[:, c0:c0 + 4], 1.0, None, ALU.add))
            V.tensor_scalar(modc[:, 32:36], modc[:, 32:36], 1.0, None, ALU.add).then_inc(read_b[b], 1)
            n = 0
            for hf in range(2):
                for c in range(KC):
                    split_lo(n, ("aT", hf, c), aTr[0][:, c, tok[hf]], aTr[1][:, c, tok[hf]])
                    n += 1

            def add_x(job, t, other):
                b = filled(dve, job)
                V.tensor_tensor(x[:, t, :], ps[:, b, :], other, ALU.add).then_inc(read_b[b], 1)
                return job

            for t in range(NT):
                add_x(("wo", t), t, x[:, t, :])
                if t == 3:
                    evacuated(dve, ("wo", 3))
                    dve.wait_ge(lpart_out, 48)
                    ln_stats(1, 0)
                    ln_norm(1, 0)
            evacuated(dve, ("wo", 7))
            ln_stats(1, 1)
            ln_hi_(1, 0)
            ln_norm(1, 1)
            ln_hi_(1, 1)

            dve.wait_ge(ffbc_in, 48)
            link(floor_gate(gb0[:, :], gb0t[:, :]))
            link(V.tensor_tensor(bb[:, :], bb[:, :], gb0[:, :], ALU.mult))
            V.tensor_tensor(gg[:, :], gg[:, :], gb0[:, :], ALU.mult).then_inc(gg_ready, 1)
            for hf in range(2):
                for m in range(2):
                    split_lo(n, ("fc1", hf, m), lat[0][:, m, tok[hf]], lat[1][:, m, tok[hf]])
                    n += 1
            b = filled(dve, "gateT")
            for t in range(NT):
                ins = V.max(top[:, t, :], ps[:, b, NE * t:NE * t + NE])
            ins.then_inc(read_b[b], 1)
            evacuated(dve, "gateT")
            V.tensor_tensor(s2[:, :], top[:, :, 0], top[:, :, 1], ALU.add).then_inc(s_top, 1)
            with dve.Fori(0, HC0 // 2) as i:
                for j in range(2):
                    for hf in range(2):
                        name = ("up", j, hf)
                        k = prods.before(name, i)
                        s = prods.at[name][0] % 2
                        dve.wait_ge(pr_first, k + 1)
                        b = banks.at[name][0]
                        V.tensor_tensor(xnb[:, s, :], ps[:, b, :], full[:, s, :], ALU.mult).then_inc(read_b[b], 1)
                        dve.wait_ge(pr_hi, k + 1)
                        c = bass.ds(2 * i + j, 1)
                        V.tensor_tensor(u[1][:, c, tok[hf]].rearrange("p o n -> p (o n)"), xnb[:, s, :],
                                        u[0][:, c, tok[hf]].rearrange("p o n -> p (o n)").bitcast(F32),
                                        ALU.subtract).then_inc(pr_lo, 1)
            for hf in range(2):
                for m in range(2):
                    split_lo(n, ("eo", hf, m), eo[0][:, m, tok[hf]], eo[1][:, m, tok[hf]])
                    n += 1

            def mlp_norm(t):
                s = t % 2
                dve.wait_ge(y_rstd, t + 1)
                link(V.tensor_scalar(yb[:, s, :], yb[:, s, :], ymv[:, s, 0:1], yrs[:, s, :], ALU.subtract, ALU.mult))
                link(V.tensor_tensor(yb[:, s, :], yb[:, s, :], gg[:, :], ALU.mult))
                dve.wait_ge(bb_added, t + 1)
                V.tensor_tensor(x[:, t, :], x[:, t, :], yb[:, s, :], ALU.add).then_inc(x_mlp, 1)

            dve.wait_ge(gg_ready, 1)
            for t in range(NT + 1):
                if t < NT:
                    s = t % 2
                    evacuated(dve, ("routed", t))
                    b = filled(dve, ("shared", t))
                    if t >= 2:
                        dve.wait_ge(x_mlp, t - 1)
                    V.tensor_tensor(yb[:, s, :], ps[:, b, :], full[:, s, :], ALU.add).then_inc(read_b[b], 1)
                    evacuated(dve, ("shared", t))
                    link(V.bn_stats(yst[:, s, :], yb[:, s, :]))
                    link(V.bn_aggr(ymv[:, s, :], yst[:, s, :]))
                    V.tensor_scalar(yve[:, s, :], ymv[:, s, 1:2], EPS, None, ALU.add).then_inc(y_var, 1)
                if t:
                    mlp_norm(t - 1)
                if t == 4:
                    dve.wait_ge(x_mlp, 4)
                    ln_stats(2, 0)
                    ln_norm(2, 0)
            dve.wait_ge(x_mlp, NT)
            ln_stats(2, 1)
            ln_hi_(2, 0)
            ln_norm(2, 1)
            ln_hi_(2, 1)

            for hf in range(2):
                evacuated(dve, ("mid", hf))
                link(V.tensor_copy(mid[0][:, tok[hf]], midf[:, tok[hf]]))
                V.tensor_tensor(mid[1][:, tok[hf]], midf[:, tok[hf]], mid[0][:, tok[hf]].bitcast(F32), ALU.subtract)\
                    .then_inc(mid_lo, 1)
            dve.wait_ge(ab_in, 64)
            link(floor_gate(t36[:, :], dg[:, :, :].rearrange("p t n -> p (t n)")))
            link(V.tensor_tensor(Bbc[:, :], Bbc[:, :], t38[:, :], ALU.add))
            link(V.tensor_tensor(Bbc[:, :], Bbc[:, :], t36[:, :], ALU.mult))
            V.scalar_tensor_tensor(out=Abc[:, :], in0=Abc[:, :], scalar=1.0, in1=t36[:, :], op0=ALU.add,
                                   op1=ALU.mult).then_inc(ab_ready, 1)
            for t in range(NT):
                hf = t // 4
                V.tensor_scalar(rt[:, t, :], x[:, t, :], mv[:, hf, t % 4, 0:1], rs[:, hf, t % 4:t % 4 + 1],
                                ALU.subtract, ALU.mult).then_inc(rn_ready, 1)
            for y in range(2):
                for hf in range(2):
                    for m in range(2):
                        evacuated(dve, ("xs", y, hf, m))
                        link(V.tensor_copy(xsr[0][:, m, tok[hf]], xs[:, m, tok[hf]]))
                        V.tensor_tensor(xsr[1][:, m, tok[hf]], xs[:, m, tok[hf]], xsr[0][:, m, tok[hf]].bitcast(F32),
                                        ALU.subtract).then_inc(xs_lo, 1)
                for hf in range(2):
                    for m in range(2):
                        n = 4 * y + 2 * hf + m
                        b = filled(dve, ("fd", y, hf, m))
                        if y:
                            dve.wait_ge(sq_ready, n - 3)
                        V.scalar_tensor_tensor(out=yz[:, m, tok[hf]], in0=ps[:, b, :], scalar=cols[:, C_D + m:C_D + m + 1],
                                               in1=xs[:, m, tok[hf]], op0=ALU.add, op1=ALU.mult).then_inc(read_b[b], 1)
                        evacuated(dve, ("z", y, hf, m))
                        evacuated(dve, ("fd", y, hf, m))
                        V.tensor_tensor(yz[:, m, tok[hf]], yz[:, m, tok[hf]], sz[:, m, tok[hf]], ALU.mult)\
                            .then_inc(yz_ready, 1)
                        dve.wait_ge(yz_ready, n + 1)
                        link(V.tensor_copy(yzr[0][:, m, tok[hf]], yz[:, m, tok[hf]]))
                        V.tensor_tensor(yzr[1][:, m, tok[hf]], yz[:, m, tok[hf]], yzr[0][:, m, tok[hf]].bitcast(F32),
                                        ALU.subtract).then_inc(yz_lo, 1)
                for hf in range(2):
                    b = filled(dve, ("ssq", y, hf))
                    V.tensor_scalar(hms[:, :], ps[:, b, 0:4], 1.0 / DIN, EPS, ALU.mult, ALU.add).then_inc(read_b[b], 1)
                    dve.wait_ge(mr_ready, 2 * y + hf + 1)
                    if 2 * y + hf:
                        filled(dve, ("rbc", y if hf else 0, 1 - hf))
                    V.tensor_tensor(dg[:, :, :], ident[:, :].unsqueeze(1).to_broadcast([P, 4, P]),
                                    hrs[:, :].unsqueeze(2).to_broadcast([P, 4, P]), ALU.mult).then_inc(dg_ready, 1)
                    evacuated(dve, ("rbc", y, hf))
                    b = filled(dve, ("hout", y, hf))
                    o = hof[:, tok[hf]]
                    if y == 0:
                        V.tensor_tensor(o, ps[:, b, :], rb[:, :], ALU.mult).then_inc(read_b[b], 1)
                        evacuated(dve, ("hout", y, hf))
                    else:
                        V.scalar_tensor_tensor(out=o, in0=ps[:, b, :], scalar=alf[:, 1:2], in1=rb[:, :], op0=ALU.mult,
                                               op1=ALU.mult).then_inc(read_b[b], 1)
                        evacuated(dve, ("hout", y, hf))
                        link(V.scalar_tensor_tensor(out=o, in0=midf[:, tok[hf]], scalar=alf[:, 0:1], in1=o,
                                                    op0=ALU.mult, op1=ALU.add))
                    link(V.tensor_copy(hob[0][:, tok[hf]], o))
                    V.tensor_tensor(hob[1][:, tok[hf]], o, hob[0][:, tok[hf]].bitcast(F32), ALU.subtract)\
                        .then_inc(ho_lo, 1)
            for t in range(NT):
                dve.wait_ge(r_ready, t + 1)
                add_x(("wup", t), t, rt[:, t, :])
                if t == 3:
                    evacuated(dve, ("wup", 3))
                    ln_stats(3, 0)
                    ln_norm(3, 0)
            evacuated(dve, ("wup", 7))
            ln_stats(3, 1)
            ln_hi_(3, 0)
            ln_norm(3, 1)
            ln_hi_(3, 1)

            def merge(piece, jobs, turn=0):
                s = raw_loaded(dve, piece, turn)
                for which, job in enumerate(jobs):
                    b = filled(dve, job, turn)
                    r = raw[:, s, 512 * which:512 * which + 512]
                    V.scalar_tensor_tensor(out=r, in0=ps[:, b, :], scalar=2.0, in1=r, op0=ALU.mult, op1=ALU.add)\
                        .then_inc(read_b[b], 1)

            def gate_unit(i, name, c):
                for hf in range(2):
                    pn = ("g", *name, hf)
                    k = prods.before(pn, i)
                    s = prods.at[pn][0] % 2
                    evacuated(dve, ("h1", *name, hf), i)
                    b = filled(dve, ("h3", *name, hf), i)
                    V.tensor_tensor(xnb[:, s, :], ps[:, b, :], full[:, s, :], ALU.mult).then_inc(read_b[b], 1)
                    dve.wait_ge(pr_hi, k + 1)
                    V.tensor_tensor(gT[1][:, bass.ds(c, 1), tok[hf]].rearrange("p o n -> p (o n)"), xnb[:, s, :],
                                    gT[0][:, bass.ds(c, 1), tok[hf]].rearrange("p o n -> p (o n)").bitcast(F32),
                                    ALU.subtract).then_inc(pr_lo, 1)

            merge(("w13", 0), [("lora", 0), ("lora3", 0)])
            with dve.Fori(0, HC1 // 2) as i:
                merge(("w13", 1), [("lora", "L", 0), ("lora3", "L", 0)], i)
                gate_unit(i, ("L", 0), 2 * i)
                merge(("w13", 2), [("lora", "L", 1), ("lora3", "L", 1)], i)
                gate_unit(i, ("L", 1), 2 * i + 1)
            dve.wait_ge(gb1_in, 16)
            floor_gate(gb1[:, :], gb1t[:, :]).then_inc(gb1_ready, 1)
            gate_unit(0, ("E", 0), HC1 - 1)
            dve.wait_ge(gb1_ready, 1)
            for q in range(2):
                for c in range(HC1):
                    s = raw_loaded(dve, ("w2", q, c))
                    b = filled(dve, ("lora2", q, c))
                    r = raw[:, s, 0:D]
                    V.scalar_tensor_tensor(out=r, in0=ps[:, b, :], scalar=2.0, in1=r, op0=ALU.mult, op1=ALU.add)\
                        .then_inc(read_b[b], 1)
                    evacuated(dve, ("lora2", q, c))
                    V.tensor_tensor(r, r, gb1[:, :], ALU.mult).then_inc(w2_scaled, 1)
                for t in range(4):
                    add_x(("down", q, t), 4 * q + t, x[:, 4 * q + t, :])

        @block.gpsimd
        def _(pool):
            chain = Chain(pool, pool_c)
            link = chain.link
            tok = [slice(0, HALF), slice(HALF, T)]

            def tscopy(dst, src):
                return nc.gpsimd.tensor_scalar(dst, src, 1.0, 0.0, ALU.mult, ALU.add)

            def split(name, n, hi, lo, turn=0, loaded=False, last=True, at=0):
                s = piece_slot(name)
                if not loaded:
                    base, per = pieces.at[name]
                    wait_before(raw_in[s], 16 * (base // 2 + 1) + (8 * per * turn if per else 0))
                r = raw[:, s, at:at + n]
                link(tscopy(hi, r))
                ins = nc.gpsimd.tensor_tensor(lo, r, hi.bitcast(F32), ALU.subtract)
                if last:
                    ins.then_inc(piece_done, 1)

            count = nc.gpsimd.alloc_register("count_waited_for")

            def wait_before(sem_, value):
                if isinstance(value, int):
                    pool.wait_ge(sem_, value)
                else:
                    nc.gpsimd.reg_add(count, value, 0)
                    pool.wait_ge(consts, 1)
                    pool.wait_ge(sem_, count)

            def rstd(L, hf):
                pool.wait_ge(ln_var, 2 * L + hf + 1)
                nc.gpsimd.tensor_tensor(rs[:, hf, :], ve[:, :], mh[:, :], ALU.pow).then_inc(ln_rstd, 1)

            def ln_lo_(L, hf):
                for c in range(KC):
                    n = 8 * L + 4 * hf + c
                    pool.wait_ge(ln_hi, n + 1)
                    nc.gpsimd.tensor_tensor(hT[1][:, c, tok[hf]], full[:, n % 2, :], hT[0][:, c, tok[hf]].bitcast(F32),
                                            ALU.subtract).then_inc(ln_lo, 1)

            wq = [w.rearrange("p c n -> p (c n)") for w in Wqkv]
            rstd(0, 0)
            split(("wqkv", 0), 1024, wq[0][:, 0:1024], wq[1][:, 0:1024])
            rstd(0, 1)
            for k in (1, 2):
                split(("wqkv", k), 1024, wq[0][:, 1024 * k:1024 * k + 1024], wq[1][:, 1024 * k:1024 * k + 1024])
            ln_lo_(0, 0)
            ln_lo_(0, 1)
            pool.wait_ge(trig_in, 32)
            for hf in range(2):
                for m in range(5):
                    n = 5 * hf + m
                    pool.wait_ge(rope_sw, n + 1)
                    nc.gpsimd.tensor_tensor(rsw[:, n % 2, :], rsw[:, n % 2, :], sinb[:, tok[hf]], ALU.mult)\
                        .then_inc(rope_sin, 1)

            pool.wait_ge(lraw_in, 16)
            link(tscopy(lpart[:, 0, :], lraw[:, :]))
            link(nc.gpsimd.tensor_tensor(lraw[:, :], lraw[:, :], lpart[:, 0, :], ALU.subtract))
            link(tscopy(lpart[:, 1, :], lraw[:, :]))
            nc.gpsimd.tensor_tensor(lpart[:, 2, :], lraw[:, :], lpart[:, 1, :], ALU.subtract).then_inc(lpart_ready, 1)
            evacuated(pool, ("vT", 0))
            evacuated(pool, ("vT", 1))
            pool.wait_ge(v_ones, 1)

            def head_v(n):
                if not (isinstance(n, int) and n == 0):
                    wait_before(pv_done, n * NTU)
                nc.gpsimd.tensor_copy(vr[:, :, 0:DH], vtok[:, :, bass.ds(n * DH, DH)]).then_inc(vr_ready, 1)

            with pool.Fori(0, NKV - 1) as n:
                head_v(n)
            head_v(NKV - 1)
            for j in range(KC):
                k, half = divmod(j, 2)
                if j == 0:
                    pool.wait_ge(ga_ready, 1)
                    pool.wait_ge(part_l, 10)
                if half == 0:
                    raw_loaded(pool, ("wo", k))
                r = raw[:, piece_slot(("wo", k)), D * half:D * half + D]
                link(nc.gpsimd.tensor_tensor(r, r, gabc[:, :], ALU.mult))
                split(("wo", k), D, Wo[0][:, j, :], Wo[1][:, j, :], loaded=True, last=half == 1, at=D * half)

            split("fc1", 1024, Wf1[0].rearrange("p a b c -> p (a b c)"), Wf1[1].rearrange("p a b c -> p (a b c)"))
            pool.wait_ge(o_read, 2 * NKV)
            split("gate", KC * NE, Wg[0].rearrange("p a b -> p (a b)"), Wg[1].rearrange("p a b -> p (a b)"))
            split("expert", 2 * LAT, Wex[0].rearrange("p a b -> p (a b)"), Wex[1].rearrange("p a b -> p (a b)"))
            rstd(1, 0)
            rstd(1, 1)
            ln_lo_(1, 0)
            filled(pool, ("wo", NT - 1))
            split("fc2", 1024, Wf2[0].rearrange("p a b -> p (a b)"), Wf2[1].rearrange("p a b -> p (a b)"))
            ln_lo_(1, 1)

            def up_pieces(turn, j):
                c = 2 * turn + j
                s = piece_slot(("up", j))
                if isinstance(turn, int) and turn == 0:
                    filled(pool, ("fc1", 1, 1))
                else:
                    filled(pool, ("up", j, 1), turn - 1)
                split(("up", j), D, Wup[j][0].rearrange("p a b -> p (a b)"), Wup[j][1].rearrange("p a b -> p (a b)"),
                      turn)
                pool.wait_ge(dn_hi, c + 1)
                nc.gpsimd.tensor_tensor(Wd0[1][:, bass.ds(c, 1), :].rearrange("p o n -> p (o n)"),
                                        raw[:, piece_slot(("down", j)), 0:D],
                                        Wd0[0][:, bass.ds(c, 1), :].rearrange("p o n -> p (o n)").bitcast(F32),
                                        ALU.subtract).then_inc(piece_done, 1)

            for j in range(2):
                up_pieces(0, j)
            pool.wait_ge(gg_ready, 1)
            pool.wait_ge(ln_xn, 16)
            for t in range(NT):
                nc.gpsimd.tensor_tensor(x[:, t, :], x[:, t, :], bb[:, :], ALU.add).then_inc(bb_added, 1)
            with pool.Fori(0, HC0 // 2 - 1) as i:
                chain.enter(i, 2)
                for j in range(2):
                    up_pieces(i + 1, j)
            chain.leave(HC0 // 2 - 1)
            for j in range(2):
                filled(pool, ("up", j, 1), HC0 // 2 - 1)
            split("wdown", D, Wdn[0].rearrange("p a b -> p (a b)"), Wdn[1].rearrange("p a b -> p (a b)"))
            split("hin", D, Whi[0].rearrange("p a b -> p (a b)"), Whi[1].rearrange("p a b -> p (a b)"))
            for t in range(NT):
                pool.wait_ge(y_var, t + 1)
                nc.gpsimd.tensor_tensor(yrs[:, t % 2, :], yve[:, t % 2, :], mh[:, 0:1], ALU.pow).then_inc(y_rstd, 1)
                if t == 4:
                    rstd(2, 0)
            rstd(2, 1)
            ln_lo_(2, 0)
            ln_lo_(2, 1)

            filled(pool, ("routed", NT - 1))
            split("fcd", D, Wfd[0].rearrange("p a b c -> p (a b c)"), Wfd[1].rearrange("p a b c -> p (a b c)"))
            raw_loaded(pool, "hout")
            s = piece_slot("hout")
            for k in range(2):
                r = raw[:, s, P * k:P * k + P]
                link(nc.gpsimd.tensor_scalar(r, r, cols[:, C_NW + k:C_NW + k + 1], 0.0, ALU.mult, ALU.add))
            split("hout", 2 * P, Who[0].rearrange("p a b -> p (a b)"), Who[1].rearrange("p a b -> p (a b)"), loaded=True)

            def inv_rms(y, hf):
                evacuated(pool, ("ssq", y, hf))
                nc.gpsimd.tensor_tensor(hrs[:, :], hms[:, :], mh[:, :], ALU.pow).then_inc(mr_ready, 1)

            def rest(t):
                r = rt[:, t, :]
                pool.wait_ge(rn_ready, t + 1)
                link(nc.gpsimd.tensor_tensor(r, r, Abc[:, :], ALU.mult))
                link(nc.gpsimd.tensor_tensor(r, r, Bbc[:, :], ALU.add))
                nc.gpsimd.tensor_tensor(r, r, x[:, t, :], ALU.add).then_inc(r_ready, 1)

            raw_loaded(pool, "wup")
            pool.wait_ge(ab_ready, 1)
            r = raw[:, piece_slot("wup"), 0:D]
            link(nc.gpsimd.tensor_tensor(r, r, t36[:, :], ALU.mult))
            split("wup", D, Wuo[0], Wuo[1], loaded=True)
            rest(0)
            inv_rms(0, 0)
            inv_rms(0, 1)
            for t in range(1, 4):
                rest(t)
            inv_rms(1, 0)
            inv_rms(1, 1)
            for t in range(4, NT):
                rest(t)
            rstd(3, 0)
            rstd(3, 1)
            ln_lo_(3, 0)
            ln_lo_(3, 1)

            def w13_lo(slot, name, k):
                pool.wait_ge(w_hi, k + 1)
                nc.gpsimd.tensor_tensor(W13[slot][1].rearrange("p a b c -> p (a b c)"), raw[:, piece_slot(name), :],
                                        W13[slot][0].rearrange("p a b c -> p (a b c)").bitcast(F32),
                                        ALU.subtract).then_inc(piece_done, 1)

            w13_lo(0, ("w13", 0), 0)
            with pool.Fori(0, HC1 // 2) as i:
                w13_lo(1, ("w13", 1), 2 * i + 1)
                w13_lo(0, ("w13", 2), 2 * i + 2)
            for q in range(2):
                for c in range(HC1):
                    k = q * HC1 + c
                    pool.wait_ge(w_hi, HC1 + k + 1)
                    nc.gpsimd.tensor_tensor(W2[k % 2][1], raw[:, piece_slot(("w2", q, c)), 0:D],
                                            W2[k % 2][0].bitcast(F32), ALU.subtract).then_inc(piece_done, 1)


def _rope(np):
    f = np.float32
    inv = f(1.0) / np.power(f(500000.0), np.arange(0, DH, 2, dtype=f) / f(DH)).astype(f)
    wavelen = f(2.0 * np.pi) / inv
    lo, hi = 1024 / 4.0, 1024 / 1.0
    scaled = np.where(wavelen > hi, inv / f(32.0), inv)
    smooth = (f(1024) / wavelen - f(1.0)) / f(3.0)
    smoothed = (f(1.0) - smooth) * scaled / f(32.0) + smooth * scaled
    scaled = np.where(~(wavelen < hi) & ~(wavelen > lo), smoothed, scaled).astype(f)
    angle = (np.arange(T, dtype=f)[:, None] * scaled[None, :]).astype(f).astype(np.float64)
    cos, sin = np.cos(angle).T, np.sin(angle).T
    return (np.tile(np.concatenate([cos, cos]), (NKV, 1)).astype(f),
            np.tile(np.concatenate([-sin, sin]), (NKV, 1)).astype(f))


def _layout(np, i):
    g = lambda name: np.asarray(i[name])
    c = np.ascontiguousarray
    d = {}

    def chunks(w):
        return c(w.reshape(-1, P, w.shape[1]).transpose(1, 0, 2)).reshape(P, -1)

    d["x"] = g("L0_attn_x").reshape(T, D)
    wq = g("L0_attn_Wq").T.reshape(D, NKV, G, DH).transpose(0, 2, 1, 3).reshape(D, D)
    d["wqkv"] = chunks(np.concatenate([wq, g("L0_attn_Wk").T, g("L0_attn_Wv").T], axis=1))
    d["wo"] = chunks(g("L0_attn_Wo").T)
    d["cos"], d["sin"] = _rope(np)
    d["ident"] = np.eye(P, dtype=np.float32)
    mask = np.where(np.arange(P)[:, None] >= np.arange(P)[None, :], 0.0, NEG).astype(np.float32)
    d["mask"] = c(np.concatenate([mask, mask.T], axis=1))
    m0, m1 = g("L0_wmod"), g("L1_wmod")
    d["wm0"] = chunks(m0[:, :1024])
    rest = np.concatenate([m0[:, 1024:], m1], axis=1)
    d["wmr"] = np.stack([chunks(rest[:, MODW * k:MODW * (k + 1)]) for k in range(8)])

    def col(v, n):
        return np.asarray(v).reshape(n, P).T

    gate1 = np.broadcast_to(g("L1_attn_gate1").reshape(1, 1), (P, 1))
    d["cols"] = c(np.concatenate([
        col(g("L0_c"), KC), col(g("L1_c"), KC), gate1, col(g("L1_attn_b_down"), 1),
        col(g("L1_attn_hy_conv_w")[:DIN, 0, 6], 2), col(g("L1_attn_hy_conv_b")[:DIN], 2),
        col(np.repeat(g("L1_attn_hy_D"), 64), 2), col(g("L1_attn_hy_norm_w"), 2)], axis=1))

    def outchunks(w):
        k, n = w.shape
        return c(w.reshape(k // P, P, n // P, P).transpose(2, 1, 0, 3)).reshape(n // P, P, k)

    d["fc1"] = c(outchunks(g("L0_ffn_fc1_w")).transpose(1, 0, 2)).reshape(P, -1)
    d["gate"] = chunks(g("L0_ffn_gate_w"))
    d["expert"] = chunks(g("L0_ffn_expert_w"))
    d["fc2"] = chunks(g("L0_ffn_fc2_w"))
    d["up"] = outchunks(g("L0_ffn_up_w"))
    d["down"] = g("L0_ffn_down_w").reshape(HC0, P, D)
    d["gamma"], d["beta"], d["bup"] = g("L0_ffn_ln_gamma"), g("L0_ffn_ln_beta"), g("L1_attn_b_up")
    d["wdown"] = chunks(g("L1_attn_w_down").T)
    d["hin"] = c(g("L1_attn_hy_in_w")[:2 * DIN].T)
    d["fcd"] = chunks(np.repeat(g("L1_attn_hy_fcD_w").T, 64, axis=1))
    d["hout"] = chunks(g("L1_attn_hy_out_w").T)
    d["wup"] = c(g("L1_attn_w_up").T)
    pad = HC1 * P - HID1

    def padrows(w):
        return np.concatenate([w, np.zeros((pad, w.shape[1]), w.dtype)], axis=0)

    w1, w3 = (outchunks(padrows(g(n)).T) for n in ("L1_ffn_w1", "L1_ffn_w3"))
    d["w13"] = c(np.concatenate([w1, w3], axis=2))
    d["w2"] = padrows(g("L1_ffn_w2").T).reshape(HC1, P, D)
    d["lora"] = c(np.concatenate([
        g("L1_ffn_lora_A1"), g("L1_ffn_lora_A3"), padrows(g("L1_ffn_lora_A2").T).T,
        padrows(g("L1_ffn_lora_B1")).T, padrows(g("L1_ffn_lora_B3")).T, g("L1_ffn_lora_B2").T],
        axis=1)).reshape(P, -1)
    return d


def kernel(**inputs):
    import numpy as _np
    import concourse.bacc as _bacc
    from concourse import mybir as _mybir
    from concourse.bass_utils import run_bass_kernel_spmd as _run

    nc = _bacc.Bacc("TRN2", target_bir_lowering=False, num_devices=1)
    arrays, args = {}, {}
    for name, v in _layout(_np, inputs).items():
        arrays[f"in_{name}"] = _np.ascontiguousarray(v)
        args[name] = nc.dram_tensor(f"in_{name}", v.shape, _mybir.dt.from_np(v.dtype), kind="ExternalInput").ap()
    out = nc.dram_tensor("out_x", (T, D), _mybir.dt.float32, kind="ExternalOutput").ap()
    adaln_two_blocks(nc, args, out)
    r = _run(nc, [arrays], core_ids=[0])
    return _np.asarray(r.results[0]["out_x"]).reshape(1, T, D)
```

```python
from contextlib import ExitStack

import concourse.bass as bass
from concourse import mybir

F32 = mybir.dt.float32
F32R = mybir.dt.float32r
BF16 = mybir.dt.bfloat16
ALU = mybir.AluOpType
ACT = mybir.ActivationFunctionType
AXX = mybir.AxisListType.X

P = 128
T = 1024
D = 512
NT = T // P
KC = D // P
HALF = T // 2
NKV, G, DH = 8, 4, 16
KROWS = 6 * DH
EPS = 1e-5
NEG = -3.0e38
HID0, LAT, NE = 1024, 256, 8
HC0 = HID0 // P
HID1 = 1376
HC1 = (HID1 + P - 1) // P
R = 16
LROWS = 6 * R
MODW = 640
DIN = 256

SB0 = 16512
AR_WORDS = 43008
HT_W, ACT_W, WR_W = 0, 8192, 8192 + 22528
X_B = SB0 + 4 * AR_WORDS
XN_B = X_B + 16384
RAW_B = XN_B + 8192
FULL_B = RAW_B + 8192
MISC_B = FULL_B + 4096
HT_B = SB0
ACT_B = SB0 + 4 * ACT_W
WR_B = SB0 + 4 * WR_W


class Order:

    def __init__(self):
        self.n = 0
        self.at = {}

    def add(self, name):
        assert name not in self.at, name
        self.at[name] = (self.n, 0)
        self.n += 1

    def loop(self, names, turns):
        for k, name in enumerate(names):
            self.at[name] = (self.n + k, len(names))
        self.n += turns * len(names)

    def before(self, name, turn=0):
        base, per = self.at[name]
        return base + turn * per if per else base


class Banks:

    def __init__(self):
        self.count = [0] * 8
        self.at = {}
        self.next = 0

    def add(self, name, bank=None):
        assert name not in self.at, name
        if bank is None:
            bank = self.next
            self.next = (self.next + 1) % 8
        self.at[name] = (bank, self.count[bank], 0)
        self.count[bank] += 1

    def loop(self, names, turns):
        start = list(self.count)
        mine = []
        for name in names:
            self.add(name)
            mine.append((name, *self.at[name][:2]))
        per = [self.count[b] - start[b] for b in range(8)]
        for name, b, c in mine:
            self.at[name] = (b, c, per[b])
        for b in range(8):
            self.count[b] = start[b] + turns * per[b]

    def get(self, name, turn=0):
        b, c, per = self.at[name]
        return b, (c + turn * per if per else c)


MIXER = [("mid", 0, 0), ("in", 0, 0), ("ln", 0, 1), ("mid", 0, 1), ("fd", 0, 0), ("in", 0, 1),
         ("out", 0, 0), ("fd", 0, 1), ("scale", 0, 0), ("out", 0, 1), ("in", 1, 0), ("scale", 0, 1),
         ("fd", 1, 0), ("in", 1, 1), ("out", 1, 0), ("fd", 1, 1), ("scale", 1, 0), ("lora", 1, 1), ("out", 1, 1),
         ("up", 1, 0), ("scale", 1, 1), ("up", 1, 1)]
W2_AHEAD = 4


def plan():
    banks, pieces, prods = Banks(), Order(), Order()
    banks.add("mod0")
    banks.add("mod0T")
    for hf in range(2):
        for c in range(KC):
            banks.add(("ln", 0, hf, c))
    for hf in range(2):
        for m in range(6):
            banks.add(("qkv", hf, m))
        banks.add(("vT", hf))
    banks.attn = list(banks.count)
    banks.add("modT")
    for hf in range(2):
        for c in range(KC):
            banks.add(("aT", hf, c))
    def turned(L, hf):
        for c in range(KC):
            banks.add(("ln", L, hf, c))

    for t in range(NT):
        banks.add(("wo", t))
        if t == 5:
            turned(1, 0)
    for hf in range(2):
        banks.add(("gate", hf))
        for m in range(2):
            banks.add(("fc1", hf, m))
        if hf == 0:
            turned(1, 1)
    banks.add("gateT")
    banks.loop([("up", j, hf) for j in range(2) for hf in range(2)], HC0 // 2)
    for hf in range(2):
        for m in range(2):
            banks.add(("eo", hf, m))
    for t in range(NT):
        banks.add(("shared", t))
        banks.add(("routed", t))
        if t == 6:
            turned(2, 0)
    for kind, y, hf in MIXER:
        if kind == "ln":
            turned(2, 1)
        elif kind == "mid":
            banks.add(("mid", hf))
        elif kind == "in":
            for m in range(2):
                banks.add(("xs", y, hf, m))
            for m in range(2):
                banks.add(("z", y, hf, m))
        elif kind == "fd":
            for m in range(2):
                banks.add(("fd", y, hf, m))
        elif kind == "out":
            banks.add(("ssq", y, hf))
            banks.add(("hout", y, hf))
        elif kind == "scale":
            banks.add(("rbc", y, hf))
        elif kind == "lora":
            for c in range(2):
                banks.add(("lora", "F", c))
                banks.add(("lora3", "F", c))
        else:
            for t in range(4 * hf, 4 * hf + 4):
                banks.add(("wup", t))
                if t == 6:
                    turned(3, 0)
    for j in range(2):
        if j == 1:
            banks.add(("lora", "F", 2))
            banks.add(("lora3", "F", 2))
        for hf in range(2):
            banks.add(("h1", "F", j, hf))
            banks.add(("h3", "F", j, hf))
            if (j, hf) == (0, 0):
                turned(3, 1)
    banks.loop([x for j in range(2) for x in
                [("lora", "L", j), ("lora3", "L", j), ("h1", "L", j, 0), ("h3", "L", j, 0),
                 ("h1", "L", j, 1), ("h3", "L", j, 1)]], HC1 // 2 - 1)
    for k in range(W2_AHEAD):
        banks.add(("lora2", k))
    for hf in range(2):
        banks.add(("h1", "E", 0, hf))
        banks.add(("h3", "E", 0, hf))
    for q in range(2):
        for t in range(4):
            banks.add(("down", q, t), bank=4 * q + t)
        if q == 0:
            for c in range(W2_AHEAD, HC1):
                banks.add(("lora2", c), bank=4 + c % 4)
    for k in range(3):
        pieces.add(("wqkv", k))
    for k in range(2):
        pieces.add(("wo", k))
    pieces.add("fc1")
    pieces.add("gate")
    pieces.add("expert")
    pieces.loop([("up", 0), ("down", 0), ("up", 1), ("down", 1)], HC0 // 2)
    pieces.add("fc2")
    pieces.add("wdown")
    pieces.add("hin")
    pieces.add("fcd")
    pieces.add("hout")
    pieces.add("wup")
    for c in range(3):
        pieces.add(("w13", c))
    pieces.loop([("w13", "L", 0), ("w13", "L", 1)], HC1 // 2 - 1)
    base = pieces.at[("w13", 0)][0]
    pieces.at[("w13", "even")] = (base + 2, 2)
    pieces.at[("w13", "last")] = (base + HC1 - 1, 0)
    for c in range(HC1):
        pieces.add(("w2", c))
    prods.loop([("up", j, hf) for j in range(2) for hf in range(2)], HC0 // 2)
    for j in range(2):
        for hf in range(2):
            prods.add(("g", "F", j, hf))
    prods.loop([("g", "L", j, hf) for j in range(2) for hf in range(2)], HC1 // 2 - 1)
    for hf in range(2):
        prods.add(("g", "E", 0, hf))
    return banks, pieces, prods


SUNITS = [(i, gp, kh) for i in range(NT) for gp in range(2) for kh in range(1 if i < 4 else 2)]
NS = len(SUNITS)
NSE = NS + 2
TUNITS = [(j, i) for j in range(NT) for i in range(j, NT)]
NTU = len(TUNITS)
AHEAD = 10
LAG = 3
PRING = 6
assert NTU % PRING == 0 and NTU % 2 == 0


def adaln_two_blocks(nc, a, out):
    banks, pieces, prods = plan()
    with ExitStack() as ctx:
        cursor = [MISC_B]

        def at(name, shape, dt, offset=None):
            if offset is None:
                offset = cursor[0]
                size = 4 if dt in (F32, F32R) else 2
                for n in shape[1:]:
                    size *= n
                cursor[0] += (size + 31) // 32 * 32
            return nc.alloc_sbuf_tensor_at(name, shape, dt, offset=offset)

        def sem(name):
            return ctx.enter_context(nc.semaphore(name))

        AR = at("arena", [P, AR_WORDS], F32R, SB0)

        def ar(word, *dims):
            n = 1
            for d in dims:
                n *= d
            v = AR[:, word:word + n]
            if len(dims) == 2:
                v = v.rearrange("p (a b) -> p a b", b=dims[1])
            if len(dims) == 3:
                v = v.rearrange("p (a b c) -> p a b c", b=dims[1], c=dims[2])
            return v

        K = 256
        hT = [ar(HT_W, KC, T), ar(HT_W + KC * T, KC, T)]
        x = at("x", [P, NT, D], F32, X_B)
        xnb = at("xnb", [P, 4, D], F32, XN_B)
        raw = at("raw", [P, 2, 1024], F32, RAW_B)
        full = at("full", [P, 2, D], F32, FULL_B)
        Qst = at("Qst", [99, NKV, G, T], BF16, ACT_B)
        Kst = at("Kst", [99, NKV, T], BF16, ACT_B + 65536)
        vtok = at("vtok", [P, NT, P], F32, ACT_B + 81920)
        vr = at("vr", [P, NT, 32], F32, ACT_B + 81920 + 4096)
        mt = at("mt", [32, 2, P], F32, ACT_B + 81920 + 5120)
        mparts = at("mparts", [32, 3, P], BF16, ACT_B + 81920 + 6144)
        maskb = at("maskb", [P, 2, P], BF16, ACT_B + 81920 + 7168)
        Wqkv = [ar(WR_W, KC, 768), ar(WR_W + 3072, KC, 768)]
        cosb = at("cosb", [P, T], F32, WR_B + 24 * 1024)
        sinb = at("sinb", [P, T], F32, WR_B + 28 * 1024)
        rsw = at("rsw", [P, 2, HALF], F32, WR_B + 32 * 1024)
        rq = at("rq", [P, 2, HALF], F32, WR_B + 36 * 1024)
        parts = at("parts", [P, 2, 3, HALF], BF16, WR_B + 40 * 1024)
        wm0 = at("wm0", [P, KC, 1024], F32, ACT_B)
        wmr = at("wmr", [P, KC, MODW], F32, WR_B)
        att = at("att", [P, NT, D], F32, HT_B)
        pr = at("pr", [P, PRING, D], F32, HT_B + 16384)
        ot = at("ot", [P, 2, D], F32, HT_B + 16384 + PRING * 2048)
        gabc = at("gabc", [P, D], F32, WR_B + 12 * 1024)
        gtmp = at("gtmp", [P, D], F32, WR_B + 14 * 1024)
        Wo = [ar(WR_W + 24 * K, KC, D), ar(WR_W + 32 * K, KC, D)]
        lraw = at("lraw", [P, 720], F32, XN_B)
        lpart = at("lpart", [P, 3, 720], BF16, XN_B + 2912)
        aTr = [ar(ACT_W, KC, T), ar(ACT_W + 16 * K, KC, T)]
        u = [ar(ACT_W, HC0, T), ar(ACT_W + 32 * K, HC0, T)]
        lat = [ar(ACT_W + 64 * K, 2, T), ar(ACT_W + 72 * K, 2, T)]
        gg = at("gg", [P, D], F32, ACT_B + 80 * 1024)
        bb = at("bb", [P, D], F32, ACT_B + 82 * 1024)
        Wex = [ar(ACT_W + 84 * K, 2, LAT), ar(ACT_W + 86 * K, 2, LAT)]
        yb = at("yb", [P, 2, D], F32, ACT_B + 84 * 1024)
        gb0 = at("gb0", [P, D], F32, ACT_B + 40 * 1024)
        gb0t = at("gb0t", [P, D], F32, ACT_B + 42 * 1024)
        Wg = [ar(ACT_W + 60 * K, KC, NE), ar(ACT_W + 60 * K + 32, KC, NE)]
        lg = at("lg", [NE, T], F32, ACT_B + 56 * 1024)
        eo = [ar(HT_W, 2, T), ar(HT_W + 2048, 2, T)]
        Wd0 = [ar(WR_W, HC0, D), ar(WR_W + 16 * K, HC0, D)]
        Wf2 = [ar(WR_W + 32 * K, 2, D), ar(WR_W + 36 * K, 2, D)]
        Wf1 = [ar(WR_W + 40 * K, 2, KC, P), ar(WR_W + 44 * K, 2, KC, P)]
        Wup = [[ar(WR_W + (40 + 4 * s) * K, KC, P), ar(WR_W + (42 + 4 * s) * K, KC, P)] for s in range(2)]
        midf = at("midf", [P, T], F32, ACT_B)
        mid = [ar(ACT_W + 4 * K, T), ar(ACT_W + 8 * K, T)]
        xs = at("xs", [P, 2, T], F32, ACT_B + 12 * 1024)
        xsr = [ar(ACT_W + 20 * K, 2, T), ar(ACT_W + 28 * K, 2, T)]
        sz = at("sz", [P, 2, T], F32, ACT_B + 36 * 1024)
        yzr = [ar(ACT_W + 44 * K, 2, T), ar(ACT_W + 52 * K, 2, T)]
        sq = at("sq", [P, 2, T], F32, ACT_B + 60 * 1024)
        hob = [ar(ACT_W + 68 * K, T), ar(ACT_W + 72 * K, T)]
        hof = at("hof", [P, T], F32, ACT_B + 76 * 1024)
        yz = at("yz", [P, 2, T], F32, ACT_B + 80 * 1024)
        dg = at("dg", [P, 4, P], F32, WR_B + 8 * 1024)
        rb = at("rb", [P, HALF], F32, WR_B + 10 * 1024)
        Wdn = [ar(WR_W + 40 * K, KC, P), ar(WR_W + 42 * K, KC, P)]
        Whi = [ar(WR_W + 44 * K, 4, P), ar(WR_W + 46 * K, 4, P)]
        Wfd = [ar(WR_W, 2, 2, P), ar(WR_W + 2 * K, 2, 2, P)]
        Who = [ar(WR_W + 4 * K, 2, P), ar(WR_W + 5 * K, 2, P)]
        Wuo = [ar(WR_W + 12 * K, D), ar(WR_W + 14 * K, D)]
        rt = at("rt", [P, NT, D], F32, WR_B + 16 * 1024)
        Abc = at("Abc", [P, D], F32, WR_B + 32 * 1024)
        Bbc = at("Bbc", [P, D], F32, WR_B + 34 * 1024)
        t36 = at("t36", [P, D], F32, WR_B + 36 * 1024)
        t38 = at("t38", [P, D], F32, WR_B + 38 * 1024)
        gT = [ar(ACT_W, HC1, T), ar(ACT_W + 44 * K, HC1, T)]
        W13 = [[ar(WR_W + 16 * K * 0 + (8 * s) * K, 2, KC, P), ar(WR_W + (8 * s + 4) * K, 2, KC, P)] for s in range(2)]
        w2_at = [WR_W + (16 + 4 * k) * K for k in range(4)] + [WR_W + 4 * k * K for k in range(4)]
        w2_at += [HT_W + 4 * k * K for k in range(HC1 - 8)]
        W2 = [[ar(w, D), ar(w + 2 * K, D)] for w in w2_at]
        Ast = at("Ast", [LROWS, 2432], BF16, WR_B + 36 * 1024)
        Bst = at("Bst", [LROWS, 3328], BF16, WR_B + 36 * 1024 + 4864)
        gb1 = at("gb1", [P, D], F32, WR_B + 34 * 1024)
        gb1t = at("gb1t", [P, D], F32, WR_B + 32 * 1024)
        ident = at("ident", [P, P], F32)
        identb = at("identb", [P, P], BF16)
        sc32 = at("sc32", [P, KC, 2, 16], F32)
        cols = at("cols", [P, 18], F32)
        modc = at("modc", [P, 40], F32)
        mod0c = at("mod0c", [P, 8], F32)
        st = at("st", [P, 4, 6], F32)
        mv = at("mv", [P, 2, 4, 2], F32)
        ve = at("ve", [P, 4], F32)
        rs = at("rs", [P, 2, 4], F32)
        mh = at("mh", [P, 4], F32)
        hms = at("hms", [P, 4], F32)
        hrs = at("hrs", [P, 4], F32)
        yst = at("yst", [P, 2, 6], F32)
        ymv = at("ymv", [P, 2, 2], F32)
        yve = at("yve", [P, 2, 1], F32)
        yrs = at("yrs", [P, 2, 1], F32)
        sce = at("sce", [P, 9], F32)
        alf = at("alf", [P, 2], F32)
        mxp = at("mxp", [P, 2, G, NT], F32)
        nm = at("nm", [P, G * NT], F32)
        rec = at("rec", [P, 2, G, 4], F32)
        top = at("top", [P, NT, 8], F32)
        s2 = at("s2", [P, NT], F32)
        ones = at("ones", [P, P], F32)
        assert cursor[0] <= 229344, cursor[0]
        C_C, C_G, C_BD, C_CW, C_CB, C_D, C_NW = 0, 8, 9, 10, 12, 14, 16

        ps = ctx.enter_context(nc.psum_tensor("ps", [P, 8, 512], F32))

        qscr = nc.dram_tensor("q_parts", (3, DH, NKV, G, T), BF16, kind="Internal").ap()
        kscr = nc.dram_tensor("k_parts", (3, DH, NKV, T), BF16, kind="Internal").ap()
        lscr = nc.dram_tensor("lora_parts", (3, R * 5760), BF16, kind="Internal").ap()
        mscr = nc.dram_tensor("mod_rows", (2, 8 * MODW), F32, kind="Internal").ap()

        full_b = [sem(f"bank{b}_full") for b in range(8)]
        read_b = [sem(f"bank{b}_read") for b in range(8)]
        raw_in = [sem(f"raw{s}_loaded") for s in range(2)]
        piece_done, piece_scaled = sem("piece_split"), sem("piece_scaled")
        x_in = [sem(f"x_half{h}_loaded") for h in range(2)]
        c_in, ident_in, mask_in, trig_in, wm0_in = (sem(n) for n in
                                                    ("cols_loaded", "ident_loaded", "mask_loaded", "trig_loaded", "wm0_loaded"))
        consts = sem("consts_ready")
        c_exp, c_silu, maxp_init = sem("exp_c_ready"), sem("silu_c_ready"), sem("maxima_initialised")
        ln_var, ln_rstd, ln_xn = sem("ln_variance_ready"), sem("ln_rstd_ready"), sem("ln_tile_normalised")
        ln_hi, ln_lo_v, ln_lo_g = sem("ln_hi_ready"), sem("ln_lo_by_vector"), sem("ln_lo_by_gpsimd")
        rope_sw, rope_sin, rope_q = sem("rope_swapped"), sem("rope_sin_applied"), sem("rope_done")
        part_h, part_r, part_m, part_l = (sem(f"part_{n}_ready") for n in "hrml")
        part_out = [sem(f"parts{s}_stored") for s in range(2)]
        v_ones = sem("v_ones_ready")
        stack_in = [sem(f"stacks_of_heads{k}_loaded") for k in range(2)]
        k_ones = sem("k_ones_ready")
        s_full, s_read = sem("score_unit_ready"), sem("score_unit_read")
        nm_ready, mt_parts, mrow_in = sem("row_maxima_ready"), sem("max_parts_ready"), sem("max_rows_loaded")
        modrow_out, wmr_in = sem("mod_piece_stored"), sem("mod_weights_loaded")
        t_full, exp_done, pv_done = sem("scoresT_ready"), sem("exp_done"), sem("pv_done")
        vr_ready, o_copied, o_turned, o_read = (sem("v_of_head_ready"), sem("ctx_copied"), sem("ctx_turned"),
                                                sem("ctx_normalised"))
        lraw_in, lpart_ready, lpart_out, lst_in = (sem("lora_loaded"), sem("lora_parts_ready"),
                                                   sem("lora_parts_stored"), sem("lora_stacks_loaded"))
        ga_in, ga_ready = sem("gate_row_loaded"), sem("gate_of_attn_ready")
        modc_in = sem("mod_chunks_loaded")
        sp_hi = sem("evac_hi_ready")
        ffbc_in, gg_ready, bb_added = sem("mlp_rows_loaded"), sem("mlp_gamma_ready"), sem("mlp_beta_added")
        s_top = sem("top2_sum_ready")
        pr_first, pr_hi, pr_lo = sem("factor_ready"), sem("product_hi_ready"), sem("product_lo_ready")
        y_var, y_rstd, x_mlp = sem("mlp_variance_ready"), sem("mlp_rstd_ready"), sem("x_after_mlp_ready")
        ab_in, ab_ready, rn_ready, xb_ready, r_ready = (
            sem("mixer_rows_loaded"), sem("mixer_rows_ready"), sem("mixer_rest_centred"),
            sem("mixer_rest_shifted"), sem("mixer_rest_ready"))
        mid_lo, xs_hi, yz_hi, xs_lo, yz_ready, sq_ready, yz_lo = (sem("mid_lo_ready"), sem("xs_hi_ready"),
                                                    sem("yz_hi_ready"), sem("xs_lo_ready"), sem("yz_ready"),
                                                    sem("yz_squared"), sem("yz_lo_ready"))
        mr_ready, dg_ready, ho_lo = sem("inverse_rms_ready"), sem("inverse_rms_diagonal_ready"), sem("hydra_out_lo_ready")
        dn_hi = sem("down_hi_ready")
        w_hi, w2_scaled = sem("merged_weights_hi_ready"), sem("w2_scaled")
        gb1_in, gb1_ready = sem("gate_mlp_loaded"), sem("gate_mlp_ready")
        out_done = sem("out_stored")
        dve_c, act_c, pool_c = sem("vector_chain"), sem("scalar_chain"), sem("gpsimd_chain")

        def filled(eng, job, turn=0):
            b, n = banks.get(job, turn)
            eng.wait_ge(full_b[b], n + 1)
            return b

        def evacuated(eng, job, turn=0):
            b, n = banks.get(job, turn)
            eng.wait_ge(read_b[b], n + 1)

        def bank_of(eng, job, turn=0):
            b, n = banks.get(job, turn)
            if not (isinstance(n, int) and n == 0):
                eng.wait_ge(read_b[b], n)
            return b

        def piece_slot(name):
            return pieces.at[name][0] % 2

        def raw_loaded(eng, name, turn=0):
            base, per = pieces.at[name]
            eng.wait_ge(raw_in[base % 2], 16 * (base // 2 + 1) + (8 * per * turn if per else 0))
            return base % 2

        def weights(eng, name, turn=0):
            eng.wait_ge(piece_done, pieces.before(name, turn) + 1)

        def ln_split(eng, L, hf):
            eng.wait_ge(ln_lo_v, 2 * (2 * L + hf) + 2)
            eng.wait_ge(ln_lo_g, 2 * (2 * L + hf) + 2)

        class Chain:

            def __init__(self, eng, s):
                self.eng, self.s, self.n, self.turn = eng, s, 0, None

            def link(self, ins):
                ins.then_inc(self.s, 1)
                self.n += 1
                if self.turn is None:
                    self.eng.wait_ge(self.s, self.n)
                else:
                    self.eng.wait_ge(self.s, self.turn * self.per + self.n)

            def tick(self, ins):
                ins.then_inc(self.s, 1)
                self.n += 1

            def wait(self):
                self.eng.wait_ge(self.s, self.n)

            def enter(self, turn, per):
                self.turn, self.per, self.at = turn, per, self.n

            def leave(self, turns):
                assert self.n - self.at == self.per, (self.n - self.at, self.per)
                self.n = self.at + turns * self.per
                self.turn = None

        block = ctx.enter_context(nc.Block())

        @block.sync
        def _(sp):
            def load_piece(name, src, cols_, turn=0):
                n = pieces.before(name, turn)
                s = piece_slot(name)
                if not (isinstance(n, int) and n < 2):
                    sp.wait_ge(piece_done, n - 1)
                sp.dma_start(raw[:, s, 0:cols_], src).then_inc(raw_in[s], 16)

            sp.dma_start(cols[:, 0:18], a["cols"]).then_inc(c_in, 16)
            for t in range(4):
                sp.dma_start(x[:, t, :], a["x"][t * P:(t + 1) * P, :]).then_inc(x_in[0], 16)
            sp.dma_start(wm0[:, :, :].rearrange("p c n -> p (c n)"), a["wm0"]).then_inc(wm0_in, 16)
            sp.dma_start(ident[:, :], a["ident"]).then_inc(ident_in, 16)
            for k in range(2):
                load_piece(("wqkv", k), a["wqkv"][:, 1024 * k:1024 * (k + 1)], 1024)
            for t in range(4, 8):
                sp.dma_start(x[:, t, :], a["x"][t * P:(t + 1) * P, :]).then_inc(x_in[1], 16)
            sp.dma_start(cosb[:, :], a["cos"]).then_inc(trig_in, 16)
            sp.dma_start(sinb[:, :], a["sin"]).then_inc(trig_in, 16)
            load_piece(("wqkv", 2), a["wqkv"][:, 2048:3072], 1024)
            sp.dma_start(rq[:, 0, 0:2 * P], a["mask"]).then_inc(mask_in, 16)

            for n in range(10):
                hf, m = divmod(n, 5)
                sp.wait_ge(part_l, n + 1)
                tok = slice(hf * HALF, (hf + 1) * HALF)
                for q in range(3):
                    src = parts[:, n % 2, q, :]
                    if m < 4:
                        dst = qscr[q, :, :, m, tok].rearrange("d n t -> n d t")
                    else:
                        dst = kscr[q, :, :, tok].rearrange("d n t -> n d t")
                    sp.dma_start(dst, src).then_inc(part_out[n % 2], 16)
            for s in range(2):
                sp.wait_ge(part_out[s], 16 * 15)
            QP, KP = (0, 0, 1, 0, 2, 1), (0, 1, 0, 2, 0, 1)
            for k, (n0, n1) in enumerate(((0, 2), (2, NKV))):
                for r in range(6):
                    rows = slice(DH * r, DH * (r + 1))
                    sp.dma_start(Kst[rows, n0:n1, :], kscr[KP[r], :, n0:n1, :]).then_inc(stack_in[k], 16)
                    sp.dma_start(Qst[rows, n0:n1, :, :].rearrange("p n g t -> p (n g) t"),
                                 qscr[QP[r], :, n0:n1, :, :].rearrange("d n g t -> d (n g) t")).then_inc(stack_in[k], 16)
            sp.dma_start(lraw[:, :], a["lora"]).then_inc(lraw_in, 16)

            b, n = banks.get(("qkv", 1, 5))
            sp.wait_ge(full_b[b], n + 1)
            sp.dma_start(wmr[:, :, :].rearrange("p c n -> p (c n)"), a["wmr"][0]).then_inc(wmr_in, 16)

            def head_dmas(h, more):
                sp.wait_ge(mt_parts, h + 1)
                for q in range(3):
                    sp.dma_start(Qst[KROWS + q:KROWS + q + 1, bass.ds(h, 1), :, :].rearrange("p n g t -> p (n g t)"),
                                 mparts[:, q, :]).then_inc(mrow_in, 16)
                sp.wait_ge(s_read, h * NSE + NSE)
                for blk in range(2):
                    sp.dma_start(mscr[blk, bass.ds(h * MODW, MODW)].rearrange("(q n) -> q n", n=MODW // 4),
                                 full[16 * blk:16 * blk + 97:32, 0, 0:MODW // 4]).then_inc(modrow_out, 16)
                if more:
                    sp.wait_ge(s_full, h * NSE + NSE)
                    sp.dma_start(wmr[:, :, :].rearrange("p c n -> p (c n)"),
                                 a["wmr"][bass.ds(h + 1, 1)].rearrange("o p n -> (o p) n")).then_inc(wmr_in, 16)

            with sp.Fori(0, NKV - 1) as h:
                head_dmas(h, True)
            head_dmas(NKV - 1, False)
            sp.wait_ge(modrow_out, 32 * NKV)

            def row(k):
                return mscr[0 if k < 4 else 1, k * D:(k + 1) * D].rearrange("(o n) -> o n", o=1).to_broadcast([P, D])

            def rowin(name):
                return a[name].rearrange("(o n) -> o n", o=1).to_broadcast([P, D])

            sp.dma_start(gabc[:, :], row(0)).then_inc(ga_in, 16)
            for blk, (k0, k1) in enumerate(((0, 16), (16, 40))):
                sp.dma_start(full[k0:k1, 1, 0:P], mscr[blk, k0 * P:k1 * P].rearrange("(k n) -> k n", n=P))\
                    .then_inc(modc_in, 16)
            for q in range(3):
                sp.wait_ge(lpart_ready, 1)
                sp.dma_start(lscr[q].rearrange("(p n) -> p n", p=P), lpart[:, q, :]).then_inc(lpart_out, 16)
            for k in range(2):
                load_piece(("wo", k), a["wo"][:, 1024 * k:1024 * (k + 1)], 1024)
            load_piece("fc1", a["fc1"], 1024)
            load_piece("gate", a["gate"], KC * NE)
            load_piece("expert", a["expert"], 2 * LAT)
            sp.wait_ge(o_read, 2 * NKV)
            sp.dma_start(gg[:, :], rowin("gamma")).then_inc(ffbc_in, 16)
            sp.dma_start(bb[:, :], rowin("beta")).then_inc(ffbc_in, 16)
            sp.dma_start(gb0[:, :], row(3)).then_inc(ffbc_in, 16)
            with sp.Fori(0, HC0 // 2) as i:
                for j in range(2):
                    for kind in ("up", "down"):
                        load_piece((kind, j), a[kind][bass.ds(2 * i + j, 1)].rearrange("o p n -> (o p) n"), D, i)
            load_piece("fc2", a["fc2"], 1024)
            load_piece("wdown", a["wdown"], D)
            load_piece("hin", a["hin"], D)
            filled(sp, ("routed", NT - 1))
            sp.dma_start(Abc[:, :], row(5)).then_inc(ab_in, 16)
            sp.dma_start(Bbc[:, :], row(4)).then_inc(ab_in, 16)
            sp.dma_start(t36[:, :], row(6)).then_inc(ab_in, 16)
            sp.dma_start(t38[:, :], rowin("bup")).then_inc(ab_in, 16)
            load_piece("fcd", a["fcd"], D)
            load_piece("hout", a["hout"], 2 * P)
            load_piece("wup", a["wup"], D)
            load_piece(("w13", 0), a["w13"][0], 1024)
            sp.wait_ge(lpart_out, 48)
            filled(sp, ("z", 1, 1, 1))
            for r in range(6):
                rows = slice(DH * r, DH * (r + 1))
                lv = [lscr[q].rearrange("(r n) -> r n", r=R) for q in (QP[r], KP[r])]
                sp.dma_start(Ast[rows, :], lv[0][:, 0:2432]).then_inc(lst_in, 16)
                sp.dma_start(Bst[rows, :], lv[1][:, 2432:5760]).then_inc(lst_in, 16)
            for c in (1, 2):
                load_piece(("w13", c), a["w13"][c], 1024)
            sp.wait_ge(r_ready, NT)
            sp.dma_start(gb1[:, :], row(9)).then_inc(gb1_in, 16)
            with sp.Fori(0, HC1 // 2 - 1) as i:
                for j in range(2):
                    load_piece(("w13", "L", j), a["w13"][bass.ds(2 * i + j + 3, 1)].rearrange("o p n -> (o p) n"), 1024, i)
            for c in range(HC1):
                load_piece(("w2", c), a["w2"][c], D)
            for t in range(NT):
                evacuated(sp, ("down", t // 4, t % 4))
                sp.dma_start(out[t * P:(t + 1) * P, :], x[:, t, :]).then_inc(out_done, 16)
            sp.wait_ge(out_done, 16 * NT)

        @block.tensor
        def _(pe):
            def mm(outp, lhs, rhs, start, stop):
                return nc.tensor.matmul(outp, lhs, rhs, start=start, stop=stop, skip_group_check=True)

            def mm3(outp, lhs, rhs, start, stop):
                mm(outp, lhs[0], rhs[0], start, False)
                mm(outp, lhs[0], rhs[1], False, False)
                return mm(outp, lhs[1], rhs[0], False, stop)

            def hilo(pair, f):
                return f(pair[0]), f(pair[1])

            def ln_turn(L, hf):
                pe.wait_ge(ln_xn, 8 * L + 4 * hf + 4)
                for c in range(KC):
                    b = bank_of(pe, ("ln", L, hf, c))
                    for t in range(4):
                        last = nc.tensor.transpose(ps[:, b, t * P:(t + 1) * P], xnb[:, t, c * P:(c + 1) * P],
                                                   ident[:, :])
                    last.then_inc(full_b[b], 1)

            tok = [slice(0, HALF), slice(HALF, T)]

            def tl(t):
                return slice(t * P, (t + 1) * P)

            pe.wait_ge(c_silu, 1)
            pe.wait_ge(wm0_in, 16)
            b = bank_of(pe, "mod0")
            for kc in range(KC):
                for q in range(4):
                    last = mm(ps[32 * q:32 * q + 32, b, 0:256], sc32[:, kc, :, :].rearrange("p l m -> p (l m)"), wm0[:, kc, 256 * q:256 * q + 256],
                              kc == 0, kc == KC - 1)
            last.then_inc(full_b[b], 1)
            evacuated(pe, "mod0")
            pe.wait_ge(ident_in, 16)
            b = bank_of(pe, "mod0T")
            for k in range(2):
                last = nc.tensor.transpose(ps[:, b, k * P:(k + 1) * P], full[:, 0, k * P:(k + 1) * P], ident[:, :])
            last.then_inc(full_b[b], 1)
            for hf in range(2):
                ln_turn(0, hf)
            for hf in range(2):
                ln_split(pe, 0, hf)
                for m in range(6):
                    if hf == 0 and m == 0:
                        weights(pe, ("wqkv", 2))
                    b = bank_of(pe, ("qkv", hf, m))
                    for kc in range(KC):
                        last = mm3(ps[:, b, :], hilo(Wqkv, lambda w: w[:, kc, m * P:(m + 1) * P]),
                                   hilo(hT, lambda h: h[:, kc, tok[hf]]), kc == 0, kc == KC - 1)
                    last.then_inc(full_b[b], 1)
                evacuated(pe, ("qkv", hf, 5))
                b = bank_of(pe, ("vT", hf))
                for t in range(4):
                    last = nc.tensor.transpose(ps[:, b, tl(t)], full[:, hf, tl(t)], ident[:, :])
                last.then_inc(full_b[b], 1)

            def s_unit(h, s):
                slot = s % 2
                i, gp, kh = SUNITS[s]
                if s >= 2:
                    pe.wait_ge(s_read, h * NSE + s - 1)
                elif not (isinstance(h, int) and h == 0):
                    pe.wait_ge(s_read, h * NSE - 1 + s)
                w = min(P * (i + 1), 512) if kh == 0 else P * (i - 3)
                diag = kh == (0 if i < 4 else 1)
                for e in range(2):
                    o = ps[:, 2 * slot + e, :]
                    last = mm(o[:, 0:w], Qst[0:KROWS, bass.ds(h, 1), 2 * gp + e, i * P:(i + 1) * P]
                              .rearrange("p n t -> p (n t)"),
                              Kst[0:KROWS, bass.ds(h, 1), 512 * kh:512 * kh + w].rearrange("p n t -> p (n t)"),
                              True, not diag)
                    if diag:
                        last = mm(o[:, w - P:w], identb[:, :], maskb[:, 0, :], False, True)
                last.then_inc(s_full, 1)

            def max_turn(h):
                pe.wait_ge(s_read, h * NSE + NS - 1)
                pe.wait_ge(nm_ready, h + 1)
                nc.tensor.transpose(ps[0:32, 0, 0:P], nm[:, :], ident[:, :]).then_inc(s_full, 1)

            def mod_step(h):
                pe.wait_ge(s_read, h * NSE + NS)
                pe.wait_ge(wmr_in, 16 * h + 16)
                w = MODW // 4
                for kc in range(KC):
                    for q in range(4):
                        last = mm(ps[32 * q:32 * q + 32, 2, 0:w], sc32[:, kc, :, :].rearrange("p l m -> p (l m)"),
                                  wmr[:, kc, w * q:w * q + w], kc == 0, kc == KC - 1)
                last.then_inc(s_full, 1)

            def t_unit(n, k):
                j, i = TUNITS[k]
                if k == 0:
                    pe.wait_ge(mrow_in, 48 * n + 48)
                if k >= 2:
                    pe.wait_ge(exp_done, n * NTU + k - 1)
                o = ps[:, 4 + k % 2, :].rearrange("p (g t) -> p g t", g=G)
                last = mm(o, Kst[:, bass.ds(n, 1), j * P:(j + 1) * P].rearrange("p n t -> p (n t)"),
                          Qst[:, bass.ds(n, 1), :, i * P:(i + 1) * P].rearrange("p n g t -> p (n g) t"),
                          True, i > j)
                if i == j:
                    last = mm(o, identb[:, :], maskb[:, 1, :].unsqueeze(1).to_broadcast([P, G, P]), False, True)
                last.then_inc(t_full, 1)

            def pv(n, k):
                j, i = TUNITS[k]
                if k == 0:
                    pe.wait_ge(vr_ready, n + 1)
                    if not (isinstance(n, int) and n == 0):
                        pe.wait_ge(o_read, 2 * n)
                pe.wait_ge(exp_done, n * NTU + k + 1)
                q = 32 * (i % 4)
                mm(ps[q:q + 32, 6 + i // 4, :], vr[:, j, :], pr[:, k % PRING, :], j == 0, j == i).then_inc(pv_done, 1)

            def ctx_turn(n):
                for b in range(2):
                    pe.wait_ge(o_copied, 2 * n + b + 1)
                    for g in range(G):
                        last = nc.tensor.transpose(ps[:, 6 + b, tl(g)], ot[:, b, tl(g)], ident[:, :])
                    last.then_inc(o_turned, 1)

            def head_body(n, nxt, nxt2):
                todo = []
                if nxt:
                    todo += [(k * 22 // (NS - AHEAD), s_unit, n + 1, AHEAD + k) for k in range(NS - AHEAD)]
                    todo += [(24, max_turn, n + 1, None), (25, mod_step, n + 1, None)]
                if nxt2:
                    todo += [(26 + k if k < AHEAD - 1 else NTU, s_unit, n + 2, k) for k in range(AHEAD)]
                for k in range(NTU + LAG):
                    if k < NTU:
                        t_unit(n, k)
                    while todo and todo[0][0] <= k:
                        _, f, h, s = todo.pop(0)
                        f(h) if s is None else f(h, s)
                    if k >= LAG:
                        pv(n, k - LAG)
                assert not todo
                ctx_turn(n)

            for b in range(8):
                if banks.attn[b]:
                    pe.wait_ge(read_b[b], banks.attn[b])
            pe.wait_ge(k_ones, 2)
            pe.wait_ge(stack_in[0], 16 * 12)
            for s in range(NS):
                s_unit(0, s)
            max_turn(0)
            mod_step(0)
            for s in range(AHEAD):
                s_unit(1, s)
            pe.wait_ge(stack_in[1], 16 * 12)
            with pe.Fori(0, NKV - 2) as n:
                head_body(n, True, True)
            head_body(NKV - 2, True, False)
            head_body(NKV - 1, False, False)

            pe.wait_ge(o_read, 2 * NKV)
            pe.wait_ge(s_read, NKV * NSE)
            pe.wait_ge(modc_in, 32)
            b = bank_of(pe, "modT")
            nc.tensor.transpose(ps[:, b, 0:40], full[0:40, 1, 0:P], ident[0:40, 0:40]).then_inc(full_b[b], 1)
            for hf in range(2):
                for c in range(KC):
                    b = bank_of(pe, ("aT", hf, c))
                    for t in range(4):
                        last = nc.tensor.transpose(ps[:, b, tl(t)], att[:, 4 * hf + t, c * P:(c + 1) * P], ident[:, :])
                    last.then_inc(full_b[b], 1)
            weights(pe, ("wo", 1))
            for t in range(NT):
                if t % 4 == 0:
                    for c in range(KC):
                        evacuated(pe, ("aT", t // 4, c))
                b = bank_of(pe, ("wo", t))
                for kc in range(KC):
                    last = mm3(ps[:, b, :], hilo(aTr, lambda h: h[:, kc, tl(t)]), hilo(Wo, lambda w: w[:, kc, :]),
                               kc == 0, kc == KC - 1)
                last.then_inc(full_b[b], 1)
                if t == 5:
                    ln_turn(1, 0)

            for hf in range(2):
                ln_split(pe, 1, hf)
                weights(pe, "gate")
                b = bank_of(pe, ("gate", hf))
                for kc in range(KC):
                    last = mm3(ps[0:NE, b, :], hilo(Wg, lambda w: w[:, kc, :]), hilo(hT, lambda h: h[:, kc, tok[hf]]),
                               kc == 0, kc == KC - 1)
                last.then_inc(full_b[b], 1)
                for m in range(2):
                    b = bank_of(pe, ("fc1", hf, m))
                    for kc in range(KC):
                        last = mm3(ps[:, b, :], hilo(Wf1, lambda w: w[:, m, kc, :]),
                                   hilo(hT, lambda h: h[:, kc, tok[hf]]), kc == 0, kc == KC - 1)
                    last.then_inc(full_b[b], 1)
                if hf == 0:
                    ln_turn(1, 1)
            evacuated(pe, ("gate", 0))
            evacuated(pe, ("gate", 1))
            b = bank_of(pe, "gateT")
            for t in range(NT):
                last = nc.tensor.transpose(ps[:, b, NE * t:NE * t + NE], lg[:, tl(t)], ident[0:NE, 0:NE])
            last.then_inc(full_b[b], 1)
            with pe.Fori(0, HC0 // 2) as i:
                for j in range(2):
                    weights(pe, ("up", j), i)
                    for hf in range(2):
                        b = bank_of(pe, ("up", j, hf), i)
                        for kc in range(KC):
                            last = mm3(ps[:, b, :], hilo(Wup[j], lambda w: w[:, kc, :]),
                                       hilo(hT, lambda h: h[:, kc, tok[hf]]), kc == 0, kc == KC - 1)
                        last.then_inc(full_b[b], 1)
            weights(pe, "expert")
            for hf in range(2):
                for m in range(2):
                    evacuated(pe, ("fc1", hf, m))
                for m in range(2):
                    b = bank_of(pe, ("eo", hf, m))
                    for kc in range(2):
                        last = mm3(ps[:, b, :], hilo(Wex, lambda w: w[:, kc, m * P:(m + 1) * P]),
                                   hilo(lat, lambda h: h[:, kc, tok[hf]]), kc == 0, kc == 1)
                    last.then_inc(full_b[b], 1)
            pe.wait_ge(pr_lo, 2 * HC0)
            for t in range(NT):
                if t == 0:
                    weights(pe, ("down", 1), HC0 // 2 - 1)
                b = bank_of(pe, ("shared", t))
                for kc in range(HC0):
                    last = mm3(ps[:, b, :], hilo(u, lambda h: h[:, kc, tl(t)]), hilo(Wd0, lambda w: w[:, kc, :]),
                               kc == 0, kc == HC0 - 1)
                last.then_inc(full_b[b], 1)
                if t % 4 == 0:
                    for m in range(2):
                        evacuated(pe, ("eo", t // 4, m))
                if t == 0:
                    weights(pe, "fc2")
                b = bank_of(pe, ("routed", t))
                for kc in range(2):
                    last = mm3(ps[:, b, :], hilo(eo, lambda h: h[:, kc, tl(t)]), hilo(Wf2, lambda w: w[:, kc, :]),
                               kc == 0, kc == 1)
                last.then_inc(full_b[b], 1)
                if t == 6:
                    ln_turn(2, 0)

            def lora(name, c, turn=0):
                for which, (kind, o) in enumerate((("lora", 0), ("lora3", HC1 * P))):
                    b = bank_of(pe, (kind, *name), turn)
                    for kc in range(KC):
                        last = mm(ps[:, b, kc * P:(kc + 1) * P],
                                  Ast[:, 512 * which + kc * P:512 * which + (kc + 1) * P],
                                  Bst[:, bass.ds(o + c * P, P)], True, True)
                    last.then_inc(full_b[b], 1)

            for kind, y, hf in MIXER:
                src = mid if y == 0 else hob
                if kind == "ln":
                    ln_turn(2, 1)
                elif kind == "mid":
                    weights(pe, "wdown")
                    ln_split(pe, 2, hf)
                    b = bank_of(pe, ("mid", hf))
                    for kc in range(KC):
                        last = mm3(ps[:, b, :], hilo(Wdn, lambda w: w[:, kc, :]), hilo(hT, lambda h: h[:, kc, tok[hf]]),
                                   kc == 0, kc == KC - 1)
                    last.then_inc(full_b[b], 1)
                elif kind == "in":
                    weights(pe, "hin")
                    pe.wait_ge(mid_lo if y == 0 else ho_lo, hf + 1)
                    for job, m0 in (("xs", 2), ("z", 0)):
                        for m in range(2):
                            b = bank_of(pe, (job, y, hf, m))
                            mm3(ps[:, b, :], hilo(Whi, lambda w: w[:, m0 + m, :]), hilo(src, lambda h: h[:, tok[hf]]),
                                True, True).then_inc(full_b[b], 1)
                elif kind == "fd":
                    weights(pe, "hout")
                    pe.wait_ge(xs_lo, 4 * y + 2 * hf + 2)
                    for m in range(2):
                        b = bank_of(pe, ("fd", y, hf, m))
                        for kc in range(2):
                            last = mm3(ps[:, b, :], hilo(Wfd, lambda w: w[:, kc, m, :]),
                                       hilo(xsr, lambda h: h[:, kc, tok[hf]]), kc == 0, kc == 1)
                        last.then_inc(full_b[b], 1)
                elif kind == "out":
                    pe.wait_ge(sq_ready, 4 * y + 2 * hf + 2)
                    b = bank_of(pe, ("ssq", y, hf))
                    for t in range(4):
                        for kc in range(2):
                            last = mm(ps[:, b, t:t + 1], sq[:, kc, tl(4 * hf + t)], ones[:, 0:1], kc == 0, kc == 1)
                    last.then_inc(full_b[b], 1)
                    pe.wait_ge(yz_lo, 4 * y + 2 * hf + 2)
                    b = bank_of(pe, ("hout", y, hf))
                    for kc in range(2):
                        last = mm3(ps[:, b, :], hilo(Who, lambda w: w[:, kc, :]), hilo(yzr, lambda h: h[:, kc, tok[hf]]),
                                   kc == 0, kc == 1)
                    last.then_inc(full_b[b], 1)
                elif kind == "scale":
                    pe.wait_ge(dg_ready, 2 * y + hf + 1)
                    b = bank_of(pe, ("rbc", y, hf))
                    mm(ps[:, b, :], ones[:, :], dg[:, :, :].rearrange("p t n -> p (t n)"), True, True)\
                        .then_inc(full_b[b], 1)
                elif kind == "lora":
                    pe.wait_ge(lst_in, 16 * 12)
                    for c in range(2):
                        lora(("F", c), c)
                else:
                    weights(pe, "wup")
                    pe.wait_ge(ho_lo, 2 + hf + 1)
                    for t in range(4 * hf, 4 * hf + 4):
                        b = bank_of(pe, ("wup", t))
                        mm3(ps[:, b, :], hilo(hob, lambda h: h[:, tl(t)]), Wuo, True, True).then_inc(full_b[b], 1)
                        if t == 6:
                            ln_turn(3, 0)

            def gated(name, piece, slot, halves=(0, 1), turn=0):
                weights(pe, piece, turn)
                for hf in halves:
                    for which, kind in enumerate(("h1", "h3")):
                        b = bank_of(pe, (kind, *name, hf), turn)
                        for kc in range(KC):
                            last = mm3(ps[:, b, :], hilo(W13[slot], lambda w: w[:, which, kc, :]),
                                       hilo(hT, lambda h: h[:, kc, tok[hf]]), kc == 0, kc == KC - 1)
                        last.then_inc(full_b[b], 1)

            def lora2(c):
                b = bank_of(pe, ("lora2", c))
                mm(ps[:, b, :], Ast[:, 1024 + c * P:1024 + (c + 1) * P], Bst[:, 2 * HC1 * P:2 * HC1 * P + D], True, True)\
                    .then_inc(full_b[b], 1)

            ln_split(pe, 3, 0)
            gated(("F", 0), ("w13", 0), 0, (0,))
            ln_turn(3, 1)
            ln_split(pe, 3, 1)
            gated(("F", 0), ("w13", 0), 0, (1,))
            lora(("F", 2), 2)
            gated(("F", 1), ("w13", 1), 1)
            with pe.Fori(0, HC1 // 2 - 1) as i:
                lora(("L", 0), 2 * i + 3, i)
                gated(("L", 0), ("w13", "even"), 0, turn=i)
                lora(("L", 1), 2 * i + 4, i)
                gated(("L", 1), ("w13", "L", 0), 1, turn=i)
            for c in range(W2_AHEAD):
                lora2(c)
            gated(("E", 0), ("w13", "last"), 0)
            for q in range(2):
                for c in range(HC1):
                    if q == 0 and c == 0:
                        for k in range(W2_AHEAD, W2_AHEAD + 3):
                            lora2(k)
                    elif q == 0 and c + 6 < HC1:
                        lora2(c + 6)
                    if q == 0 and c == 0:
                        pe.wait_ge(pr_lo, 2 * HC0 + 2 * HC1)
                    if q == 0:
                        weights(pe, ("w2", c))
                    for t in range(4):
                        b = bank_of(pe, ("down", q, t)) if c == 0 else banks.get(("down", q, t))[0]
                        last = mm3(ps[:, b, :], hilo(gT, lambda h: h[:, c, tl(4 * q + t)]), W2[c], c == 0, c == HC1 - 1)
                        if c == HC1 - 1:
                            last.then_inc(full_b[b], 1)

        @block.scalar
        def _(act):
            A = nc.scalar.activation
            chain = Chain(act, act_c)

            def ln_full(L, hf, c, scale, bias):
                n = 8 * L + 4 * hf + c
                b = filled(act, ("ln", L, hf, c))
                if n >= 2:
                    act.wait_ge(ln_lo_v if c % 2 else ln_lo_g, n // 2)
                A(full[:, n % 2, :], ps[:, b, :], ACT.Identity, scale=scale, bias=bias).then_inc(read_b[b], 1)

            def split_hi(job, dst):
                b = filled(act, job)
                A(dst, ps[:, b, :], ACT.Copy).then_inc(sp_hi, 1)

            tok = [slice(0, HALF), slice(HALF, T)]

            act.wait_ge(c_in, 16)
            A(sce[:, :], cols[:, 0:9], ACT.Exp, scale=-1.0).then_inc(c_exp, 1)
            b = filled(act, "mod0")
            A(full[:, 0, 0:256], ps[:, b, 0:256], ACT.Copy).then_inc(read_b[b], 1)
            evacuated(act, "mod0T")
            for hf in range(2):
                for c in range(KC):
                    ln_full(0, hf, c, mod0c[:, 4 + c:5 + c], mod0c[:, c:c + 1])
            for hf in range(2):
                for m in range(5):
                    n = 5 * hf + m
                    act.wait_ge(rope_q, n + 1)
                    if n >= 2:
                        act.wait_ge(part_out[n % 2], 48 * (n // 2))
                    A(parts[:, n % 2, 0, :], rq[:, n % 2, :], ACT.Copy).then_inc(part_h, 1)
                    act.wait_ge(part_r, n + 1)
                    A(parts[:, n % 2, 1, :], rq[:, n % 2, :], ACT.Copy).then_inc(part_m, 1)
                b = filled(act, ("qkv", hf, 5))
                if hf == 0:
                    ln_split(act, 0, 1)
                A(full[:, hf, :], ps[:, b, :], ACT.Copy).then_inc(read_b[b], 1)
                b = filled(act, ("vT", hf))
                A(vtok[:, 4 * hf:4 * hf + 4, :].rearrange("p t n -> p (t n)"), ps[:, b, :], ACT.Copy)\
                    .then_inc(read_b[b], 1)

            def head_body(n):
                for k in range(NTU):
                    act.wait_ge(t_full, n * NTU + k + 1)
                    if k >= PRING:
                        act.wait_ge(pv_done, n * NTU + k - PRING + 1)
                    elif k == 0 and not (isinstance(n, int) and n == 0):
                        act.wait_ge(pv_done, n * NTU)
                    A(pr[:, k % PRING, :], ps[:, 4 + k % 2, :], ACT.Exp, scale=float(DH) ** -0.5).then_inc(exp_done, 1)
                act.wait_ge(pv_done, n * NTU + NTU)
                for b in range(2):
                    A(ot[:, b, :], ps[:, 6 + b, :], ACT.Copy).then_inc(o_copied, 1)

            with act.Fori(0, NKV) as n:
                head_body(n)
            for hf in range(2):
                for c in range(KC):
                    split_hi(("aT", hf, c), aTr[0][:, c, tok[hf]])
            evacuated(act, "modT")

            for hf in range(2):
                for c in range(KC):
                    ln_full(1, hf, c, modc[:, 8 + c:9 + c], modc[:, 4 + c:5 + c])
                b = filled(act, ("gate", hf))
                A(lg[:, tok[hf]], ps[0:NE, b, :], ACT.Copy).then_inc(read_b[b], 1)
                for m in range(2):
                    split_hi(("fc1", hf, m), lat[0][:, m, tok[hf]])

            def relu_unit(i, j, hf):
                name = ("up", j, hf)
                s = prods.at[name][0] % 2
                b = filled(act, name, i)
                A(full[:, s, :], ps[:, b, :], ACT.Relu).then_inc(pr_first, 1)
                evacuated(act, name, i)
                A(u[0][:, bass.ds(2 * i + j, 1), tok[hf]].rearrange("p o n -> p (o n)"), xnb[:, s, :], ACT.Copy)\
                    .then_inc(pr_hi, 1)

            def down_hi(i, j):
                s = raw_loaded(act, ("down", j), i)
                A(Wd0[0][:, bass.ds(2 * i + j, 1), :].rearrange("p o n -> p (o n)"), raw[:, s, 0:D], ACT.Copy)\
                    .then_inc(dn_hi, 1)

            def up_turn(i, more):
                for j in range(2):
                    if j == 0:
                        down_hi(i, 1)
                    elif more:
                        down_hi(i + 1, 0)
                    for hf in range(2):
                        relu_unit(i, j, hf)

            ln_split(act, 1, 1)
            down_hi(0, 0)
            with act.Fori(0, HC0 // 2 - 1) as i:
                up_turn(i, True)
            up_turn(HC0 // 2 - 1, False)
            for hf in range(2):
                for m in range(2):
                    split_hi(("eo", hf, m), eo[0][:, m, tok[hf]])
            act.wait_ge(s_top, 1)
            for t in range(NT):
                if t == NT - 1:
                    act.wait_ge(y_var, t)
                    for c in range(KC):
                        ln_full(2, 0, c, modc[:, 20 + c:21 + c], modc[:, 16 + c:17 + c])
                    act.wait_ge(ln_lo_v, 2 * (2 * 2 + 0) + 2)
                elif t >= 2:
                    act.wait_ge(y_var, t - 1)
                b = filled(act, ("routed", t))
                A(full[:, t % 2, :], ps[:, b, :], ACT.Copy, scale=s2[:, t:t + 1]).then_inc(read_b[b], 1)

            def w13_hi(piece, slot, job, turn=0):
                evacuated(act, job, turn)
                A(W13[slot][0][:, :, :, :].rearrange("p a c n -> p (a c n)"), raw[:, piece_slot(piece), :], ACT.Copy)\
                    .then_inc(w_hi, 1)

            def squares(y, hf):
                for m in range(2):
                    act.wait_ge(yz_ready, 4 * y + 2 * hf + m + 1)
                    if y == 1:
                        filled(act, ("hout", 0, hf))
                    A(yzr[0][:, m, tok[hf]], yz[:, m, tok[hf]], ACT.Copy).then_inc(yz_hi, 1)
                    A(sq[:, m, tok[hf]], yz[:, m, tok[hf]], ACT.Square).then_inc(sq_ready, 1)

            for kind, y, hf in MIXER:
                if kind == "ln":
                    act.wait_ge(y_var, NT)
                    for c in range(KC):
                        ln_full(2, 1, c, modc[:, 20 + c:21 + c], modc[:, 16 + c:17 + c])
                elif kind == "mid":
                    b = filled(act, ("mid", hf))
                    A(midf[:, tok[hf]], ps[:, b, :], ACT.Gelu, bias=cols[:, C_BD:C_BD + 1]).then_inc(read_b[b], 1)
                elif kind == "in":
                    for m in range(2):
                        b = filled(act, ("xs", y, hf, m))
                        if y == 1:
                            act.wait_ge(yz_ready, 2 * hf + m + 1)
                            act.wait_ge(xs_lo, 2 * hf + m + 1)
                        A(xs[:, m, tok[hf]], ps[:, b, :], ACT.Silu, scale=cols[:, C_CW + m:C_CW + m + 1],
                          bias=cols[:, C_CB + m:C_CB + m + 1]).then_inc(read_b[b], 1)
                        evacuated(act, ("xs", y, hf, m))
                        A(xsr[0][:, m, tok[hf]], xs[:, m, tok[hf]], ACT.Copy).then_inc(xs_hi, 1)
                    for m in range(2):
                        b = filled(act, ("z", y, hf, m))
                        A(sz[:, m, tok[hf]], ps[:, b, :], ACT.Silu).then_inc(read_b[b], 1)
                elif kind == "fd":
                    squares(y, hf)
                elif kind == "scale":
                    b = filled(act, ("rbc", y, hf))
                    if 2 * y + hf >= 1:
                        evacuated(act, ("hout", y if hf else 0, 1 - hf))
                    A(rb[:, :], ps[:, b, :], ACT.Copy).then_inc(read_b[b], 1)
                elif kind == "up" and hf == 0:
                    filled(act, ("hout", 1, 1))
                    w13_hi(("w13", 0), 0, ("lora3", "F", 0))

            def gate_unit(i, name, c):
                for hf in range(2):
                    pn = ("g", *name, hf)
                    s = prods.at[pn][0] % 2
                    b = filled(act, ("h1", *name, hf), i)
                    A(full[:, s, :], ps[:, b, :], ACT.Silu).then_inc(read_b[b], 1)
                    evacuated(act, ("h3", *name, hf), i)
                    A(gT[0][:, bass.ds(c, 1), tok[hf]].rearrange("p o n -> p (o n)"), xnb[:, s, :], ACT.Copy)\
                        .then_inc(pr_hi, 1)

            for c in range(KC):
                ln_full(3, 0, c, modc[:, 32 + c:33 + c], modc[:, 28 + c:29 + c])
            filled(act, ("wup", NT - 1))
            w13_hi(("w13", 1), 1, ("lora3", "F", 1))
            for c in range(KC):
                ln_full(3, 1, c, modc[:, 32 + c:33 + c], modc[:, 28 + c:29 + c])
            ln_split(act, 3, 1)
            gate_unit(0, ("F", 0), 0)
            w13_hi(("w13", 2), 0, ("lora3", "F", 2))
            gate_unit(0, ("F", 1), 1)
            with act.Fori(0, HC1 // 2 - 1) as i:
                w13_hi(("w13", "L", 0), 1, ("lora3", "L", 0), i)
                gate_unit(i, ("L", 0), 2 * i + 2)
                w13_hi(("w13", "L", 1), 0, ("lora3", "L", 1), i)
                gate_unit(i, ("L", 1), 2 * i + 3)

            def w2_hi(c):
                act.wait_ge(w2_scaled, c + 1)
                A(W2[c][0], raw[:, piece_slot(("w2", c)), 0:D], ACT.Copy).then_inc(w_hi, 1)

            for c in range(W2_AHEAD):
                w2_hi(c)
            gate_unit(0, ("E", 0), HC1 - 1)
            filled(act, ("h3", "E", 0, 1))
            for c in range(W2_AHEAD, HC1):
                w2_hi(c)

        @block.vector
        def _(dve):
            V = nc.vector
            chain = Chain(dve, dve_c)
            link = chain.link
            tok = [slice(0, HALF), slice(HALF, T)]

            def ln_stat(hf, t):
                chain.tick(V.bn_stats(st[:, t, :], x[:, 4 * hf + t, :]))

            def ln_finish(L, hf):
                chain.wait()
                for t in range(4):
                    ins = V.bn_aggr(mv[:, hf, t, :], st[:, t, :])
                    if t < 3:
                        chain.tick(ins)
                link(ins)
                V.tensor_scalar(ve[:, :], mv[:, hf, :, 1], EPS, None, ALU.add).then_inc(ln_var, 1)

            def ln_norm(L, hf):
                dve.wait_ge(ln_rstd, 2 * L + hf + 1)
                if hf:
                    filled(dve, ("ln", L, 0, KC - 1))
                for t in range(4):
                    V.tensor_scalar(xnb[:, t, :], x[:, 4 * hf + t, :], mv[:, hf, t, 0:1], rs[:, hf, t:t + 1],
                                    ALU.subtract, ALU.mult).then_inc(ln_xn, 1)

            def ln_hi_(L, hf):
                for c in range(KC):
                    n = 8 * L + 4 * hf + c
                    evacuated(dve, ("ln", L, hf, c))
                    V.tensor_copy(hT[0][:, c, tok[hf]], full[:, n % 2, :]).then_inc(ln_hi, 1)
                    if c % 2:
                        dve.wait_ge(ln_hi, n + 1)
                        V.tensor_tensor(hT[1][:, c, tok[hf]], full[:, n % 2, :], hT[0][:, c, tok[hf]].bitcast(F32),
                                        ALU.subtract).then_inc(ln_lo_v, 1)

            def split_lo(order_n, job, hi, dst):
                dve.wait_ge(sp_hi, order_n + 1)
                b = banks.get(job)[0]
                V.tensor_tensor(dst, ps[:, b, :], hi.bitcast(F32), ALU.subtract).then_inc(read_b[b], 1)

            def floor_gate(v, tmp):
                link(V.tensor_scalar(tmp, v, 0.0, 2.0, ALU.is_ge, ALU.mult))
                link(V.scalar_tensor_tensor(out=v, in0=v, scalar=-1.0, in1=v, op0=ALU.mult, op1=ALU.max))
                link(V.tensor_scalar(v, v, 0.25, None, ALU.max))
                return V.scalar_tensor_tensor(out=v, in0=tmp, scalar=-1.0, in1=v, op0=ALU.add, op1=ALU.mult)

            V.memset(ones[:, :], 1.0).then_inc(consts, 1)
            V.memset(mh[:, :], -0.5).then_inc(consts, 1)
            V.memset(mxp[:, :, :, :], NEG).then_inc(maxp_init, 1)
            dve.wait_ge(c_exp, 1)
            link(V.tensor_scalar(sce[:, :], sce[:, :], 1.0, None, ALU.add))
            link(V.reciprocal(sce[:, :], sce[:, :]))
            V.tensor_tensor(sc32[:, :, :, :].rearrange("p k l m -> p l k m"),
                            cols[:, 0:8].rearrange("p (l k) -> p l k", l=2).unsqueeze(3).to_broadcast([P, 2, KC, 16]),
                            sce[:, 0:8].rearrange("p (l k) -> p l k", l=2).unsqueeze(3).to_broadcast([P, 2, KC, 16]),
                            ALU.mult).then_inc(c_silu, 1)
            V.tensor_scalar(alf[:, 0:1], sce[:, 8:9], 1.0, None, ALU.add).then_inc(consts, 1)
            V.tensor_scalar(alf[:, 1:2], sce[:, 8:9], -1.0, 1.0, ALU.mult, ALU.add).then_inc(consts, 1)
            dve.wait_ge(consts, 4)
            for hf in range(2):
                dve.wait_ge(x_in[hf], 64)
                for t in range(4):
                    ln_stat(hf, t)
                ln_finish(0, hf)
                if hf == 0:
                    ln_norm(0, 0)
            dve.wait_ge(ident_in, 16)
            V.tensor_copy(identb[:, :], ident[:, :]).then_inc(k_ones, 1)
            b = filled(dve, "mod0T")
            cview = ps[:, b, 0:256].rearrange("p (k q m) -> p q k m", k=2, m=32)[:, :, :, 0]
            link(V.tensor_copy(mod0c[:, 0:4].rearrange("p (q k) -> p q k", k=2), cview[:, 0:2, :]))
            V.tensor_scalar(mod0c[:, 4:8].rearrange("p (q k) -> p q k", k=2), cview[:, 2:4, :], 1.0, None, ALU.add)\
                .then_inc(read_b[b], 1)
            dve.wait_ge(mask_in, 16)
            link(V.tensor_copy(maskb[:, :, :].rearrange("p a b -> p (a b)"), rq[:, 0, 0:2 * P]))
            ln_norm(0, 1)
            for hf in range(2):
                ln_hi_(0, hf)
            V.memset(vr[:, :, 16:32], 1.0).then_inc(v_ones, 1)
            V.memset(Kst[KROWS:KROWS + 3, :, :], 1.0).then_inc(k_ones, 1)

            dve.wait_ge(trig_in, 32)
            swap = [p ^ 8 for p in range(32)]
            for hf in range(2):
                for m in range(5):
                    n = 5 * hf + m
                    s = n % 2
                    b = filled(dve, ("qkv", hf, m))
                    if n >= 2:
                        dve.wait_ge(part_l, n - 1)
                    V.stream_shuffle(rsw[:, s, :], ps[:, b, :], swap).then_inc(rope_sw, 1)
                    V.tensor_tensor(rq[:, s, :], ps[:, b, :], cosb[:, tok[hf]], ALU.mult).then_inc(read_b[b], 1)
                    dve.wait_ge(rope_sin, n + 1)
                    evacuated(dve, ("qkv", hf, m))
                    V.tensor_tensor(rq[:, s, :], rq[:, s, :], rsw[:, s, :], ALU.add).then_inc(rope_q, 1)
                    dve.wait_ge(part_h, n + 1)
                    V.tensor_tensor(rq[:, s, :], rq[:, s, :], parts[:, s, 0, :], ALU.subtract).then_inc(part_r, 1)
                    dve.wait_ge(part_m, n + 1)
                    V.tensor_tensor(parts[:, s, 2, :], rq[:, s, :], parts[:, s, 1, :], ALU.subtract).then_inc(part_l, 1)

            def s_unit(h, s):
                i, gp, kh = SUNITS[s]
                slot = s % 2
                w = min(P * (i + 1), 512) if kh == 0 else P * (i - 3)
                dve.wait_ge(s_full, h * NSE + s + 1)
                V.tensor_reduce(mxp[:, kh, 2 * gp:2 * gp + 2, i], ps[:, 2 * slot:2 * slot + 2, 0:w], AXX, ALU.max)\
                    .then_inc(s_read, 1)

            def maxima(h, mod):
                dve.wait_ge(s_read, h * NSE + NS)
                V.tensor_tensor(nm[:, :], mxp[:, 0, :, :].rearrange("p g i -> p (g i)"),
                                mxp[:, 1, :, :].rearrange("p g i -> p (g i)"), ALU.max).then_inc(nm_ready, 1)
                dve.wait_ge(s_full, h * NSE + NS + 1)
                if not (isinstance(h, int) and h == 0):
                    dve.wait_ge(mrow_in, 48 * h)
                V.tensor_scalar(mt[:, 0, :], ps[0:32, 0, 0:P], -1.0, None, ALU.mult).then_inc(s_read, 1)
                dve.wait_ge(s_read, h * NSE + NS + 1)
                link(V.tensor_copy(mparts[:, 0, :], mt[:, 0, :]))
                link(V.tensor_tensor(mt[:, 1, :], mt[:, 0, :], mparts[:, 0, :], ALU.subtract))
                link(V.tensor_copy(mparts[:, 1, :], mt[:, 1, :]))
                V.tensor_tensor(mparts[:, 2, :], mt[:, 1, :], mparts[:, 1, :], ALU.subtract).then_inc(mt_parts, 1)
                dve.wait_ge(s_full, h * NSE + NSE)
                if not (isinstance(h, int) and h == 0):
                    dve.wait_ge(modrow_out, 32 * h)
                V.tensor_copy(full[:, 0, 0:MODW // 4], ps[:, 2, 0:MODW // 4]).then_inc(s_read, 1)

            def ctx_norm(n):
                for b in range(2):
                    v = ps[:, 6 + b, :].rearrange("p (g i c) -> p g i c", g=G, c=32)
                    dve.wait_ge(o_turned, 2 * n + b + 1)
                    link(V.reciprocal(rec[:, b, :, :], v[:, :, :, 16]))
                    V.tensor_tensor(att[:, 4 * b:4 * b + 4, bass.ds(n * G * DH, G * DH)]
                                    .rearrange("p i (g d) -> p g i d", g=G),
                                    v[:, :, :, 0:DH], rec[:, b, :, :].unsqueeze(3).to_broadcast([P, G, 4, DH]),
                                    ALU.mult).then_inc(o_read, 1)

            def head_body(n, nxt, nxt2):
                if nxt:
                    for s in range(AHEAD, NS):
                        s_unit(n + 1, s)
                    maxima(n + 1, True)
                if nxt2:
                    for s in range(AHEAD):
                        s_unit(n + 2, s)
                ctx_norm(n)

            evacuated(dve, ("vT", 1))
            dve.wait_ge(maxp_init, 1)
            for s in range(NS):
                s_unit(0, s)
            maxima(0, True)
            for s in range(AHEAD):
                s_unit(1, s)
            with dve.Fori(0, NKV - 2) as n:
                chain.enter(n, 5)
                head_body(n, True, True)
            chain.leave(NKV - 2)
            head_body(NKV - 2, True, False)
            dve.wait_ge(ga_in, 16)
            floor_gate(gabc[:, :], gtmp[:, :]).then_inc(ga_ready, 1)
            head_body(NKV - 1, False, False)
            b = filled(dve, "modT")
            link(V.tensor_copy(modc[:, :], ps[:, b, 0:40]))
            for c0 in (8, 20):
                link(V.tensor_scalar(modc[:, c0:c0 + 4], modc[:, c0:c0 + 4], 1.0, None, ALU.add))
            V.tensor_scalar(modc[:, 32:36], modc[:, 32:36], 1.0, None, ALU.add).then_inc(read_b[b], 1)
            n = 0
            for hf in range(2):
                for c in range(KC):
                    split_lo(n, ("aT", hf, c), aTr[0][:, c, tok[hf]], aTr[1][:, c, tok[hf]])
                    n += 1

            def add_x(job, t, other):
                b = filled(dve, job)
                V.tensor_tensor(x[:, t, :], ps[:, b, :], other, ALU.add).then_inc(read_b[b], 1)
                return job

            for t in range(NT):
                add_x(("wo", t), t, x[:, t, :])
                if t % 4:
                    evacuated(dve, ("wo", t - 1))
                    ln_stat(t // 4, t % 4 - 1)
                if t % 4 == 3:
                    evacuated(dve, ("wo", t))
                    ln_stat(t // 4, 3)
                    ln_finish(1, t // 4)
                if t == 3:
                    dve.wait_ge(lpart_out, 48)
                    ln_norm(1, 0)
                if t == 5:
                    ln_hi_(1, 0)
            ln_norm(1, 1)

            for hf in range(2):
                if hf:
                    ln_hi_(1, 1)
                for m in range(2):
                    split_lo(n, ("fc1", hf, m), lat[0][:, m, tok[hf]], lat[1][:, m, tok[hf]])
                    n += 1
            b = filled(dve, "gateT")
            for t in range(NT):
                ins = V.max(top[:, t, :], ps[:, b, NE * t:NE * t + NE])
            ins.then_inc(read_b[b], 1)
            evacuated(dve, "gateT")
            V.tensor_tensor(s2[:, :], top[:, :, 0], top[:, :, 1], ALU.add).then_inc(s_top, 1)
            dve.wait_ge(ffbc_in, 48)
            link(floor_gate(gb0[:, :], gb0t[:, :]))
            link(V.tensor_tensor(bb[:, :], bb[:, :], gb0[:, :], ALU.mult))
            V.tensor_tensor(gg[:, :], gg[:, :], gb0[:, :], ALU.mult).then_inc(gg_ready, 1)
            with dve.Fori(0, HC0 // 2) as i:
                for j in range(2):
                    for hf in range(2):
                        name = ("up", j, hf)
                        k = prods.before(name, i)
                        s = prods.at[name][0] % 2
                        dve.wait_ge(pr_first, k + 1)
                        b = banks.at[name][0]
                        V.tensor_tensor(xnb[:, s, :], ps[:, b, :], full[:, s, :], ALU.mult).then_inc(read_b[b], 1)
                        dve.wait_ge(pr_hi, k + 1)
                        c = bass.ds(2 * i + j, 1)
                        V.tensor_tensor(u[1][:, c, tok[hf]].rearrange("p o n -> p (o n)"), xnb[:, s, :],
                                        u[0][:, c, tok[hf]].rearrange("p o n -> p (o n)").bitcast(F32),
                                        ALU.subtract).then_inc(pr_lo, 1)
            for hf in range(2):
                for m in range(2):
                    split_lo(n, ("eo", hf, m), eo[0][:, m, tok[hf]], eo[1][:, m, tok[hf]])
                    n += 1

            def mlp_norm(t):
                s = t % 2
                dve.wait_ge(y_rstd, t + 1)
                link(V.tensor_scalar(yb[:, s, :], yb[:, s, :], ymv[:, s, 0:1], yrs[:, s, :], ALU.subtract, ALU.mult))
                link(V.tensor_tensor(yb[:, s, :], yb[:, s, :], gg[:, :], ALU.mult))
                dve.wait_ge(bb_added, t + 1)
                V.tensor_tensor(x[:, t, :], x[:, t, :], yb[:, s, :], ALU.add).then_inc(x_mlp, 1)

            dve.wait_ge(gg_ready, 1)
            for t in range(NT + 1):
                if t == NT - 1:
                    ln_hi_(2, 0)
                if t < NT:
                    s = t % 2
                    evacuated(dve, ("routed", t))
                    b = filled(dve, ("shared", t))
                    if t >= 2:
                        dve.wait_ge(x_mlp, t - 1)
                    V.tensor_tensor(yb[:, s, :], ps[:, b, :], full[:, s, :], ALU.add).then_inc(read_b[b], 1)
                    evacuated(dve, ("shared", t))
                    link(V.bn_stats(yst[:, s, :], yb[:, s, :]))
                    link(V.bn_aggr(ymv[:, s, :], yst[:, s, :]))
                    V.tensor_scalar(yve[:, s, :], ymv[:, s, 1:2], EPS, None, ALU.add).then_inc(y_var, 1)
                if t:
                    mlp_norm(t - 1)
                if t >= 2:
                    dve.wait_ge(x_mlp, t - 1)
                    ln_stat((t - 2) // 4, (t - 2) % 4)
                if t == 5:
                    ln_finish(2, 0)
                    ln_norm(2, 0)
            dve.wait_ge(x_mlp, NT)
            ln_stat(1, 3)
            ln_finish(2, 1)
            ln_norm(2, 1)

            def merge(piece, jobs, turn=0):
                s = raw_loaded(dve, piece, turn)
                for which, job in enumerate(jobs):
                    b = filled(dve, job, turn)
                    r = raw[:, s, 512 * which:512 * which + 512]
                    V.scalar_tensor_tensor(out=r, in0=ps[:, b, :], scalar=2.0, in1=r, op0=ALU.mult, op1=ALU.add)\
                        .then_inc(read_b[b], 1)

            def centred(t):
                V.scalar_tensor_tensor(out=rt[:, t, :], in0=x[:, t, :], scalar=mv[:, t // 4, t % 4, 0:1], in1=Abc[:, :],
                                       op0=ALU.subtract, op1=ALU.mult).then_inc(rn_ready, 1)

            def rest(t):
                dve.wait_ge(xb_ready, t + 1)
                V.scalar_tensor_tensor(out=x[:, t, :], in0=rt[:, t, :], scalar=rs[:, t // 4, t % 4:t % 4 + 1],
                                       in1=x[:, t, :], op0=ALU.mult, op1=ALU.add).then_inc(r_ready, 1)

            for kind, y, hf in MIXER:
                if kind == "ln":
                    ln_hi_(2, 1)
                elif kind == "mid":
                    evacuated(dve, ("mid", hf))
                    link(V.tensor_copy(mid[0][:, tok[hf]], midf[:, tok[hf]]))
                    V.tensor_tensor(mid[1][:, tok[hf]], midf[:, tok[hf]], mid[0][:, tok[hf]].bitcast(F32), ALU.subtract)\
                        .then_inc(mid_lo, 1)
                    if hf:
                        dve.wait_ge(ab_in, 64)
                        link(floor_gate(t36[:, :], rb[:, :]))
                        link(V.tensor_tensor(Bbc[:, :], Bbc[:, :], t38[:, :], ALU.add))
                        link(V.tensor_tensor(Bbc[:, :], Bbc[:, :], t36[:, :], ALU.mult))
                        link(V.scalar_tensor_tensor(out=Abc[:, :], in0=Abc[:, :], scalar=1.0, in1=t36[:, :], op0=ALU.add,
                                                    op1=ALU.mult))
                        for t in range(NT):
                            centred(t)
                elif kind == "fd":
                    for m in range(2):
                        n = 4 * y + 2 * hf + m
                        b = filled(dve, ("fd", y, hf, m))
                        if y:
                            dve.wait_ge(sq_ready, n - 3)
                        V.scalar_tensor_tensor(out=yz[:, m, tok[hf]], in0=ps[:, b, :], scalar=cols[:, C_D + m:C_D + m + 1],
                                               in1=xs[:, m, tok[hf]], op0=ALU.add, op1=ALU.mult).then_inc(read_b[b], 1)
                        evacuated(dve, ("z", y, hf, m))
                        evacuated(dve, ("fd", y, hf, m))
                        V.tensor_tensor(yz[:, m, tok[hf]], yz[:, m, tok[hf]], sz[:, m, tok[hf]], ALU.mult)\
                            .then_inc(yz_ready, 1)
                    for m in range(2):
                        n = 4 * y + 2 * hf + m
                        dve.wait_ge(yz_hi, n + 1)
                        V.tensor_tensor(yzr[1][:, m, tok[hf]], yz[:, m, tok[hf]], yzr[0][:, m, tok[hf]].bitcast(F32),
                                        ALU.subtract).then_inc(yz_lo, 1)
                    if y == 0:
                        for t in range(4 * hf, 4 * hf + 4):
                            rest(t)
                elif kind == "out":
                    b = filled(dve, ("ssq", y, hf))
                    V.tensor_scalar(hms[:, :], ps[:, b, 0:4], 1.0 / DIN, EPS, ALU.mult, ALU.add).then_inc(read_b[b], 1)
                elif kind == "scale":
                    dve.wait_ge(mr_ready, 2 * y + hf + 1)
                    if 2 * y + hf:
                        filled(dve, ("rbc", y if hf else 0, 1 - hf))
                    V.tensor_tensor(dg[:, :, :], ident[:, :].unsqueeze(1).to_broadcast([P, 4, P]),
                                    hrs[:, :].unsqueeze(2).to_broadcast([P, 4, P]), ALU.mult).then_inc(dg_ready, 1)
                    evacuated(dve, ("rbc", y, hf))
                    b = filled(dve, ("hout", y, hf))
                    o = hof[:, tok[hf]]
                    if y == 0:
                        V.tensor_tensor(o, ps[:, b, :], rb[:, :], ALU.mult).then_inc(read_b[b], 1)
                        evacuated(dve, ("hout", y, hf))
                    else:
                        V.scalar_tensor_tensor(out=o, in0=ps[:, b, :], scalar=alf[:, 1:2], in1=rb[:, :], op0=ALU.mult,
                                               op1=ALU.mult).then_inc(read_b[b], 1)
                        evacuated(dve, ("hout", y, hf))
                        link(V.scalar_tensor_tensor(out=o, in0=midf[:, tok[hf]], scalar=alf[:, 0:1], in1=o,
                                                    op0=ALU.mult, op1=ALU.add))
                    if y == 1:
                        filled(dve, ("z", 1, hf, 1))
                    link(V.tensor_copy(hob[0][:, tok[hf]], o))
                    V.tensor_tensor(hob[1][:, tok[hf]], o, hob[0][:, tok[hf]].bitcast(F32), ALU.subtract)\
                        .then_inc(ho_lo, 1)
                elif kind == "lora":
                    for c in range(2):
                        merge(("w13", c), [("lora", "F", c), ("lora3", "F", c)])
                elif kind == "up":
                    for t in range(4 * hf, 4 * hf + 4):
                        if hf == 0:
                            dve.wait_ge(r_ready, t + 1)
                        add_x(("wup", t), t, x[:, t, :])
                        if t % 4:
                            evacuated(dve, ("wup", t - 1))
                            ln_stat(hf, t % 4 - 1)
                    evacuated(dve, ("wup", t))
                    ln_stat(hf, 3)
                    ln_finish(3, hf)
                    if hf == 0:
                        ln_norm(3, 0)
            ln_hi_(3, 0)
            ln_norm(3, 1)
            ln_hi_(3, 1)

            def gate_unit(i, name, c):
                for hf in range(2):
                    pn = ("g", *name, hf)
                    k = prods.before(pn, i)
                    s = prods.at[pn][0] % 2
                    evacuated(dve, ("h1", *name, hf), i)
                    b = filled(dve, ("h3", *name, hf), i)
                    V.tensor_tensor(xnb[:, s, :], ps[:, b, :], full[:, s, :], ALU.mult).then_inc(read_b[b], 1)
                    dve.wait_ge(pr_hi, k + 1)
                    V.tensor_tensor(gT[1][:, bass.ds(c, 1), tok[hf]].rearrange("p o n -> p (o n)"), xnb[:, s, :],
                                    gT[0][:, bass.ds(c, 1), tok[hf]].rearrange("p o n -> p (o n)").bitcast(F32),
                                    ALU.subtract).then_inc(pr_lo, 1)

            gate_unit(0, ("F", 0), 0)
            merge(("w13", 2), [("lora", "F", 2), ("lora3", "F", 2)])
            gate_unit(0, ("F", 1), 1)
            with dve.Fori(0, HC1 // 2 - 1) as i:
                for j in range(2):
                    merge(("w13", "L", j), [("lora", "L", j), ("lora3", "L", j)], i)
                    gate_unit(i, ("L", j), 2 * i + 2 + j)
            dve.wait_ge(gb1_in, 16)
            floor_gate(gb1[:, :], gb1t[:, :]).then_inc(gb1_ready, 1)
            dve.wait_ge(gb1_ready, 1)

            def merge2(c):
                s = raw_loaded(dve, ("w2", c))
                b = filled(dve, ("lora2", c))
                r = raw[:, s, 0:D]
                V.scalar_tensor_tensor(out=r, in0=ps[:, b, :], scalar=2.0, in1=r, op0=ALU.mult, op1=ALU.add)\
                    .then_inc(read_b[b], 1)
                evacuated(dve, ("lora2", c))
                V.tensor_tensor(r, r, gb1[:, :], ALU.mult).then_inc(w2_scaled, 1)

            for c in range(W2_AHEAD):
                merge2(c)
            gate_unit(0, ("E", 0), HC1 - 1)
            for c in range(W2_AHEAD, HC1):
                merge2(c)
            for q in range(2):
                for t in range(4):
                    add_x(("down", q, t), 4 * q + t, x[:, 4 * q + t, :])

        @block.gpsimd
        def _(pool):
            chain = Chain(pool, pool_c)
            link = chain.link
            tok = [slice(0, HALF), slice(HALF, T)]

            def tscopy(dst, src):
                return nc.gpsimd.tensor_scalar(dst, src, 1.0, 0.0, ALU.mult, ALU.add)

            def split(name, n, hi, lo, turn=0, loaded=False, last=True, at=0):
                s = piece_slot(name)
                if not loaded:
                    base, per = pieces.at[name]
                    wait_before(raw_in[s], 16 * (base // 2 + 1) + (8 * per * turn if per else 0))
                r = raw[:, s, at:at + n]
                link(tscopy(hi, r))
                ins = nc.gpsimd.tensor_tensor(lo, r, hi.bitcast(F32), ALU.subtract)
                if last:
                    ins.then_inc(piece_done, 1)

            count = nc.gpsimd.alloc_register("count_waited_for")

            def wait_before(sem_, value):
                if isinstance(value, int):
                    pool.wait_ge(sem_, value)
                else:
                    nc.gpsimd.reg_add(count, value, 0)
                    pool.wait_ge(consts, 1)
                    pool.wait_ge(sem_, count)

            def rstd(L, hf):
                pool.wait_ge(ln_var, 2 * L + hf + 1)
                nc.gpsimd.tensor_tensor(rs[:, hf, :], ve[:, :], mh[:, :], ALU.pow).then_inc(ln_rstd, 1)

            def ln_lo_(L, hf):
                for c in range(0, KC, 2):
                    n = 8 * L + 4 * hf + c
                    pool.wait_ge(ln_hi, n + 1)
                    nc.gpsimd.tensor_tensor(hT[1][:, c, tok[hf]], full[:, n % 2, :], hT[0][:, c, tok[hf]].bitcast(F32),
                                            ALU.subtract).then_inc(ln_lo_g, 1)

            wq = [w.rearrange("p c n -> p (c n)") for w in Wqkv]
            rstd(0, 0)
            split(("wqkv", 0), 1024, wq[0][:, 0:1024], wq[1][:, 0:1024])
            rstd(0, 1)
            for k in (1, 2):
                split(("wqkv", k), 1024, wq[0][:, 1024 * k:1024 * k + 1024], wq[1][:, 1024 * k:1024 * k + 1024])
            ln_lo_(0, 0)
            ln_lo_(0, 1)
            pool.wait_ge(trig_in, 32)
            for hf in range(2):
                for m in range(5):
                    n = 5 * hf + m
                    pool.wait_ge(rope_sw, n + 1)
                    nc.gpsimd.tensor_tensor(rsw[:, n % 2, :], rsw[:, n % 2, :], sinb[:, tok[hf]], ALU.mult)\
                        .then_inc(rope_sin, 1)

            pool.wait_ge(lraw_in, 16)
            link(tscopy(lpart[:, 0, :], lraw[:, :]))
            link(nc.gpsimd.tensor_tensor(lraw[:, :], lraw[:, :], lpart[:, 0, :], ALU.subtract))
            link(tscopy(lpart[:, 1, :], lraw[:, :]))
            nc.gpsimd.tensor_tensor(lpart[:, 2, :], lraw[:, :], lpart[:, 1, :], ALU.subtract).then_inc(lpart_ready, 1)
            evacuated(pool, ("vT", 0))
            evacuated(pool, ("vT", 1))
            pool.wait_ge(v_ones, 1)

            def head_v(n):
                if not (isinstance(n, int) and n == 0):
                    wait_before(pv_done, n * NTU)
                nc.gpsimd.tensor_copy(vr[:, :, 0:DH], vtok[:, :, bass.ds(n * DH, DH)]).then_inc(vr_ready, 1)

            with pool.Fori(0, NKV - 1) as n:
                head_v(n)
            head_v(NKV - 1)
            for j in range(KC):
                k, half = divmod(j, 2)
                if j == 0:
                    pool.wait_ge(ga_ready, 1)
                    pool.wait_ge(part_l, 10)
                if half == 0:
                    raw_loaded(pool, ("wo", k))
                r = raw[:, piece_slot(("wo", k)), D * half:D * half + D]
                link(nc.gpsimd.tensor_tensor(r, r, gabc[:, :], ALU.mult))
                split(("wo", k), D, Wo[0][:, j, :], Wo[1][:, j, :], loaded=True, last=half == 1, at=D * half)

            split("fc1", 1024, Wf1[0].rearrange("p a b c -> p (a b c)"), Wf1[1].rearrange("p a b c -> p (a b c)"))
            pool.wait_ge(o_read, 2 * NKV)
            split("gate", KC * NE, Wg[0].rearrange("p a b -> p (a b)"), Wg[1].rearrange("p a b -> p (a b)"))
            split("expert", 2 * LAT, Wex[0].rearrange("p a b -> p (a b)"), Wex[1].rearrange("p a b -> p (a b)"))
            rstd(1, 0)
            ln_lo_(1, 0)
            rstd(1, 1)
            ln_lo_(1, 1)

            def up_pieces(turn, j):
                c = 2 * turn + j
                s = piece_slot(("up", j))
                if isinstance(turn, int) and turn == 0:
                    filled(pool, ("fc1", 1, 1))
                else:
                    filled(pool, ("up", j, 1), turn - 1)
                split(("up", j), D, Wup[j][0].rearrange("p a b -> p (a b)"), Wup[j][1].rearrange("p a b -> p (a b)"),
                      turn)
                pool.wait_ge(dn_hi, c + 1)
                nc.gpsimd.tensor_tensor(Wd0[1][:, bass.ds(c, 1), :].rearrange("p o n -> p (o n)"),
                                        raw[:, piece_slot(("down", j)), 0:D],
                                        Wd0[0][:, bass.ds(c, 1), :].rearrange("p o n -> p (o n)").bitcast(F32),
                                        ALU.subtract).then_inc(piece_done, 1)

            for j in range(2):
                up_pieces(0, j)
            with pool.Fori(0, HC0 // 2 - 1) as i:
                chain.enter(i, 2)
                for j in range(2):
                    up_pieces(i + 1, j)
            chain.leave(HC0 // 2 - 1)
            for j in range(2):
                filled(pool, ("up", j, 1), HC0 // 2 - 1)
            split("fc2", 1024, Wf2[0].rearrange("p a b -> p (a b)"), Wf2[1].rearrange("p a b -> p (a b)"))
            split("wdown", D, Wdn[0].rearrange("p a b -> p (a b)"), Wdn[1].rearrange("p a b -> p (a b)"))
            split("hin", D, Whi[0].rearrange("p a b -> p (a b)"), Whi[1].rearrange("p a b -> p (a b)"))
            pool.wait_ge(gg_ready, 1)
            pool.wait_ge(ln_xn, 16)
            for t in range(NT):
                nc.gpsimd.tensor_tensor(x[:, t, :], x[:, t, :], bb[:, :], ALU.add).then_inc(bb_added, 1)
                pool.wait_ge(y_var, t + 1)
                nc.gpsimd.tensor_tensor(yrs[:, t % 2, :], yve[:, t % 2, :], mh[:, 0:1], ALU.pow).then_inc(y_rstd, 1)
                if t == 5:
                    rstd(2, 0)
                if t == 6:
                    ln_lo_(2, 0)
            rstd(2, 1)

            def rest(t):
                pool.wait_ge(rn_ready, t + 1)
                nc.gpsimd.tensor_tensor(x[:, t, :], x[:, t, :], Bbc[:, :], ALU.add).then_inc(xb_ready, 1)

            def w13_lo(slot, name, k):
                pool.wait_ge(w_hi, k + 1)
                nc.gpsimd.tensor_tensor(W13[slot][1].rearrange("p a b c -> p (a b c)"), raw[:, piece_slot(name), :],
                                        W13[slot][0].rearrange("p a b c -> p (a b c)").bitcast(F32),
                                        ALU.subtract).then_inc(piece_done, 1)

            for kind, y, hf in MIXER:
                if kind == "ln":
                    ln_lo_(2, 1)
                elif kind == "in":
                    for m in range(2):
                        n = 4 * y + 2 * hf + m
                        pool.wait_ge(xs_hi, n + 1)
                        nc.gpsimd.tensor_tensor(xsr[1][:, m, tok[hf]], xs[:, m, tok[hf]],
                                                xsr[0][:, m, tok[hf]].bitcast(F32), ALU.subtract).then_inc(xs_lo, 1)
                    if (y, hf) == (0, 0):
                        split("fcd", D, Wfd[0].rearrange("p a b c -> p (a b c)"), Wfd[1].rearrange("p a b c -> p (a b c)"))
                        raw_loaded(pool, "hout")
                        s = piece_slot("hout")
                        for k in range(2):
                            r = raw[:, s, P * k:P * k + P]
                            link(nc.gpsimd.tensor_scalar(r, r, cols[:, C_NW + k:C_NW + k + 1], 0.0, ALU.mult, ALU.add))
                        split("hout", 2 * P, Who[0].rearrange("p a b -> p (a b)"), Who[1].rearrange("p a b -> p (a b)"),
                              loaded=True)
                    if (y, hf) == (0, 1):
                        for t in range(NT):
                            rest(t)
                elif kind == "out":
                    evacuated(pool, ("ssq", y, hf))
                    nc.gpsimd.tensor_tensor(hrs[:, :], hms[:, :], mh[:, :], ALU.pow).then_inc(mr_ready, 1)
                    if (y, hf) == (0, 1):
                        raw_loaded(pool, "wup")
                        r = raw[:, piece_slot("wup"), 0:D]
                        link(nc.gpsimd.tensor_tensor(r, r, t36[:, :], ALU.mult))
                        split("wup", D, Wuo[0], Wuo[1], loaded=True)
                elif kind == "up" and hf == 0:
                    w13_lo(0, ("w13", 0), 0)
                    rstd(3, 0)
            rstd(3, 1)
            ln_lo_(3, 0)
            w13_lo(1, ("w13", 1), 1)
            ln_lo_(3, 1)

            w13_lo(0, ("w13", 2), 2)
            with pool.Fori(0, HC1 // 2 - 1) as i:
                w13_lo(1, ("w13", "L", 0), 2 * i + 3)
                w13_lo(0, ("w13", "L", 1), 2 * i + 4)
            for c in range(HC1):
                pool.wait_ge(w_hi, HC1 + c + 1)
                nc.gpsimd.tensor_tensor(W2[c][1], raw[:, piece_slot(("w2", c)), 0:D], W2[c][0].bitcast(F32),
                                        ALU.subtract).then_inc(piece_done, 1)


def _rope(np):
    f = np.float32
    inv = f(1.0) / np.power(f(500000.0), np.arange(0, DH, 2, dtype=f) / f(DH)).astype(f)
    wavelen = f(2.0 * np.pi) / inv
    lo, hi = 1024 / 4.0, 1024 / 1.0
    scaled = np.where(wavelen > hi, inv / f(32.0), inv)
    smooth = (f(1024) / wavelen - f(1.0)) / f(3.0)
    smoothed = (f(1.0) - smooth) * scaled / f(32.0) + smooth * scaled
    scaled = np.where(~(wavelen < hi) & ~(wavelen > lo), smoothed, scaled).astype(f)
    angle = (np.arange(T, dtype=f)[:, None] * scaled[None, :]).astype(f).astype(np.float64)
    cos, sin = np.cos(angle).T, np.sin(angle).T
    return (np.tile(np.concatenate([cos, cos]), (NKV, 1)).astype(f),
            np.tile(np.concatenate([-sin, sin]), (NKV, 1)).astype(f))


def _layout(np, i):
    g = lambda name: np.asarray(i[name])
    c = np.ascontiguousarray
    d = {}

    def chunks(w):
        return c(w.reshape(-1, P, w.shape[1]).transpose(1, 0, 2)).reshape(P, -1)

    d["x"] = g("L0_attn_x").reshape(T, D)
    wq = g("L0_attn_Wq").T.reshape(D, NKV, G, DH).transpose(0, 2, 1, 3).reshape(D, D)
    d["wqkv"] = chunks(np.concatenate([wq, g("L0_attn_Wk").T, g("L0_attn_Wv").T], axis=1))
    d["wo"] = chunks(g("L0_attn_Wo").T)
    d["cos"], d["sin"] = _rope(np)
    d["ident"] = np.eye(P, dtype=np.float32)
    mask = np.where(np.arange(P)[:, None] >= np.arange(P)[None, :], 0.0, NEG).astype(np.float32)
    d["mask"] = c(np.concatenate([mask, mask.T], axis=1))
    m0, m1 = g("L0_wmod"), g("L1_wmod")
    d["wm0"] = chunks(m0[:, :1024])
    rest = np.concatenate([m0[:, 1024:], m1], axis=1)
    d["wmr"] = np.stack([chunks(rest[:, MODW * k:MODW * (k + 1)]) for k in range(8)])

    def col(v, n):
        return np.asarray(v).reshape(n, P).T

    gate1 = np.broadcast_to(g("L1_attn_gate1").reshape(1, 1), (P, 1))
    d["cols"] = c(np.concatenate([
        col(g("L0_c"), KC), col(g("L1_c"), KC), gate1, col(g("L1_attn_b_down"), 1),
        col(g("L1_attn_hy_conv_w")[:DIN, 0, 6], 2), col(g("L1_attn_hy_conv_b")[:DIN], 2),
        col(np.repeat(g("L1_attn_hy_D"), 64), 2), col(g("L1_attn_hy_norm_w"), 2)], axis=1))

    def outchunks(w):
        k, n = w.shape
        return c(w.reshape(k // P, P, n // P, P).transpose(2, 1, 0, 3)).reshape(n // P, P, k)

    d["fc1"] = c(outchunks(g("L0_ffn_fc1_w")).transpose(1, 0, 2)).reshape(P, -1)
    d["gate"] = chunks(g("L0_ffn_gate_w"))
    d["expert"] = chunks(g("L0_ffn_expert_w"))
    d["fc2"] = chunks(g("L0_ffn_fc2_w"))
    d["up"] = outchunks(g("L0_ffn_up_w"))
    d["down"] = g("L0_ffn_down_w").reshape(HC0, P, D)
    d["gamma"], d["beta"], d["bup"] = g("L0_ffn_ln_gamma"), g("L0_ffn_ln_beta"), g("L1_attn_b_up")
    d["wdown"] = chunks(g("L1_attn_w_down").T)
    d["hin"] = c(g("L1_attn_hy_in_w")[:2 * DIN].T)
    d["fcd"] = chunks(np.repeat(g("L1_attn_hy_fcD_w").T, 64, axis=1))
    d["hout"] = chunks(g("L1_attn_hy_out_w").T)
    d["wup"] = c(g("L1_attn_w_up").T)
    pad = HC1 * P - HID1

    def padrows(w):
        return np.concatenate([w, np.zeros((pad, w.shape[1]), w.dtype)], axis=0)

    w1, w3 = (outchunks(padrows(g(n)).T) for n in ("L1_ffn_w1", "L1_ffn_w3"))
    d["w13"] = c(np.concatenate([w1, w3], axis=2))
    d["w2"] = padrows(g("L1_ffn_w2").T).reshape(HC1, P, D)
    d["lora"] = c(np.concatenate([
        g("L1_ffn_lora_A1"), g("L1_ffn_lora_A3"), padrows(g("L1_ffn_lora_A2").T).T,
        padrows(g("L1_ffn_lora_B1")).T, padrows(g("L1_ffn_lora_B3")).T, g("L1_ffn_lora_B2").T],
        axis=1)).reshape(P, -1)
    return d


def kernel(**inputs):
    import numpy as _np
    import concourse.bacc as _bacc
    from concourse import mybir as _mybir
    from concourse.bass_utils import run_bass_kernel_spmd as _run

    nc = _bacc.Bacc("TRN2", target_bir_lowering=False, num_devices=1)
    arrays, args = {}, {}
    for name, v in _layout(_np, inputs).items():
        arrays[f"in_{name}"] = _np.ascontiguousarray(v)
        args[name] = nc.dram_tensor(f"in_{name}", v.shape, _mybir.dt.from_np(v.dtype), kind="ExternalInput").ap()
    out = nc.dram_tensor("out_x", (T, D), _mybir.dt.float32, kind="ExternalOutput").ap()
    adaln_two_blocks(nc, args, out)
    r = _run(nc, [arrays], core_ids=[0])
    return _np.asarray(r.results[0]["out_x"]).reshape(1, T, D)
```

```python
from contextlib import ExitStack

import concourse.bass as bass
from concourse import mybir

F32 = mybir.dt.float32
F32R = mybir.dt.float32r
BF16 = mybir.dt.bfloat16
ALU = mybir.AluOpType
ACT = mybir.ActivationFunctionType
AXX = mybir.AxisListType.X

P = 128
T = 1024
D = 512
NT = T // P
KC = D // P
HALF = T // 2
NKV, G, DH = 8, 4, 16
KROWS = 6 * DH
EPS = 1e-5
NEG = -3.0e38
HID0, LAT, NE = 1024, 256, 8
HC0 = HID0 // P
HID1 = 1376
HC1 = (HID1 + P - 1) // P
R = 16
LROWS = 6 * R
MODW = 640
DIN = 256

SB0 = 16512
AR_WORDS = 43008
HT_W, ACT_W, WR_W = 0, 8192, 8192 + 22528
X_B = SB0 + 4 * AR_WORDS
XN_B = X_B + 16384
RAW_B = XN_B + 8192
FULL_B = RAW_B + 8192
MISC_B = FULL_B + 4096
HT_B = SB0
ACT_B = SB0 + 4 * ACT_W
WR_B = SB0 + 4 * WR_W


class Order:

    def __init__(self):
        self.n = 0
        self.at = {}

    def add(self, name):
        assert name not in self.at, name
        self.at[name] = (self.n, 0)
        self.n += 1

    def loop(self, names, turns):
        for k, name in enumerate(names):
            self.at[name] = (self.n + k, len(names))
        self.n += turns * len(names)

    def before(self, name, turn=0):
        base, per = self.at[name]
        return base + turn * per if per else base


class Banks:

    def __init__(self):
        self.count = [0] * 8
        self.at = {}
        self.next = 0

    def add(self, name, bank=None):
        assert name not in self.at, name
        if bank is None:
            bank = self.next
            self.next = (self.next + 1) % 8
        self.at[name] = (bank, self.count[bank], 0)
        self.count[bank] += 1

    def loop(self, names, turns):
        start = list(self.count)
        mine = []
        for name in names:
            self.add(name)
            mine.append((name, *self.at[name][:2]))
        per = [self.count[b] - start[b] for b in range(8)]
        for name, b, c in mine:
            self.at[name] = (b, c, per[b])
        for b in range(8):
            self.count[b] = start[b] + turns * per[b]

    def get(self, name, turn=0):
        b, c, per = self.at[name]
        return b, (c + turn * per if per else c)


MIXER = [("mid", 0, 0), ("in", 0, 0), ("ln", 0, 1), ("mid", 0, 1), ("fd", 0, 0), ("in", 0, 1),
         ("out", 0, 0), ("dg", 0, 0), ("scale", 0, 0), ("fd", 0, 1), ("in", 1, 0),
         ("out", 0, 1), ("dg", 0, 1), ("rest", 0, 0), ("scale", 0, 1), ("fd", 1, 0), ("in", 1, 1),
         ("out", 1, 0), ("dg", 1, 0), ("rest", 0, 1), ("scale", 1, 0), ("fd", 1, 1), ("up", 1, 0),
         ("out", 1, 1), ("dg", 1, 1), ("lora", 1, 1), ("scale", 1, 1), ("up", 1, 1)]
MIXER_POOL = list(MIXER)
for k in range(1, len(MIXER)):
    if MIXER[k][0] == "out" and MIXER[k - 1][0] == "in":
        MIXER_POOL[k - 1], MIXER_POOL[k] = MIXER[k], MIXER[k - 1]
MIXER_POOL.remove(("out", 1, 1))
MIXER_POOL.insert(MIXER_POOL.index(("up", 1, 0)), ("out", 1, 1))
MIXER_POOL.remove(("ln", 0, 1))
MIXER_POOL.insert(1, ("ln", 0, 1))
W2_PIECES = (HC1 + 1) // 2
W2_AHEAD = 4


def plan():
    banks, pieces, prods = Banks(), Order(), Order()
    banks.add("mod0")
    banks.add("mod0T")
    for c in range(KC):
        banks.add(("ln", 0, 0, c))
    for hf in range(2):
        for m in range(6):
            banks.add(("qkv", hf, m))
            if (hf, m) == (0, 0):
                for c in range(KC):
                    banks.add(("ln", 0, 1, c))
    for hf in range(2):
        banks.add(("vT", hf))
    banks.attn = list(banks.count)
    banks.add("modT")
    for hf in range(2):
        for c in range(KC):
            banks.add(("aT", hf, c))
    def turned(L, hf):
        for c in range(KC):
            banks.add(("ln", L, hf, c))

    for t in range(NT):
        banks.add(("wo", t))
        if t == 5:
            turned(1, 0)
    for hf in range(2):
        banks.add(("gate", hf))
        for m in range(2):
            banks.add(("fc1", hf, m))
        if hf == 0:
            turned(1, 1)
    banks.add("gateT")
    banks.loop([("up", j, hf) for j in range(2) for hf in range(2)], HC0 // 2)
    for hf in range(2):
        for m in range(2):
            banks.add(("eo", hf, m))
    for t in range(NT):
        banks.add(("shared", t))
        banks.add(("routed", t))
        if t == 6:
            turned(2, 0)
    for kind, y, hf in MIXER:
        if kind == "ln":
            turned(2, 1)
        elif kind == "mid":
            banks.add(("mid", hf))
        elif kind == "in":
            for m in range(2):
                banks.add(("xs", y, hf, m))
            for m in range(2):
                banks.add(("z", y, hf, m))
        elif kind == "fd":
            for m in range(2):
                banks.add(("fd", y, hf, m))
        elif kind == "out":
            banks.add(("ssq", y, hf))
            banks.add(("hout", y, hf))
        elif kind == "scale":
            banks.add(("rbc", y, hf))
        elif kind == "lora":
            for c in range(2):
                banks.add(("lora", "F", c))
                banks.add(("lora3", "F", c))
        elif kind == "up":
            if hf:
                turned(3, 0)
            for t in range(4 * hf, 4 * hf + 4):
                banks.add(("wup", t))
    for hf in range(2):
        for j in range(2):
            if (hf, j) == (1, 1):
                banks.add(("lora", "F", 2))
                banks.add(("lora3", "F", 2))
            banks.add(("h1", "F", j, hf))
            banks.add(("h3", "F", j, hf))
        if hf == 0:
            turned(3, 1)
    banks.loop([x for j in range(2) for x in
                [("lora", "L", j), ("lora3", "L", j), ("h1", "L", j, 0), ("h3", "L", j, 0),
                 ("h1", "L", j, 1), ("h3", "L", j, 1)]], HC1 // 2 - 1)
    for k in range(W2_AHEAD):
        banks.add(("lora2", k))
    for hf in range(2):
        banks.add(("h1", "E", 0, hf))
        banks.add(("h3", "E", 0, hf))
    for q in range(2):
        for t in range(4):
            banks.add(("down", q, t), bank=4 * q + t)
        if q == 0:
            for c in range(W2_AHEAD, HC1):
                banks.add(("lora2", c), bank=4 + c % 4)
    for k in range(2):
        pieces.add(("wqkv", k))
    for k in range(2):
        pieces.add(("wo", k))
    pieces.add("fc1")
    pieces.add("gate")
    pieces.add("expert")
    pieces.loop([("up", 0), ("down", 0), ("up", 1), ("down", 1)], HC0 // 2)
    pieces.add("fc2")
    pieces.add("wdown")
    pieces.add("hin")
    pieces.add("fcd")
    pieces.add("hout")
    pieces.add("wup")
    for c in range(3):
        pieces.add(("w13", c))
    pieces.loop([("w13", "L", 0), ("w13", "L", 1)], HC1 // 2 - 1)
    base = pieces.at[("w13", 0)][0]
    pieces.at[("w13", "even")] = (base + 2, 2)
    pieces.at[("w13", "last")] = (base + HC1 - 1, 0)
    for k in range(W2_PIECES):
        pieces.add(("w2", k))
    prods.loop([("up", j, hf) for j in range(2) for hf in range(2)], HC0 // 2)
    for hf in range(2):
        for j in range(2):
            prods.add(("g", "F", j, hf))
    prods.loop([("g", "L", j, hf) for j in range(2) for hf in range(2)], HC1 // 2 - 1)
    for hf in range(2):
        prods.add(("g", "E", 0, hf))
    return banks, pieces, prods


SUNITS = [(i, gp, kh) for i in range(NT) for gp in range(2) for kh in range(1 if i < 4 else 2)]
NS = len(SUNITS)
AHEAD = 6
CTX_AT = AHEAD + 2


def width(s):
    i, _, kh = SUNITS[s]
    return min(P * (i + 1), 512) if kh == 0 else P * (i - 3)


def slots_before(h, s=0):
    if isinstance(h, int) and h < 2:
        return h * (NS + 2) + s
    base = h * (NS + 4) - 4
    if s == "ctx":
        return base + CTX_AT
    return base + s + (2 if s >= CTX_AT else 0)


def ctx_at(n):
    if isinstance(n, int) and n >= NKV - 2:
        return slots_before(NKV) + 2 * (n - (NKV - 2))
    return slots_before(n + 2, "ctx")


def body_steps(nxt, nxt2, ctx):
    todo = []
    if nxt:
        for s in range(AHEAD, NS):
            if s == CTX_AT and ctx:
                todo.append(("ctx", -1, None, 1400))
            todo.append(("s", 1, s, 110 + 2 * width(s)))
        todo.append(("max", 1, None, 1600))
        todo.append(("mod", 1, None, 300))
    elif ctx:
        todo.append(("ctx", -1, None, 1400))
    if nxt2:
        todo += [("s", 2, s, 110 + 2 * width(s)) for s in range(AHEAD)]
    total = sum(x[3] for x in todo)
    out, sofar = [], 0
    for what, d, s, cost in todo:
        step = sofar * (NTU + 1) // max(total, 24000)
        out.append((max(step, 3) if what == "ctx" else step, what, d, s))
        sofar += cost
    return out




def transposed_units():
    units, used = [], {}
    for j in range(NT):
        left = list(range(j, NT))
        while left:
            i = min(left, key=lambda i: (used.get(i % 4, -1), -i))
            left.remove(i)
            used[i % 4] = len(units)
            units.append((j, i))
    return units


TUNITS = transposed_units()
NTU = len(TUNITS)
LAG = 3
PRING = 6
assert NTU % PRING == 0 and NTU % 2 == 0


def adaln_two_blocks(nc, a, out):
    banks, pieces, prods = plan()
    with ExitStack() as ctx:
        cursor = [MISC_B]

        def at(name, shape, dt, offset=None):
            if offset is None:
                offset = cursor[0]
                size = 4 if dt in (F32, F32R) else 2
                for n in shape[1:]:
                    size *= n
                cursor[0] += (size + 31) // 32 * 32
            return nc.alloc_sbuf_tensor_at(name, shape, dt, offset=offset)

        def sem(name):
            return ctx.enter_context(nc.semaphore(name))

        AR = at("arena", [P, AR_WORDS], F32R, SB0)

        def ar(word, *dims):
            n = 1
            for d in dims:
                n *= d
            v = AR[:, word:word + n]
            if len(dims) == 2:
                v = v.rearrange("p (a b) -> p a b", b=dims[1])
            if len(dims) == 3:
                v = v.rearrange("p (a b c) -> p a b c", b=dims[1], c=dims[2])
            return v

        K = 256
        hT = [ar(HT_W, KC, T), ar(HT_W + KC * T, KC, T)]
        x = at("x", [P, NT, D], F32, X_B)
        xnb = at("xnb", [P, 4, D], F32, XN_B)
        raw = at("raw", [P, 2, 1024], F32, RAW_B)
        full = at("full", [P, 2, D], F32, FULL_B)
        Qst = at("Qst", [99, NKV, G, T], BF16, ACT_B)
        Kst = at("Kst", [99, NKV, T], BF16, ACT_B + 65536)
        vtok = at("vtok", [P, NT, P], F32, ACT_B + 81920)
        wq2 = at("wq2", [P, 1024], F32, ACT_B + 81920)
        vr = at("vr", [P, NT, 32], F32, ACT_B + 81920 + 4096)
        mt = at("mt", [32, 2, P], F32, ACT_B + 81920 + 5120)
        mparts = at("mparts", [32, 3, P], BF16, ACT_B + 81920 + 6144)
        maskb = at("maskb", [P, 2, P], BF16, ACT_B + 81920 + 7168)
        Wqkv = [ar(WR_W, KC, 768), ar(WR_W + 3072, KC, 768)]
        cosb = at("cosb", [P, T], F32, WR_B + 24 * 1024)
        sinb = at("sinb", [P, T], F32, WR_B + 28 * 1024)
        rsw = at("rsw", [P, 2, HALF], F32, WR_B + 32 * 1024)
        rq = [at(f"rq{k}", [P, HALF], F32, WR_B + b * 1024) for k, b in enumerate((36, 38, 46))]
        parts = [at(f"parts{k}", [P, 3, HALF], BF16, b)
                 for k, b in enumerate((WR_B + 40 * 1024, WR_B + 43 * 1024, XN_B))]
        wm0 = at("wm0", [P, KC, 1024], F32, ACT_B)
        wmr = at("wmr", [P, KC, MODW], F32, WR_B)
        att = at("att", [P, NT, D], F32, HT_B)
        pr = at("pr", [P, PRING, D], F32, HT_B + 16384)
        ot = at("ot", [P, 2, D], F32, HT_B + 16384 + PRING * 2048)
        gabc = at("gabc", [P, D], F32, WR_B + 12 * 1024)
        gtmp = at("gtmp", [P, D], F32, WR_B + 14 * 1024)
        Wo = [ar(WR_W + 24 * K, KC, D), ar(WR_W + 32 * K, KC, D)]
        lraw = at("lraw", [P, 720], F32, XN_B)
        lpart = at("lpart", [P, 3, 720], BF16, XN_B + 2912)
        aTr = [ar(ACT_W, KC, T), ar(ACT_W + 16 * K, KC, T)]
        u = [ar(ACT_W, HC0, T), ar(ACT_W + 32 * K, HC0, T)]
        lat = [ar(ACT_W + 64 * K, 2, T), ar(ACT_W + 72 * K, 2, T)]
        gg = at("gg", [P, D], F32, ACT_B + 80 * 1024)
        bb = at("bb", [P, D], F32, ACT_B + 82 * 1024)
        Wex = [ar(ACT_W + 84 * K, 2, LAT), ar(ACT_W + 86 * K, 2, LAT)]
        yb = at("yb", [P, 2, D], F32, ACT_B + 84 * 1024)
        gb0 = at("gb0", [P, D], F32, ACT_B + 40 * 1024)
        gb0t = at("gb0t", [P, D], F32, ACT_B + 42 * 1024)
        Wg = [ar(ACT_W + 60 * K, KC, NE), ar(ACT_W + 60 * K + 32, KC, NE)]
        lg = at("lg", [NE, T], F32, ACT_B + 56 * 1024)
        eo = [ar(HT_W, 2, T), ar(HT_W + 2048, 2, T)]
        Wd0 = [ar(WR_W, HC0, D), ar(WR_W + 16 * K, HC0, D)]
        Wf2 = [ar(WR_W + 32 * K, 2, D), ar(WR_W + 36 * K, 2, D)]
        Wf1 = [ar(WR_W + 40 * K, 2, KC, P), ar(WR_W + 44 * K, 2, KC, P)]
        Wup = [[ar(WR_W + (40 + 4 * s) * K, KC, P), ar(WR_W + (42 + 4 * s) * K, KC, P)] for s in range(2)]
        midf = at("midf", [P, T], F32, ACT_B)
        mid = [ar(ACT_W + 4 * K, T), ar(ACT_W + 8 * K, T)]
        xs = at("xs", [P, 2, T], F32, ACT_B + 12 * 1024)
        xsr = [ar(ACT_W + 20 * K, 2, T), ar(ACT_W + 28 * K, 2, T)]
        sz = at("sz", [P, 2, T], F32, ACT_B + 36 * 1024)
        yzr = [ar(ACT_W + 44 * K, 2, T), ar(ACT_W + 52 * K, 2, T)]
        sq = at("sq", [P, 2, T], F32, ACT_B + 60 * 1024)
        hob = [ar(ACT_W + 68 * K, T), ar(ACT_W + 72 * K, T)]
        hof = at("hof", [P, T], F32, ACT_B + 76 * 1024)
        yz = at("yz", [P, 2, T], F32, ACT_B + 80 * 1024)
        dg = at("dg", [P, 4, P], F32, WR_B + 8 * 1024)
        rb = at("rb", [P, HALF], F32, WR_B + 10 * 1024)
        Wdn = [ar(WR_W + 40 * K, KC, P), ar(WR_W + 42 * K, KC, P)]
        Whi = [ar(WR_W + 44 * K, 4, P), ar(WR_W + 46 * K, 4, P)]
        Wfd = [ar(WR_W, 2, 2, P), ar(WR_W + 2 * K, 2, 2, P)]
        Who = [ar(WR_W + 4 * K, 2, P), ar(WR_W + 5 * K, 2, P)]
        Wuo = [ar(WR_W + 12 * K, D), ar(WR_W + 14 * K, D)]
        rt = at("rt", [P, NT, D], F32, WR_B + 16 * 1024)
        Abc = at("Abc", [P, D], F32, WR_B + 32 * 1024)
        Bbc = at("Bbc", [P, D], F32, WR_B + 34 * 1024)
        t36 = at("t36", [P, D], F32, WR_B + 36 * 1024)
        t38 = at("t38", [P, D], F32, WR_B + 38 * 1024)
        gT = [ar(ACT_W, HC1, T), ar(ACT_W + 44 * K, HC1, T)]
        W13 = [[ar(WR_W + 16 * K * 0 + (8 * s) * K, 2, KC, P), ar(WR_W + (8 * s + 4) * K, 2, KC, P)] for s in range(2)]
        w2_at = [WR_W + (16 + 4 * k) * K for k in range(4)] + [WR_W + 4 * k * K for k in range(4)]
        w2_at += [HT_W + 4 * k * K for k in range(HC1 - 8)]
        W2 = [[ar(w, D), ar(w + 2 * K, D)] for w in w2_at]
        Ast = at("Ast", [LROWS, 2432], BF16, WR_B + 36 * 1024)
        Bst = at("Bst", [LROWS, 3328], BF16, WR_B + 36 * 1024 + 4864)
        gb1 = at("gb1", [P, D], F32, WR_B + 34 * 1024)
        gb1t = at("gb1t", [P, D], F32, WR_B + 32 * 1024)
        ident = at("ident", [P, P], F32)
        identb = at("identb", [P, P], BF16)
        sc32 = at("sc32", [P, KC, 2, 16], F32)
        cols = at("cols", [P, 18], F32)
        modc = at("modc", [P, 40], F32)
        mod0c = at("mod0c", [P, 8], F32)
        st = at("st", [P, 4, 6], F32)
        mv = at("mv", [P, 2, 4, 2], F32)
        ve = at("ve", [P, 4], F32)
        rs = at("rs", [P, 2, 4], F32)
        mh = at("mh", [P, 4], F32)
        hms = at("hms", [P, 4], F32)
        hrs = at("hrs", [P, 4], F32)
        yst = at("yst", [P, 2, 6], F32)
        ymv = at("ymv", [P, 2, 2], F32)
        yve = at("yve", [P, 2, 1], F32)
        yrs = at("yrs", [P, 2, 1], F32)
        sce = at("sce", [P, 9], F32)
        alf = at("alf", [P, 2], F32)
        mxp = at("mxp", [P, 2, G, NT], F32)
        nm = at("nm", [P, G * NT], F32)
        rec = at("rec", [P, 2, G, 4], F32)
        top = at("top", [P, NT, 8], F32)
        s2 = at("s2", [P, NT], F32)
        ones = at("ones", [P, P], F32)
        assert cursor[0] <= 229344, cursor[0]
        C_C, C_G, C_BD, C_CW, C_CB, C_D, C_NW = 0, 8, 9, 10, 12, 14, 16

        ps = ctx.enter_context(nc.psum_tensor("ps", [P, 8, 512], F32))

        qscr = nc.dram_tensor("q_parts", (3, DH, NKV, G, T), BF16, kind="Internal").ap()
        kscr = nc.dram_tensor("k_parts", (3, DH, NKV, T), BF16, kind="Internal").ap()
        lscr = nc.dram_tensor("lora_parts", (3, R * 5760), BF16, kind="Internal").ap()
        mscr = nc.dram_tensor("mod_rows", (2, 8 * MODW), F32, kind="Internal").ap()

        full_b = [sem(f"bank{b}_full") for b in range(8)]
        read_b = [sem(f"bank{b}_read") for b in range(8)]
        raw_in = [sem(f"raw{s}_loaded") for s in range(2)]
        piece_done, piece_scaled = sem("piece_split"), sem("piece_scaled")
        x_in = [sem(f"x_half{h}_loaded") for h in range(2)]
        c_in, ident_in, mask_in, trig_in, wm0_in = (sem(n) for n in
                                                    ("cols_loaded", "ident_loaded", "mask_loaded", "trig_loaded", "wm0_loaded"))
        consts = sem("consts_ready")
        c_exp, c_silu, maxp_init = sem("exp_c_ready"), sem("silu_c_ready"), sem("maxima_initialised")
        ln_var, ln_rstd, ln_xn = sem("ln_variance_ready"), sem("ln_rstd_ready"), sem("ln_tile_normalised")
        ln_hi, ln_lo_v, ln_lo_g = sem("ln_hi_ready"), sem("ln_lo_by_vector"), sem("ln_lo_by_gpsimd")
        rope_sw, rope_sin, rope_q = sem("rope_swapped"), sem("rope_sin_applied"), sem("rope_done")
        part_h, part_r, part_m, part_l = (sem(f"part_{n}_ready") for n in "hrml")
        part_out = [sem(f"parts{s}_stored") for s in range(3)]
        v_ones = sem("v_ones_ready")
        wq_hi, wq2_in, wq2_done = (sem("qkv_weights_hi_ready"), sem("qkv_weights_2_loaded"),
                                   sem("qkv_weights_2_split"))
        stack_in = [sem(f"stacks_of_heads{k}_loaded") for k in range(2)]
        k_ones = sem("k_ones_ready")
        s_full, s_read = sem("score_unit_ready"), sem("score_unit_read")
        nm_ready, mt_parts, mrow_in = sem("row_maxima_ready"), sem("max_parts_ready"), sem("max_rows_loaded")
        modrow_out, wmr_in = sem("mod_piece_stored"), sem("mod_weights_loaded")
        t_full, exp_done, pv_done = sem("scoresT_ready"), sem("exp_done"), sem("pv_done")
        vr_ready, o_copied = sem("v_of_head_ready"), sem("ctx_copied")
        lraw_in, lpart_ready, lpart_out, lst_in = (sem("lora_loaded"), sem("lora_parts_ready"),
                                                   sem("lora_parts_stored"), sem("lora_stacks_loaded"))
        ga_in, ga_ready = sem("gate_row_loaded"), sem("gate_of_attn_ready")
        modc_in = sem("mod_chunks_loaded")
        sp_hi = sem("evac_hi_ready")
        ffbc_in, gg_ready, bb_added = sem("mlp_rows_loaded"), sem("mlp_gamma_ready"), sem("mlp_beta_added")
        s_top = sem("top2_sum_ready")
        pr_first, pr_hi, pr_lo = sem("factor_ready"), sem("product_hi_ready"), sem("product_lo_ready")
        y_var, y_rstd, x_mlp = sem("mlp_variance_ready"), sem("mlp_rstd_ready"), sem("x_after_mlp_ready")
        ab_in, ab_ready, rn_ready, xb_ready, r_ready = (
            sem("mixer_rows_loaded"), sem("mixer_rows_ready"), sem("mixer_rest_centred"),
            sem("mixer_rest_shifted"), sem("mixer_rest_ready"))
        mid_lo, xs_hi, yz_hi, xs_lo, yz_ready, sq_ready, yz_lo = (sem("mid_lo_ready"), sem("xs_hi_ready"),
                                                    sem("yz_hi_ready"), sem("xs_lo_ready"), sem("yz_ready"),
                                                    sem("yz_squared"), sem("yz_lo_ready"))
        mr_ready, dg_ready, ho_lo = sem("inverse_rms_ready"), sem("inverse_rms_diagonal_ready"), sem("hydra_out_lo_ready")
        dn_hi = sem("down_hi_ready")
        w_hi, w2_scaled = sem("merged_weights_hi_ready"), sem("w2_scaled")
        gb1_in, gb1_ready = sem("gate_mlp_loaded"), sem("gate_mlp_ready")
        out_done = sem("out_stored")
        dve_c, act_c, pool_c = sem("vector_chain"), sem("scalar_chain"), sem("gpsimd_chain")

        def filled(eng, job, turn=0):
            b, n = banks.get(job, turn)
            eng.wait_ge(full_b[b], n + 1)
            return b

        def evacuated(eng, job, turn=0):
            b, n = banks.get(job, turn)
            eng.wait_ge(read_b[b], n + 1)

        def bank_of(eng, job, turn=0):
            b, n = banks.get(job, turn)
            if not (isinstance(n, int) and n == 0):
                eng.wait_ge(read_b[b], n)
            return b

        def piece_slot(name):
            return pieces.at[name][0] % 2

        def raw_loaded(eng, name, turn=0):
            base, per = pieces.at[name]
            eng.wait_ge(raw_in[base % 2], 16 * (base // 2 + 1) + (8 * per * turn if per else 0))
            return base % 2

        def weights(eng, name, turn=0):
            eng.wait_ge(piece_done, pieces.before(name, turn) + 1)

        def turned_chunk(c):
            return full[:, c, :] if c < 2 else xnb[:, c, :]

        def ln_split(eng, L, hf):
            eng.wait_ge(ln_lo_v, 2 * (2 * L + hf) + 2)
            eng.wait_ge(ln_lo_g, 2 * (2 * L + hf) + 2)

        class Chain:

            def __init__(self, eng, s):
                self.eng, self.s, self.n, self.turn = eng, s, 0, None

            def link(self, ins):
                ins.then_inc(self.s, 1)
                self.n += 1
                if self.turn is None:
                    self.eng.wait_ge(self.s, self.n)
                else:
                    self.eng.wait_ge(self.s, self.turn * self.per + self.n)

            def tick(self, ins):
                ins.then_inc(self.s, 1)
                self.n += 1

            def wait(self):
                self.eng.wait_ge(self.s, self.n)

            def enter(self, turn, per):
                self.turn, self.per, self.at = turn, per, self.n

            def leave(self, turns):
                assert self.n - self.at == self.per, (self.n - self.at, self.per)
                self.n = self.at + turns * self.per
                self.turn = None

        Q_ROWS = ((0, 3), (1, 2), (2, 1))
        K_ROWS = (3, 2, 1)
        assert sum(n for _, n in Q_ROWS) == sum(K_ROWS) == 6

        block = ctx.enter_context(nc.Block())

        @block.sync
        def _(sp):
            def load_piece(name, src, cols_, turn=0):
                n = pieces.before(name, turn)
                s = piece_slot(name)
                if not (isinstance(n, int) and n < 2):
                    sp.wait_ge(piece_done, n - 1)
                sp.dma_start(raw[:, s, 0:cols_], src).then_inc(raw_in[s], 16)

            sp.dma_start(cols[:, 0:18], a["cols"]).then_inc(c_in, 16)
            for t in range(4):
                sp.dma_start(x[:, t, :], a["x"][t * P:(t + 1) * P, :]).then_inc(x_in[0], 16)
            sp.dma_start(wm0[:, :, :].rearrange("p c n -> p (c n)"), a["wm0"]).then_inc(wm0_in, 16)
            sp.dma_start(ident[:, :], a["ident"]).then_inc(ident_in, 16)
            for k in range(2):
                load_piece(("wqkv", k), a["wqkv"][:, 1024 * k:1024 * (k + 1)], 1024)
            sp.dma_start(wq2[:, :], a["wqkv"][:, 2048:3072]).then_inc(wq2_in, 16)
            for t in range(4, 8):
                sp.dma_start(x[:, t, :], a["x"][t * P:(t + 1) * P, :]).then_inc(x_in[1], 16)
            sp.dma_start(cosb[:, :], a["cos"]).then_inc(trig_in, 16)
            sp.dma_start(sinb[:, :], a["sin"]).then_inc(trig_in, 16)
            sp.dma_start(rq[0][:, 0:2 * P], a["mask"]).then_inc(mask_in, 16)

            for n in range(10):
                hf, m = divmod(n, 5)
                sp.wait_ge(part_l, n + 1)
                tok = slice(hf * HALF, (hf + 1) * HALF)
                for q in range(3):
                    src = parts[n % 3][:, q, :]
                    if m < 4:
                        dst = qscr[q, :, :, m, tok].rearrange("d n t -> n d t")
                    else:
                        dst = kscr[q, :, :, tok].rearrange("d n t -> n d t")
                    sp.dma_start(dst, src).then_inc(part_out[n % 3], 16)
            for s in range(3):
                sp.wait_ge(part_out[s], 48 * (4 if s == 0 else 3))
            for k, (n0, n1) in enumerate(((0, 2), (2, NKV))):
                r = 0
                for n in K_ROWS:
                    sp.dma_start(Kst[DH * r:DH * (r + n), n0:n1, :], kscr[0:n, :, n0:n1, :].rearrange("q d n t -> (q d) n t"))\
                        .then_inc(stack_in[k], 16)
                    r += n
            sp.dma_start(lraw[:, :], a["lora"]).then_inc(lraw_in, 16)

            b, n = banks.get(("qkv", 1, 5))
            sp.wait_ge(full_b[b], n + 1)
            sp.dma_start(wmr[:, :, :].rearrange("p c n -> p (c n)"), a["wmr"][0]).then_inc(wmr_in, 16)

            def head_dmas(h, more):
                sp.wait_ge(mt_parts, h + 1)
                for q in range(3):
                    sp.dma_start(Qst[KROWS + q:KROWS + q + 1, bass.ds(h, 1), :, :].rearrange("p n g t -> p (n g t)"),
                                 mparts[:, q, :]).then_inc(mrow_in, 16)
                sp.wait_ge(s_read, slots_before(h, NS + 1) + 1)
                for blk in range(2):
                    sp.dma_start(mscr[blk, bass.ds(h * MODW, MODW)].rearrange("(q n) -> q n", n=MODW // 4),
                                 full[16 * blk:16 * blk + 97:32, 0, 0:MODW // 4]).then_inc(modrow_out, 16)
                if more:
                    sp.wait_ge(s_full, slots_before(h, NS + 1) + 1)
                    sp.dma_start(wmr[:, :, :].rearrange("p c n -> p (c n)"),
                                 a["wmr"][bass.ds(h + 1, 1)].rearrange("o p n -> (o p) n")).then_inc(wmr_in, 16)

            for h in range(2):
                head_dmas(h, True)
            with sp.Fori(0, NKV - 3) as k:
                head_dmas(k + 2, True)
            head_dmas(NKV - 1, False)
            sp.wait_ge(modrow_out, 32 * NKV)

            def row(k):
                return mscr[0 if k < 4 else 1, k * D:(k + 1) * D].rearrange("(o n) -> o n", o=1).to_broadcast([P, D])

            def rowin(name):
                return a[name].rearrange("(o n) -> o n", o=1).to_broadcast([P, D])

            sp.dma_start(gabc[:, :], row(0)).then_inc(ga_in, 16)
            for blk, (k0, k1) in enumerate(((0, 16), (16, 40))):
                sp.dma_start(full[k0:k1, 1, 0:P], mscr[blk, k0 * P:k1 * P].rearrange("(k n) -> k n", n=P))\
                    .then_inc(modc_in, 16)
            for q in range(3):
                sp.wait_ge(lpart_ready, 1)
                sp.dma_start(lscr[q].rearrange("(p n) -> p n", p=P), lpart[:, q, :]).then_inc(lpart_out, 16)
            for k in range(2):
                load_piece(("wo", k), a["wo"][:, 1024 * k:1024 * (k + 1)], 1024)
            load_piece("fc1", a["fc1"], 1024)
            load_piece("gate", a["gate"], KC * NE)
            load_piece("expert", a["expert"], 2 * LAT)
            sp.wait_ge(s_read, ctx_at(NKV - 1) + 2)
            sp.dma_start(gg[:, :], rowin("gamma")).then_inc(ffbc_in, 16)
            sp.dma_start(bb[:, :], rowin("beta")).then_inc(ffbc_in, 16)
            sp.dma_start(gb0[:, :], row(3)).then_inc(ffbc_in, 16)
            with sp.Fori(0, HC0 // 2) as i:
                for j in range(2):
                    for kind in ("up", "down"):
                        load_piece((kind, j), a[kind][bass.ds(2 * i + j, 1)].rearrange("o p n -> (o p) n"), D, i)
            load_piece("fc2", a["fc2"], 1024)
            load_piece("wdown", a["wdown"], D)
            load_piece("hin", a["hin"], D)
            filled(sp, ("routed", NT - 1))
            sp.dma_start(Abc[:, :], row(5)).then_inc(ab_in, 16)
            sp.dma_start(Bbc[:, :], row(4)).then_inc(ab_in, 16)
            sp.dma_start(t36[:, :], row(6)).then_inc(ab_in, 16)
            sp.dma_start(t38[:, :], rowin("bup")).then_inc(ab_in, 16)
            load_piece("fcd", a["fcd"], D)
            load_piece("hout", a["hout"], 2 * P)
            load_piece("wup", a["wup"], D)
            load_piece(("w13", 0), a["w13"][0], 1024)
            sp.wait_ge(lpart_out, 48)
            filled(sp, ("z", 1, 1, 1))
            weights(sp, "wup")
            lora_parts = lscr.rearrange("q (r n) -> q r n", r=R)
            r = 0
            for part, n in Q_ROWS:
                sp.dma_start(Ast[R * r:R * (r + n), :], lora_parts[part, :, 0:2432].unsqueeze(0).to_broadcast([n, R, 2432]))\
                    .then_inc(lst_in, 16)
                r += n
            r = 0
            for n in K_ROWS:
                for q in range(n):
                    sp.dma_start(Bst[R * (r + q):R * (r + q + 1), :], lora_parts[q, :, 2432:5760]).then_inc(lst_in, 16)
                r += n
            for c in (1, 2):
                load_piece(("w13", c), a["w13"][c], 1024)
            sp.wait_ge(r_ready, NT)
            sp.dma_start(gb1[:, :], row(9)).then_inc(gb1_in, 16)
            with sp.Fori(0, HC1 // 2 - 1) as i:
                for j in range(2):
                    load_piece(("w13", "L", j), a["w13"][bass.ds(2 * i + j + 3, 1)].rearrange("o p n -> (o p) n"), 1024, i)
            for k in range(W2_PIECES):
                n = min(2, HC1 - 2 * k)
                load_piece(("w2", k), a["w2"][k, :, 0:n * D], n * D)
            for t in range(NT):
                evacuated(sp, ("down", t // 4, t % 4))
                sp.dma_start(out[t * P:(t + 1) * P, :], x[:, t, :]).then_inc(out_done, 16)
            sp.wait_ge(out_done, 16 * NT)

        @block.tensor
        def _(pe):
            def mm(outp, lhs, rhs, start, stop):
                return nc.tensor.matmul(outp, lhs, rhs, start=start, stop=stop, skip_group_check=True)

            def mm3(outp, lhs, rhs, start, stop):
                mm(outp, lhs[0], rhs[0], start, False)
                mm(outp, lhs[0], rhs[1], False, False)
                return mm(outp, lhs[1], rhs[0], False, stop)

            def hilo(pair, f):
                return f(pair[0]), f(pair[1])

            def ln_turn(L, hf):
                pe.wait_ge(ln_xn, 8 * L + 4 * hf + 4)
                for c in range(KC):
                    b = bank_of(pe, ("ln", L, hf, c))
                    for t in range(4):
                        last = nc.tensor.transpose(ps[:, b, t * P:(t + 1) * P], xnb[:, t, c * P:(c + 1) * P],
                                                   ident[:, :])
                    last.then_inc(full_b[b], 1)

            tok = [slice(0, HALF), slice(HALF, T)]

            def tl(t):
                return slice(t * P, (t + 1) * P)

            pe.wait_ge(c_silu, 1)
            pe.wait_ge(wm0_in, 16)
            b = bank_of(pe, "mod0")
            for kc in range(KC):
                for q in range(4):
                    last = mm(ps[32 * q:32 * q + 32, b, 0:256], sc32[:, kc, :, :].rearrange("p l m -> p (l m)"), wm0[:, kc, 256 * q:256 * q + 256],
                              kc == 0, kc == KC - 1)
            last.then_inc(full_b[b], 1)
            evacuated(pe, "mod0")
            pe.wait_ge(ident_in, 16)
            b = bank_of(pe, "mod0T")
            for k in range(2):
                last = nc.tensor.transpose(ps[:, b, k * P:(k + 1) * P], full[:, 0, k * P:(k + 1) * P], ident[:, :])
            last.then_inc(full_b[b], 1)
            ln_turn(0, 0)
            for hf in range(2):
                ln_split(pe, 0, hf)
                for m in range(6):
                    if hf == 0 and m == 0:
                        weights(pe, ("wqkv", 1))
                        pe.wait_ge(wq2_done, 1)
                    b = bank_of(pe, ("qkv", hf, m))
                    for kc in range(KC):
                        last = mm3(ps[:, b, :], hilo(Wqkv, lambda w: w[:, kc, m * P:(m + 1) * P]),
                                   hilo(hT, lambda h: h[:, kc, tok[hf]]), kc == 0, kc == KC - 1)
                    last.then_inc(full_b[b], 1)
                    if (hf, m) == (0, 0):
                        ln_turn(0, 1)
            for hf in range(2):
                evacuated(pe, ("qkv", hf, 5))
                b = bank_of(pe, ("vT", hf))
                for t in range(4):
                    last = nc.tensor.transpose(ps[:, b, tl(t)], full[:, hf, tl(t)], ident[:, :])
                last.then_inc(full_b[b], 1)

            def s_unit(h, s):
                slot = s % 2
                i, gp, kh = SUNITS[s]
                w = width(s)
                before = slots_before(h, s)
                if not isinstance(before, int) or before >= 2:
                    pe.wait_ge(s_read, before - 1)
                diag = kh == (0 if i < 4 else 1)
                for e in range(2):
                    o = ps[:, 2 * slot + e, :]
                    last = mm(o[:, 0:w], Qst[0:KROWS, bass.ds(h, 1), 2 * gp + e, i * P:(i + 1) * P]
                              .rearrange("p n t -> p (n t)"),
                              Kst[0:KROWS, bass.ds(h, 1), 512 * kh:512 * kh + w].rearrange("p n t -> p (n t)"),
                              True, not diag)
                    if diag:
                        last = mm(o[:, w - P:w], identb[:, :], maskb[:, 0, :], False, True)
                last.then_inc(s_full, 1)

            def max_turn(h):
                pe.wait_ge(s_read, slots_before(h, NS) - 1)
                pe.wait_ge(nm_ready, h + 1)
                nc.tensor.transpose(ps[0:32, 0, 0:P], nm[:, :], ident[:, :]).then_inc(s_full, 1)

            def mod_step(h):
                pe.wait_ge(s_read, slots_before(h, NS + 1) - 1)
                pe.wait_ge(wmr_in, 16 * h + 16)
                w = MODW // 4
                for kc in range(KC):
                    for q in range(4):
                        last = mm(ps[32 * q:32 * q + 32, 2, 0:w], sc32[:, kc, :, :].rearrange("p l m -> p (l m)"),
                                  wmr[:, kc, w * q:w * q + w], kc == 0, kc == KC - 1)
                last.then_inc(s_full, 1)

            def t_unit(n, k):
                j, i = TUNITS[k]
                if k == 0:
                    pe.wait_ge(mrow_in, 48 * n + 48)
                if k >= 2:
                    pe.wait_ge(exp_done, n * NTU + k - 1)
                o = ps[:, 4 + k % 2, :].rearrange("p (g t) -> p g t", g=G)
                last = mm(o, Kst[:, bass.ds(n, 1), j * P:(j + 1) * P].rearrange("p n t -> p (n t)"),
                          Qst[:, bass.ds(n, 1), :, i * P:(i + 1) * P].rearrange("p n g t -> p (n g) t"),
                          True, i > j)
                if i == j:
                    last = mm(o, identb[:, :], maskb[:, 1, :].unsqueeze(1).to_broadcast([P, G, P]), False, True)
                last.then_inc(t_full, 1)

            def pv(n, k):
                j, i = TUNITS[k]
                if k == 0:
                    pe.wait_ge(vr_ready, n + 1)
                    if not (isinstance(n, int) and n == 0):
                        pe.wait_ge(o_copied, 2 * n)
                pe.wait_ge(exp_done, n * NTU + k + 1)
                q = 32 * (i % 4)
                mm(ps[q:q + 32, 6 + i // 4, :], vr[:, j, :], pr[:, k % PRING, :], j == 0, j == i).then_inc(pv_done, 1)

            def ctx_turn(n, at):
                for b in range(2):
                    pe.wait_ge(s_read, at + b - 1)
                    pe.wait_ge(o_copied, 2 * n + b + 1)
                    for g in range(G):
                        last = nc.tensor.transpose(ps[:, 2 * b, tl(g)], ot[:, b, tl(g)], ident[:, :])
                    last.then_inc(s_full, 1)

            def head_body(n, nxt, nxt2, ctx):
                todo = body_steps(nxt, nxt2, ctx)
                for k in range(NTU + LAG):
                    if k < NTU:
                        t_unit(n, k)
                    while todo and (todo[0][0] <= k or k == NTU + LAG - 1):
                        _, what, d, s = todo.pop(0)
                        if what == "s":
                            s_unit(n + d, s)
                        elif what == "max":
                            max_turn(n + d)
                        elif what == "mod":
                            mod_step(n + d)
                        else:
                            ctx_turn(n - 1, ctx_at(n - 1))
                    if k >= LAG:
                        pv(n, k - LAG)

            for b in range(8):
                if banks.attn[b]:
                    pe.wait_ge(read_b[b], banks.attn[b])
            pe.wait_ge(k_ones, 3)
            pe.wait_ge(stack_in[0], 16 * 6)
            for s in range(NS):
                s_unit(0, s)
            max_turn(0)
            mod_step(0)
            for s in range(AHEAD):
                s_unit(1, s)
            pe.wait_ge(stack_in[1], 16 * 6)
            head_body(0, True, True, False)
            with pe.Fori(0, NKV - 3) as k:
                head_body(k + 1, True, True, True)
            head_body(NKV - 2, True, False, True)
            head_body(NKV - 1, False, False, True)
            ctx_turn(NKV - 1, ctx_at(NKV - 1))

            pe.wait_ge(s_read, ctx_at(NKV - 1) + 2)
            pe.wait_ge(modc_in, 32)
            b = bank_of(pe, "modT")
            nc.tensor.transpose(ps[:, b, 0:40], full[0:40, 1, 0:P], ident[0:40, 0:40]).then_inc(full_b[b], 1)
            for hf in range(2):
                for c in range(KC):
                    b = bank_of(pe, ("aT", hf, c))
                    for t in range(4):
                        last = nc.tensor.transpose(ps[:, b, tl(t)], att[:, 4 * hf + t, c * P:(c + 1) * P], ident[:, :])
                    last.then_inc(full_b[b], 1)
            weights(pe, ("wo", 1))
            for t in range(NT):
                if t % 4 == 0:
                    for c in range(KC):
                        evacuated(pe, ("aT", t // 4, c))
                b = bank_of(pe, ("wo", t))
                for kc in range(KC):
                    last = mm3(ps[:, b, :], hilo(aTr, lambda h: h[:, kc, tl(t)]), hilo(Wo, lambda w: w[:, kc, :]),
                               kc == 0, kc == KC - 1)
                last.then_inc(full_b[b], 1)
                if t == 5:
                    ln_turn(1, 0)

            for hf in range(2):
                ln_split(pe, 1, hf)
                weights(pe, "gate")
                b = bank_of(pe, ("gate", hf))
                for kc in range(KC):
                    last = mm3(ps[0:NE, b, :], hilo(Wg, lambda w: w[:, kc, :]), hilo(hT, lambda h: h[:, kc, tok[hf]]),
                               kc == 0, kc == KC - 1)
                last.then_inc(full_b[b], 1)
                for m in range(2):
                    b = bank_of(pe, ("fc1", hf, m))
                    for kc in range(KC):
                        last = mm3(ps[:, b, :], hilo(Wf1, lambda w: w[:, m, kc, :]),
                                   hilo(hT, lambda h: h[:, kc, tok[hf]]), kc == 0, kc == KC - 1)
                    last.then_inc(full_b[b], 1)
                if hf == 0:
                    ln_turn(1, 1)
            evacuated(pe, ("gate", 0))
            evacuated(pe, ("gate", 1))
            b = bank_of(pe, "gateT")
            for t in range(NT):
                last = nc.tensor.transpose(ps[:, b, NE * t:NE * t + NE], lg[:, tl(t)], ident[0:NE, 0:NE])
            last.then_inc(full_b[b], 1)
            with pe.Fori(0, HC0 // 2) as i:
                for j in range(2):
                    weights(pe, ("up", j), i)
                    for hf in range(2):
                        b = bank_of(pe, ("up", j, hf), i)
                        for kc in range(KC):
                            last = mm3(ps[:, b, :], hilo(Wup[j], lambda w: w[:, kc, :]),
                                       hilo(hT, lambda h: h[:, kc, tok[hf]]), kc == 0, kc == KC - 1)
                        last.then_inc(full_b[b], 1)
            weights(pe, "expert")
            for hf in range(2):
                for m in range(2):
                    evacuated(pe, ("fc1", hf, m))
                for m in range(2):
                    b = bank_of(pe, ("eo", hf, m))
                    for kc in range(2):
                        last = mm3(ps[:, b, :], hilo(Wex, lambda w: w[:, kc, m * P:(m + 1) * P]),
                                   hilo(lat, lambda h: h[:, kc, tok[hf]]), kc == 0, kc == 1)
                    last.then_inc(full_b[b], 1)
            pe.wait_ge(pr_lo, 2 * HC0)
            for t in range(NT):
                if t == 0:
                    weights(pe, ("down", 1), HC0 // 2 - 1)
                b = bank_of(pe, ("shared", t))
                for kc in range(HC0):
                    last = mm3(ps[:, b, :], hilo(u, lambda h: h[:, kc, tl(t)]), hilo(Wd0, lambda w: w[:, kc, :]),
                               kc == 0, kc == HC0 - 1)
                last.then_inc(full_b[b], 1)
                if t % 4 == 0:
                    for m in range(2):
                        evacuated(pe, ("eo", t // 4, m))
                if t == 0:
                    weights(pe, "fc2")
                b = bank_of(pe, ("routed", t))
                for kc in range(2):
                    last = mm3(ps[:, b, :], hilo(eo, lambda h: h[:, kc, tl(t)]), hilo(Wf2, lambda w: w[:, kc, :]),
                               kc == 0, kc == 1)
                last.then_inc(full_b[b], 1)
                if t == 6:
                    ln_turn(2, 0)

            def lora(name, c, turn=0):
                for which, (kind, o) in enumerate((("lora", 0), ("lora3", HC1 * P))):
                    b = bank_of(pe, (kind, *name), turn)
                    for kc in range(KC):
                        last = mm(ps[:, b, kc * P:(kc + 1) * P],
                                  Ast[:, 512 * which + kc * P:512 * which + (kc + 1) * P],
                                  Bst[:, bass.ds(o + c * P, P)], True, True)
                    last.then_inc(full_b[b], 1)

            for kind, y, hf in MIXER:
                src = mid if y == 0 else hob
                if kind == "ln":
                    ln_turn(2, 1)
                elif kind == "mid":
                    weights(pe, "wdown")
                    ln_split(pe, 2, hf)
                    b = bank_of(pe, ("mid", hf))
                    for kc in range(KC):
                        last = mm3(ps[:, b, :], hilo(Wdn, lambda w: w[:, kc, :]), hilo(hT, lambda h: h[:, kc, tok[hf]]),
                                   kc == 0, kc == KC - 1)
                    last.then_inc(full_b[b], 1)
                elif kind == "in":
                    weights(pe, "hin")
                    pe.wait_ge(mid_lo if y == 0 else ho_lo, hf + 1)
                    for job, m0 in (("xs", 2), ("z", 0)):
                        for m in range(2):
                            b = bank_of(pe, (job, y, hf, m))
                            mm3(ps[:, b, :], hilo(Whi, lambda w: w[:, m0 + m, :]), hilo(src, lambda h: h[:, tok[hf]]),
                                True, True).then_inc(full_b[b], 1)
                elif kind == "fd":
                    weights(pe, "hout")
                    pe.wait_ge(xs_lo, 4 * y + 2 * hf + 2)
                    for m in range(2):
                        b = bank_of(pe, ("fd", y, hf, m))
                        for kc in range(2):
                            last = mm3(ps[:, b, :], hilo(Wfd, lambda w: w[:, kc, m, :]),
                                       hilo(xsr, lambda h: h[:, kc, tok[hf]]), kc == 0, kc == 1)
                        last.then_inc(full_b[b], 1)
                elif kind == "out":
                    pe.wait_ge(sq_ready, 4 * y + 2 * hf + 2)
                    b = bank_of(pe, ("ssq", y, hf))
                    for t in range(4):
                        for kc in range(2):
                            last = mm(ps[:, b, t:t + 1], sq[:, kc, tl(4 * hf + t)], ones[:, 0:1], kc == 0, kc == 1)
                    last.then_inc(full_b[b], 1)
                    pe.wait_ge(yz_lo, 4 * y + 2 * hf + 2)
                    b = bank_of(pe, ("hout", y, hf))
                    for kc in range(2):
                        last = mm3(ps[:, b, :], hilo(Who, lambda w: w[:, kc, :]), hilo(yzr, lambda h: h[:, kc, tok[hf]]),
                                   kc == 0, kc == 1)
                    last.then_inc(full_b[b], 1)
                elif kind == "scale":
                    pe.wait_ge(dg_ready, 2 * y + hf + 1)
                    b = bank_of(pe, ("rbc", y, hf))
                    mm(ps[:, b, :], ones[:, :], dg[:, :, :].rearrange("p t n -> p (t n)"), True, True)\
                        .then_inc(full_b[b], 1)
                elif kind == "lora":
                    pe.wait_ge(lst_in, 16 * 9)
                    for c in range(2):
                        lora(("F", c), c)
                elif kind == "up":
                    if hf:
                        ln_turn(3, 0)
                    weights(pe, "wup")
                    pe.wait_ge(ho_lo, 2 + hf + 1)
                    for t in range(4 * hf, 4 * hf + 4):
                        b = bank_of(pe, ("wup", t))
                        mm3(ps[:, b, :], hilo(hob, lambda h: h[:, tl(t)]), Wuo, True, True).then_inc(full_b[b], 1)

            def gated(name, piece, slot, halves=(0, 1), turn=0):
                weights(pe, piece, turn)
                for hf in halves:
                    for which, kind in enumerate(("h1", "h3")):
                        b = bank_of(pe, (kind, *name, hf), turn)
                        for kc in range(KC):
                            last = mm3(ps[:, b, :], hilo(W13[slot], lambda w: w[:, which, kc, :]),
                                       hilo(hT, lambda h: h[:, kc, tok[hf]]), kc == 0, kc == KC - 1)
                        last.then_inc(full_b[b], 1)

            def lora2(c):
                b = bank_of(pe, ("lora2", c))
                mm(ps[:, b, :], Ast[:, 1024 + c * P:1024 + (c + 1) * P], Bst[:, 2 * HC1 * P:2 * HC1 * P + D], True, True)\
                    .then_inc(full_b[b], 1)

            ln_split(pe, 3, 0)
            gated(("F", 0), ("w13", 0), 0, (0,))
            gated(("F", 1), ("w13", 1), 1, (0,))
            ln_turn(3, 1)
            ln_split(pe, 3, 1)
            gated(("F", 0), ("w13", 0), 0, (1,))
            lora(("F", 2), 2)
            gated(("F", 1), ("w13", 1), 1, (1,))
            with pe.Fori(0, HC1 // 2 - 1) as i:
                lora(("L", 0), 2 * i + 3, i)
                gated(("L", 0), ("w13", "even"), 0, turn=i)
                lora(("L", 1), 2 * i + 4, i)
                gated(("L", 1), ("w13", "L", 0), 1, turn=i)
            for c in range(W2_AHEAD):
                lora2(c)
            gated(("E", 0), ("w13", "last"), 0)

            def down(q, c, t):
                b = bank_of(pe, ("down", q, t)) if c == 0 else banks.get(("down", q, t))[0]
                last = mm3(ps[:, b, :], hilo(gT, lambda h: h[:, c, tl(4 * q + t)]), W2[c], c == 0, c == HC1 - 1)
                if c == HC1 - 1:
                    last.then_inc(full_b[b], 1)

            for k in range(W2_AHEAD, W2_AHEAD + 4):
                lora2(k)
            for c in range(HC1):
                if W2_AHEAD + 4 + c < HC1:
                    lora2(W2_AHEAD + 4 + c)
                if c in (0, HC1 - 1):
                    pe.wait_ge(pr_lo, 2 * HC0 + 2 * (HC1 - 1 if c == 0 else HC1))
                weights(pe, ("w2", c // 2))
                for t in range(4):
                    down(0, c, t)
            for t in range(4):
                for c in range(HC1):
                    down(1, c, t)

        @block.scalar
        def _(act):
            A = nc.scalar.activation
            chain = Chain(act, act_c)

            def ln_full(L, hf, c, scale, bias):
                b = filled(act, ("ln", L, hf, c))
                half = 2 * L + hf
                if c >= 2:
                    filled(act, ("ln", L, hf, KC - 1))
                elif half:
                    act.wait_ge(ln_lo_v if c % 2 else ln_lo_g, 2 * (half - 1) + 1)
                A(turned_chunk(c), ps[:, b, :], ACT.Identity, scale=scale, bias=bias).then_inc(read_b[b], 1)

            def split_hi(job, dst):
                b = filled(act, job)
                A(dst, ps[:, b, :], ACT.Copy).then_inc(sp_hi, 1)

            tok = [slice(0, HALF), slice(HALF, T)]

            act.wait_ge(c_in, 16)
            A(sce[:, :], cols[:, 0:9], ACT.Exp, scale=-1.0).then_inc(c_exp, 1)
            b = filled(act, "mod0")
            A(full[:, 0, 0:256], ps[:, b, 0:256], ACT.Copy).then_inc(read_b[b], 1)

            def wqkv_hi(k):
                if k < 2:
                    src = raw[:, raw_loaded(act, ("wqkv", k)), :]
                else:
                    act.wait_ge(wq2_in, 16)
                    src = wq2[:, :]
                A(Wqkv[0].rearrange("p c n -> p (c n)")[:, 1024 * k:1024 * k + 1024], src, ACT.Copy).then_inc(wq_hi, 1)

            wqkv_hi(0)
            evacuated(act, "mod0T")
            for c in range(2):
                ln_full(0, 0, c, mod0c[:, 4 + c:5 + c], mod0c[:, c:c + 1])
            wqkv_hi(1)
            wqkv_hi(2)
            for c in range(2, KC):
                ln_full(0, 0, c, mod0c[:, 4 + c:5 + c], mod0c[:, c:c + 1])
            for c in range(KC):
                ln_full(0, 1, c, mod0c[:, 4 + c:5 + c], mod0c[:, c:c + 1])
            for n in range(11):
                if n:
                    act.wait_ge(part_r, n)
                    A(parts[(n - 1) % 3][:, 1, :], rq[(n - 1) % 3][:, :], ACT.Copy).then_inc(part_m, 1)
                if n < 10:
                    act.wait_ge(rope_q, n + 1)
                    if n >= 3:
                        act.wait_ge(part_out[n % 3], 48 * (n // 3))
                    A(parts[n % 3][:, 0, :], rq[n % 3][:, :], ACT.Copy).then_inc(part_h, 1)
                if n % 5 == 4:
                    hf = n // 5
                    b = filled(act, ("qkv", hf, 5))
                    if hf == 0:
                        ln_split(act, 0, 1)
                    A(full[:, hf, :], ps[:, b, :], ACT.Copy).then_inc(read_b[b], 1)
            for s in range(3):
                act.wait_ge(part_out[s], 48 * (4 if s == 0 else 3))
            for k, (n0, n1) in enumerate(((0, 2), (2, NKV))):
                r = 0
                for part, n in Q_ROWS:
                    src = qscr[part, :, n0:n1, :, :].rearrange("d n g t -> d (n g t)")
                    act.dma_start(Qst[DH * r:DH * (r + n), n0:n1, :, :].rearrange("p n g t -> p (n g t)"),
                                  src.unsqueeze(0).to_broadcast([n, DH, (n1 - n0) * G * T])).then_inc(stack_in[k], 16)
                    r += n
            for hf in range(2):
                b = filled(act, ("vT", hf))
                A(vtok[:, 4 * hf:4 * hf + 4, :].rearrange("p t n -> p (t n)"), ps[:, b, :], ACT.Copy)\
                    .then_inc(read_b[b], 1)

            def copy_ctx(n):
                act.wait_ge(pv_done, n * NTU + NTU)
                if not (isinstance(n, int) and n == 0):
                    act.wait_ge(s_full, ctx_at(n - 1) + 2)
                for b in range(2):
                    A(ot[:, b, :], ps[:, 6 + b, :], ACT.Copy).then_inc(o_copied, 1)

            def head_body(n, first):
                for k in range(NTU):
                    if k == 2 and not first:
                        copy_ctx(n - 1)
                    act.wait_ge(t_full, n * NTU + k + 1)
                    if k >= PRING or not first:
                        act.wait_ge(pv_done, n * NTU + k - PRING + 1)
                    A(pr[:, k % PRING, :], ps[:, 4 + k % 2, :], ACT.Exp, scale=float(DH) ** -0.5).then_inc(exp_done, 1)

            head_body(0, True)
            head_body(1, False)
            with act.Fori(0, NKV - 2) as k:
                head_body(k + 2, False)
            copy_ctx(NKV - 1)
            for hf in range(2):
                for c in range(KC):
                    split_hi(("aT", hf, c), aTr[0][:, c, tok[hf]])
            evacuated(act, "modT")

            for hf in range(2):
                for c in range(KC):
                    ln_full(1, hf, c, modc[:, 8 + c:9 + c], modc[:, 4 + c:5 + c])
                b = filled(act, ("gate", hf))
                A(lg[:, tok[hf]], ps[0:NE, b, :], ACT.Copy).then_inc(read_b[b], 1)
                for m in range(2):
                    split_hi(("fc1", hf, m), lat[0][:, m, tok[hf]])

            def relu_unit(i, j, hf):
                name = ("up", j, hf)
                s = prods.at[name][0] % 2
                b = filled(act, name, i)
                A(full[:, s, :], ps[:, b, :], ACT.Relu).then_inc(pr_first, 1)
                evacuated(act, name, i)
                A(u[0][:, bass.ds(2 * i + j, 1), tok[hf]].rearrange("p o n -> p (o n)"), xnb[:, s, :], ACT.Copy)\
                    .then_inc(pr_hi, 1)

            def down_hi(i, j):
                s = raw_loaded(act, ("down", j), i)
                A(Wd0[0][:, bass.ds(2 * i + j, 1), :].rearrange("p o n -> p (o n)"), raw[:, s, 0:D], ACT.Copy)\
                    .then_inc(dn_hi, 1)

            def up_turn(i, more):
                for j in range(2):
                    if j == 0:
                        down_hi(i, 1)
                    elif more:
                        down_hi(i + 1, 0)
                    for hf in range(2):
                        relu_unit(i, j, hf)

            ln_split(act, 1, 1)
            down_hi(0, 0)
            with act.Fori(0, HC0 // 2 - 1) as i:
                up_turn(i, True)
            up_turn(HC0 // 2 - 1, False)
            for hf in range(2):
                for m in range(2):
                    split_hi(("eo", hf, m), eo[0][:, m, tok[hf]])
            act.wait_ge(s_top, 1)
            for t in range(NT):
                if t == NT - 1:
                    act.wait_ge(y_var, t)
                    for c in range(KC):
                        ln_full(2, 0, c, modc[:, 20 + c:21 + c], modc[:, 16 + c:17 + c])
                    act.wait_ge(ln_lo_v, 2 * (2 * 2 + 0) + 2)
                elif t >= 2:
                    act.wait_ge(y_var, t - 1)
                b = filled(act, ("routed", t))
                A(full[:, t % 2, :], ps[:, b, :], ACT.Copy, scale=s2[:, t:t + 1]).then_inc(read_b[b], 1)

            def w13_hi(piece, slot, job, turn=0):
                evacuated(act, job, turn)
                A(W13[slot][0][:, :, :, :].rearrange("p a c n -> p (a c n)"), raw[:, piece_slot(piece), :], ACT.Copy)\
                    .then_inc(w_hi, 1)

            def squares(y, hf):
                for m in range(2):
                    act.wait_ge(yz_ready, 4 * y + 2 * hf + m + 1)
                    if y == 1:
                        filled(act, ("hout", 0, hf))
                    A(yzr[0][:, m, tok[hf]], yz[:, m, tok[hf]], ACT.Copy).then_inc(yz_hi, 1)
                    A(sq[:, m, tok[hf]], yz[:, m, tok[hf]], ACT.Square).then_inc(sq_ready, 1)

            for kind, y, hf in MIXER:
                if kind == "ln":
                    act.wait_ge(y_var, NT)
                    for c in range(KC):
                        ln_full(2, 1, c, modc[:, 20 + c:21 + c], modc[:, 16 + c:17 + c])
                elif kind == "mid":
                    b = filled(act, ("mid", hf))
                    A(midf[:, tok[hf]], ps[:, b, :], ACT.Gelu, bias=cols[:, C_BD:C_BD + 1]).then_inc(read_b[b], 1)
                elif kind == "in":
                    for m in range(2):
                        b = filled(act, ("xs", y, hf, m))
                        if y == 1:
                            act.wait_ge(yz_ready, 2 * hf + m + 1)
                            act.wait_ge(xs_lo, 2 * hf + m + 1)
                        A(xs[:, m, tok[hf]], ps[:, b, :], ACT.Silu, scale=cols[:, C_CW + m:C_CW + m + 1],
                          bias=cols[:, C_CB + m:C_CB + m + 1]).then_inc(read_b[b], 1)
                        evacuated(act, ("xs", y, hf, m))
                        A(xsr[0][:, m, tok[hf]], xs[:, m, tok[hf]], ACT.Copy).then_inc(xs_hi, 1)
                    for m in range(2):
                        b = filled(act, ("z", y, hf, m))
                        A(sz[:, m, tok[hf]], ps[:, b, :], ACT.Silu).then_inc(read_b[b], 1)
                elif kind == "fd":
                    squares(y, hf)
                elif kind == "scale":
                    b = filled(act, ("rbc", y, hf))
                    if 2 * y + hf >= 1:
                        evacuated(act, ("hout", y if hf else 0, 1 - hf))
                    A(rb[:, :], ps[:, b, :], ACT.Copy).then_inc(read_b[b], 1)
                elif kind == "up" and hf == 1:
                    filled(act, ("hout", 1, 1))
                    w13_hi(("w13", 0), 0, ("lora3", "F", 0))
                    for c in range(KC):
                        ln_full(3, 0, c, modc[:, 32 + c:33 + c], modc[:, 28 + c:29 + c])

            def gate_unit(i, name, c, halves=(0, 1)):
                for hf in halves:
                    pn = ("g", *name, hf)
                    s = prods.at[pn][0] % 2
                    b = filled(act, ("h1", *name, hf), i)
                    A(full[:, s, :], ps[:, b, :], ACT.Silu).then_inc(read_b[b], 1)
                    evacuated(act, ("h3", *name, hf), i)
                    A(gT[0][:, bass.ds(c, 1), tok[hf]].rearrange("p o n -> p (o n)"), xnb[:, s, :], ACT.Copy)\
                        .then_inc(pr_hi, 1)

            filled(act, ("wup", NT - 1))
            w13_hi(("w13", 1), 1, ("lora3", "F", 1))
            for c in range(KC):
                ln_full(3, 1, c, modc[:, 32 + c:33 + c], modc[:, 28 + c:29 + c])
            ln_split(act, 3, 1)
            gate_unit(0, ("F", 0), 0, (0,))
            gate_unit(0, ("F", 1), 1, (0,))
            gate_unit(0, ("F", 0), 0, (1,))
            w13_hi(("w13", 2), 0, ("lora3", "F", 2))
            gate_unit(0, ("F", 1), 1, (1,))
            with act.Fori(0, HC1 // 2 - 1) as i:
                w13_hi(("w13", "L", 0), 1, ("lora3", "L", 0), i)
                gate_unit(i, ("L", 0), 2 * i + 2)
                w13_hi(("w13", "L", 1), 0, ("lora3", "L", 1), i)
                gate_unit(i, ("L", 1), 2 * i + 3)

            def w2_hi(c):
                act.wait_ge(w2_scaled, c + 1)
                A(W2[c][0], raw[:, piece_slot(("w2", c // 2)), D * (c % 2):D * (c % 2) + D], ACT.Copy).then_inc(w_hi, 1)

            for c in range(2):
                w2_hi(c)
            gate_unit(0, ("E", 0), HC1 - 1)
            for c in range(2, W2_AHEAD):
                w2_hi(c)
            filled(act, ("h3", "E", 0, 1))
            for c in range(W2_AHEAD, HC1):
                w2_hi(c)

        @block.vector
        def _(dve):
            V = nc.vector
            chain = Chain(dve, dve_c)
            link = chain.link
            tok = [slice(0, HALF), slice(HALF, T)]

            def ln_stat(hf, t):
                chain.tick(V.bn_stats(st[:, t, :], x[:, 4 * hf + t, :]))

            def ln_finish(L, hf):
                chain.wait()
                for t in range(4):
                    ins = V.bn_aggr(mv[:, hf, t, :], st[:, t, :])
                    if t < 3:
                        chain.tick(ins)
                link(ins)
                V.tensor_scalar(ve[:, :], mv[:, hf, :, 1], EPS, None, ALU.add).then_inc(ln_var, 1)

            def ln_norm(L, hf):
                dve.wait_ge(ln_rstd, 2 * L + hf + 1)
                if 2 * L + hf:
                    ln_split(dve, *divmod(2 * L + hf - 1, 2))
                for t in range(4):
                    V.tensor_scalar(xnb[:, t, :], x[:, 4 * hf + t, :], mv[:, hf, t, 0:1], rs[:, hf, t:t + 1],
                                    ALU.subtract, ALU.mult).then_inc(ln_xn, 1)

            def ln_hi_(L, hf, between=None):
                for c in range(KC):
                    n = 8 * L + 4 * hf + c
                    if c == 2 and between:
                        between()
                    evacuated(dve, ("ln", L, hf, c))
                    V.tensor_copy(hT[0][:, c, tok[hf]], turned_chunk(c)).then_inc(ln_hi, 1)
                    if c % 2:
                        dve.wait_ge(ln_hi, n + 1)
                        V.tensor_tensor(hT[1][:, c, tok[hf]], turned_chunk(c), hT[0][:, c, tok[hf]].bitcast(F32),
                                        ALU.subtract).then_inc(ln_lo_v, 1)

            def split_lo(order_n, job, hi, dst):
                dve.wait_ge(sp_hi, order_n + 1)
                b = banks.get(job)[0]
                V.tensor_tensor(dst, ps[:, b, :], hi.bitcast(F32), ALU.subtract).then_inc(read_b[b], 1)

            def floor_gate(v, tmp):
                link(V.tensor_scalar(tmp, v, 0.0, 2.0, ALU.is_ge, ALU.mult))
                link(V.scalar_tensor_tensor(out=v, in0=v, scalar=-1.0, in1=v, op0=ALU.mult, op1=ALU.max))
                link(V.tensor_scalar(v, v, 0.25, None, ALU.max))
                return V.scalar_tensor_tensor(out=v, in0=tmp, scalar=-1.0, in1=v, op0=ALU.add, op1=ALU.mult)

            V.memset(ones[:, :], 1.0).then_inc(consts, 1)
            V.memset(mh[:, :], -0.5).then_inc(consts, 1)
            V.memset(mxp[:, :, :, :], NEG).then_inc(maxp_init, 1)
            dve.wait_ge(c_exp, 1)
            link(V.tensor_scalar(sce[:, :], sce[:, :], 1.0, None, ALU.add))
            link(V.reciprocal(sce[:, :], sce[:, :]))
            V.tensor_tensor(sc32[:, :, :, :].rearrange("p k l m -> p l k m"),
                            cols[:, 0:8].rearrange("p (l k) -> p l k", l=2).unsqueeze(3).to_broadcast([P, 2, KC, 16]),
                            sce[:, 0:8].rearrange("p (l k) -> p l k", l=2).unsqueeze(3).to_broadcast([P, 2, KC, 16]),
                            ALU.mult).then_inc(c_silu, 1)
            V.tensor_scalar(alf[:, 0:1], sce[:, 8:9], 1.0, None, ALU.add).then_inc(consts, 1)
            V.tensor_scalar(alf[:, 1:2], sce[:, 8:9], -1.0, 1.0, ALU.mult, ALU.add).then_inc(consts, 1)
            V.memset(Kst[KROWS:KROWS + 3, 0:3, :], 1.0).then_inc(k_ones, 1)
            dve.wait_ge(consts, 4)

            def wq2_lo():
                dve.wait_ge(wq_hi, 3)
                V.tensor_tensor(Wqkv[1].rearrange("p c n -> p (c n)")[:, 2048:3072], wq2[:, :],
                                Wqkv[0].rearrange("p c n -> p (c n)")[:, 2048:3072].bitcast(F32),
                                ALU.subtract).then_inc(wq2_done, 1)

            def first_modulation():
                dve.wait_ge(ident_in, 16)
                V.tensor_copy(identb[:, :], ident[:, :]).then_inc(k_ones, 1)
                b = filled(dve, "mod0T")
                cview = ps[:, b, 0:256].rearrange("p (k q m) -> p q k m", k=2, m=32)[:, :, :, 0]
                link(V.tensor_copy(mod0c[:, 0:4].rearrange("p (q k) -> p q k", k=2), cview[:, 0:2, :]))
                V.tensor_scalar(mod0c[:, 4:8].rearrange("p (q k) -> p q k", k=2), cview[:, 2:4, :], 1.0, None, ALU.add)\
                    .then_inc(read_b[b], 1)

            for hf in range(2):
                dve.wait_ge(x_in[hf], 64)
                for t in range(4):
                    ln_stat(hf, t)
                ln_finish(0, hf)
                ln_norm(0, hf)
                if hf:
                    break
                V.memset(vr[:, :, 16:32], 1.0).then_inc(v_ones, 1)
                V.memset(Kst[KROWS:KROWS + 3, 3:NKV, :], 1.0).then_inc(k_ones, 1)
                first_modulation()
                ln_hi_(0, 0, wq2_lo)
            dve.wait_ge(mask_in, 16)
            link(V.tensor_copy(maskb[:, :, :].rearrange("p a b -> p (a b)"), rq[0][:, 0:2 * P]))
            ln_hi_(0, 1)

            dve.wait_ge(trig_in, 32)
            swap = [p ^ 8 for p in range(32)]
            for n in range(11):
                hf, m = divmod(n, 5)
                s = n % 2
                if n < 10:
                    b = filled(dve, ("qkv", hf, m))
                    V.stream_shuffle(rsw[:, s, :], ps[:, b, :], swap).then_inc(rope_sw, 1)
                    if n >= 3:
                        dve.wait_ge(part_l, n - 2)
                    V.tensor_tensor(rq[n % 3][:, :], ps[:, b, :], cosb[:, tok[hf]], ALU.mult).then_inc(read_b[b], 1)
                if n:
                    dve.wait_ge(part_h, n)
                    V.tensor_tensor(rq[(n - 1) % 3][:, :], rq[(n - 1) % 3][:, :], parts[(n - 1) % 3][:, 0, :], ALU.subtract)\
                        .then_inc(part_r, 1)
                if n < 10:
                    dve.wait_ge(rope_sin, n + 1)
                    evacuated(dve, ("qkv", hf, m))
                    V.tensor_tensor(rq[n % 3][:, :], rq[n % 3][:, :], rsw[:, s, :], ALU.add).then_inc(rope_q, 1)

            def s_unit(h, s):
                i, gp, kh = SUNITS[s]
                slot = s % 2
                w = width(s)
                dve.wait_ge(s_full, slots_before(h, s) + 1)
                V.tensor_reduce(mxp[:, kh, 2 * gp:2 * gp + 2, i], ps[:, 2 * slot:2 * slot + 2, 0:w], AXX, ALU.max)\
                    .then_inc(s_read, 1)

            def maxima(h):
                dve.wait_ge(s_read, slots_before(h, NS))
                V.tensor_tensor(nm[:, :], mxp[:, 0, :, :].rearrange("p g i -> p (g i)"),
                                mxp[:, 1, :, :].rearrange("p g i -> p (g i)"), ALU.max).then_inc(nm_ready, 1)
                dve.wait_ge(s_full, slots_before(h, NS) + 1)
                if not (isinstance(h, int) and h == 0):
                    dve.wait_ge(mrow_in, 48 * h)
                V.tensor_scalar(mt[:, 0, :], ps[0:32, 0, 0:P], -1.0, None, ALU.mult).then_inc(s_read, 1)
                dve.wait_ge(s_read, slots_before(h, NS) + 1)
                link(V.tensor_copy(mparts[:, 0, :], mt[:, 0, :]))
                link(V.tensor_tensor(mt[:, 1, :], mt[:, 0, :], mparts[:, 0, :], ALU.subtract))
                link(V.tensor_copy(mparts[:, 1, :], mt[:, 1, :]))
                V.tensor_tensor(mparts[:, 2, :], mt[:, 1, :], mparts[:, 1, :], ALU.subtract).then_inc(mt_parts, 1)
                dve.wait_ge(s_full, slots_before(h, NS + 1) + 1)
                if not (isinstance(h, int) and h == 0):
                    dve.wait_ge(modrow_out, 32 * h)
                V.tensor_copy(full[:, 0, 0:MODW // 4], ps[:, 2, 0:MODW // 4]).then_inc(s_read, 1)

            def ctx_norm(n):
                for b in range(2):
                    v = ps[:, 2 * b, :].rearrange("p (g i c) -> p g i c", g=G, c=32)
                    dve.wait_ge(s_full, ctx_at(n) + b + 1)
                    link(V.reciprocal(rec[:, b, :, :], v[:, :, :, 16]))
                    V.tensor_tensor(att[:, 4 * b:4 * b + 4, bass.ds(n * G * DH, G * DH)]
                                    .rearrange("p i (g d) -> p g i d", g=G),
                                    v[:, :, :, 0:DH], rec[:, b, :, :].unsqueeze(3).to_broadcast([P, G, 4, DH]),
                                    ALU.mult).then_inc(s_read, 1)

            def head_body(n, nxt, nxt2, ctx):
                for _, what, d, s in body_steps(nxt, nxt2, ctx):
                    if what == "s":
                        s_unit(n + d, s)
                    elif what == "max":
                        maxima(n + d)
                    elif what == "ctx":
                        ctx_norm(n - 1)

            evacuated(dve, ("vT", 1))
            dve.wait_ge(maxp_init, 1)
            for s in range(NS):
                s_unit(0, s)
            maxima(0)
            for s in range(AHEAD):
                s_unit(1, s)
            head_body(0, True, True, False)
            with dve.Fori(0, NKV - 3) as k:
                chain.enter(k, 5)
                head_body(k + 1, True, True, True)
            chain.leave(NKV - 3)
            head_body(NKV - 2, True, False, True)
            dve.wait_ge(ga_in, 16)
            floor_gate(gabc[:, :], gtmp[:, :]).then_inc(ga_ready, 1)
            head_body(NKV - 1, False, False, True)
            ctx_norm(NKV - 1)
            b = filled(dve, "modT")
            link(V.tensor_copy(modc[:, :], ps[:, b, 0:40]))
            for c0 in (8, 20):
                link(V.tensor_scalar(modc[:, c0:c0 + 4], modc[:, c0:c0 + 4], 1.0, None, ALU.add))
            V.tensor_scalar(modc[:, 32:36], modc[:, 32:36], 1.0, None, ALU.add).then_inc(read_b[b], 1)
            n = 0
            for hf in range(2):
                for c in range(KC):
                    split_lo(n, ("aT", hf, c), aTr[0][:, c, tok[hf]], aTr[1][:, c, tok[hf]])
                    n += 1

            def add_x(job, t, other):
                b = filled(dve, job)
                V.tensor_tensor(x[:, t, :], ps[:, b, :], other, ALU.add).then_inc(read_b[b], 1)
                return job

            for t in range(NT):
                add_x(("wo", t), t, x[:, t, :])
                if t % 4:
                    evacuated(dve, ("wo", t - 1))
                    ln_stat(t // 4, t % 4 - 1)
                if t % 4 == 3:
                    evacuated(dve, ("wo", t))
                    ln_stat(t // 4, 3)
                    ln_finish(1, t // 4)
                if t == 3:
                    dve.wait_ge(lpart_out, 48)
                    ln_norm(1, 0)
                if t == 5:
                    ln_hi_(1, 0)
            ln_norm(1, 1)

            for hf in range(2):
                if hf:
                    ln_hi_(1, 1)
                for m in range(2):
                    split_lo(n, ("fc1", hf, m), lat[0][:, m, tok[hf]], lat[1][:, m, tok[hf]])
                    n += 1
            b = filled(dve, "gateT")
            for t in range(NT):
                ins = V.max(top[:, t, :], ps[:, b, NE * t:NE * t + NE])
            ins.then_inc(read_b[b], 1)
            evacuated(dve, "gateT")
            V.tensor_tensor(s2[:, :], top[:, :, 0], top[:, :, 1], ALU.add).then_inc(s_top, 1)
            dve.wait_ge(ffbc_in, 48)
            link(floor_gate(gb0[:, :], gb0t[:, :]))
            link(V.tensor_tensor(bb[:, :], bb[:, :], gb0[:, :], ALU.mult))
            V.tensor_tensor(gg[:, :], gg[:, :], gb0[:, :], ALU.mult).then_inc(gg_ready, 1)
            with dve.Fori(0, HC0 // 2) as i:
                for j in range(2):
                    for hf in range(2):
                        name = ("up", j, hf)
                        k = prods.before(name, i)
                        s = prods.at[name][0] % 2
                        dve.wait_ge(pr_first, k + 1)
                        b = banks.at[name][0]
                        V.tensor_tensor(xnb[:, s, :], ps[:, b, :], full[:, s, :], ALU.mult).then_inc(read_b[b], 1)
                        dve.wait_ge(pr_hi, k + 1)
                        c = bass.ds(2 * i + j, 1)
                        V.tensor_tensor(u[1][:, c, tok[hf]].rearrange("p o n -> p (o n)"), xnb[:, s, :],
                                        u[0][:, c, tok[hf]].rearrange("p o n -> p (o n)").bitcast(F32),
                                        ALU.subtract).then_inc(pr_lo, 1)
            for hf in range(2):
                for m in range(2):
                    split_lo(n, ("eo", hf, m), eo[0][:, m, tok[hf]], eo[1][:, m, tok[hf]])
                    n += 1

            def mlp_norm(t):
                s = t % 2
                dve.wait_ge(y_rstd, t + 1)
                link(V.tensor_scalar(yb[:, s, :], yb[:, s, :], ymv[:, s, 0:1], yrs[:, s, :], ALU.subtract, ALU.mult))
                link(V.tensor_tensor(yb[:, s, :], yb[:, s, :], gg[:, :], ALU.mult))
                dve.wait_ge(bb_added, t + 1)
                V.tensor_tensor(x[:, t, :], x[:, t, :], yb[:, s, :], ALU.add).then_inc(x_mlp, 1)

            def mid_split(hf):
                evacuated(dve, ("mid", hf))
                link(V.tensor_copy(mid[0][:, tok[hf]], midf[:, tok[hf]]))
                V.tensor_tensor(mid[1][:, tok[hf]], midf[:, tok[hf]], mid[0][:, tok[hf]].bitcast(F32), ALU.subtract)\
                    .then_inc(mid_lo, 1)

            dve.wait_ge(gg_ready, 1)
            for t in range(NT + 1):
                if t == NT - 1:
                    ln_hi_(2, 0)
                if t < NT:
                    s = t % 2
                    evacuated(dve, ("routed", t))
                    b = filled(dve, ("shared", t))
                    if t >= 2:
                        dve.wait_ge(x_mlp, t - 1)
                    V.tensor_tensor(yb[:, s, :], ps[:, b, :], full[:, s, :], ALU.add).then_inc(read_b[b], 1)
                    evacuated(dve, ("shared", t))
                    link(V.bn_stats(yst[:, s, :], yb[:, s, :]))
                    link(V.bn_aggr(ymv[:, s, :], yst[:, s, :]))
                    V.tensor_scalar(yve[:, s, :], ymv[:, s, 1:2], EPS, None, ALU.add).then_inc(y_var, 1)
                if t:
                    mlp_norm(t - 1)
                if t == NT:
                    mid_split(0)
                if t >= 2:
                    dve.wait_ge(x_mlp, t - 1)
                    ln_stat((t - 2) // 4, (t - 2) % 4)
                if t == 5:
                    ln_finish(2, 0)
                    ln_norm(2, 0)
            dve.wait_ge(x_mlp, NT)
            ln_stat(1, 3)
            ln_finish(2, 1)
            ln_norm(2, 1)

            def merge(piece, jobs, turn=0):
                s = raw_loaded(dve, piece, turn)
                for which, job in enumerate(jobs):
                    b = filled(dve, job, turn)
                    r = raw[:, s, 512 * which:512 * which + 512]
                    V.scalar_tensor_tensor(out=r, in0=ps[:, b, :], scalar=2.0, in1=r, op0=ALU.mult, op1=ALU.add)\
                        .then_inc(read_b[b], 1)

            def centred(t):
                V.scalar_tensor_tensor(out=rt[:, t, :], in0=x[:, t, :], scalar=mv[:, t // 4, t % 4, 0:1], in1=Abc[:, :],
                                       op0=ALU.subtract, op1=ALU.mult).then_inc(rn_ready, 1)

            def rest(t):
                dve.wait_ge(xb_ready, t + 1)
                V.scalar_tensor_tensor(out=x[:, t, :], in0=rt[:, t, :], scalar=rs[:, t // 4, t % 4:t % 4 + 1],
                                       in1=x[:, t, :], op0=ALU.mult, op1=ALU.add).then_inc(r_ready, 1)

            def mean_squares(y, hf):
                b = filled(dve, ("ssq", y, hf))
                V.tensor_scalar(hms[:, :], ps[:, b, 0:4], 1.0 / DIN, EPS, ALU.mult, ALU.add).then_inc(read_b[b], 1)

            for kind, y, hf in MIXER:
                if kind == "in" and (y, hf) == (0, 0):
                    dve.wait_ge(ab_in, 64)
                    link(floor_gate(t36[:, :], rb[:, :]))
                elif kind == "in" and (y, hf) == (0, 1):
                    for t in range(4, NT):
                        centred(t)
                elif kind == "ln":
                    ln_hi_(2, 1)
                    link(V.tensor_tensor(Bbc[:, :], Bbc[:, :], t38[:, :], ALU.add))
                    link(V.tensor_tensor(Bbc[:, :], Bbc[:, :], t36[:, :], ALU.mult))
                    link(V.scalar_tensor_tensor(out=Abc[:, :], in0=Abc[:, :], scalar=1.0, in1=t36[:, :], op0=ALU.add,
                                                op1=ALU.mult))
                    for t in range(4):
                        centred(t)
                elif kind == "mid" and hf:
                    mid_split(1)
                elif kind == "fd":
                    for m in range(2):
                        n = 4 * y + 2 * hf + m
                        b = filled(dve, ("fd", y, hf, m))
                        if y:
                            dve.wait_ge(sq_ready, n - 3)
                        V.scalar_tensor_tensor(out=yz[:, m, tok[hf]], in0=ps[:, b, :], scalar=cols[:, C_D + m:C_D + m + 1],
                                               in1=xs[:, m, tok[hf]], op0=ALU.add, op1=ALU.mult).then_inc(read_b[b], 1)
                        evacuated(dve, ("z", y, hf, m))
                        evacuated(dve, ("fd", y, hf, m))
                        V.tensor_tensor(yz[:, m, tok[hf]], yz[:, m, tok[hf]], sz[:, m, tok[hf]], ALU.mult)\
                            .then_inc(yz_ready, 1)
                    for m in range(2):
                        n = 4 * y + 2 * hf + m
                        dve.wait_ge(yz_hi, n + 1)
                        V.tensor_tensor(yzr[1][:, m, tok[hf]], yz[:, m, tok[hf]], yzr[0][:, m, tok[hf]].bitcast(F32),
                                        ALU.subtract).then_inc(yz_lo, 1)
                elif kind == "rest":
                    for t in range(4 * hf, 4 * hf + 4):
                        rest(t)
                elif kind == "out" and (y, hf) != (1, 1):
                    mean_squares(y, hf)
                elif kind == "dg":
                    dve.wait_ge(mr_ready, 2 * y + hf + 1)
                    if 2 * y + hf:
                        filled(dve, ("rbc", y if hf else 0, 1 - hf))
                    V.tensor_tensor(dg[:, :, :], ident[:, :].unsqueeze(1).to_broadcast([P, 4, P]),
                                    hrs[:, :].unsqueeze(2).to_broadcast([P, 4, P]), ALU.mult).then_inc(dg_ready, 1)
                elif kind == "scale":
                    evacuated(dve, ("rbc", y, hf))
                    b = filled(dve, ("hout", y, hf))
                    o = hof[:, tok[hf]]
                    if y == 0:
                        V.tensor_tensor(o, ps[:, b, :], rb[:, :], ALU.mult).then_inc(read_b[b], 1)
                        evacuated(dve, ("hout", y, hf))
                    else:
                        V.scalar_tensor_tensor(out=o, in0=ps[:, b, :], scalar=alf[:, 1:2], in1=rb[:, :], op0=ALU.mult,
                                               op1=ALU.mult).then_inc(read_b[b], 1)
                        evacuated(dve, ("hout", y, hf))
                        link(V.scalar_tensor_tensor(out=o, in0=midf[:, tok[hf]], scalar=alf[:, 0:1], in1=o,
                                                    op0=ALU.mult, op1=ALU.add))
                    if y == 1:
                        filled(dve, ("z", 1, hf, 1))
                    link(V.tensor_copy(hob[0][:, tok[hf]], o))
                    V.tensor_tensor(hob[1][:, tok[hf]], o, hob[0][:, tok[hf]].bitcast(F32), ALU.subtract)\
                        .then_inc(ho_lo, 1)
                elif kind == "lora":
                    for c in range(2):
                        merge(("w13", c), [("lora", "F", c), ("lora3", "F", c)])
                    ln_norm(3, 0)
                elif kind == "up":
                    if hf:
                        ln_hi_(3, 0)
                    for t in range(4 * hf, 4 * hf + 4):
                        if hf == 0:
                            dve.wait_ge(r_ready, t + 1)
                        add_x(("wup", t), t, x[:, t, :])
                        if t % 4:
                            evacuated(dve, ("wup", t - 1))
                            ln_stat(hf, t % 4 - 1)
                        if t == 1:
                            mean_squares(1, 1)
                    evacuated(dve, ("wup", t))
                    ln_stat(hf, 3)
                    ln_finish(3, hf)
            ln_norm(3, 1)
            ln_hi_(3, 1)

            def gate_unit(i, name, c, halves=(0, 1)):
                for hf in halves:
                    pn = ("g", *name, hf)
                    k = prods.before(pn, i)
                    s = prods.at[pn][0] % 2
                    evacuated(dve, ("h1", *name, hf), i)
                    b = filled(dve, ("h3", *name, hf), i)
                    V.tensor_tensor(xnb[:, s, :], ps[:, b, :], full[:, s, :], ALU.mult).then_inc(read_b[b], 1)
                    dve.wait_ge(pr_hi, k + 1)
                    V.tensor_tensor(gT[1][:, bass.ds(c, 1), tok[hf]].rearrange("p o n -> p (o n)"), xnb[:, s, :],
                                    gT[0][:, bass.ds(c, 1), tok[hf]].rearrange("p o n -> p (o n)").bitcast(F32),
                                    ALU.subtract).then_inc(pr_lo, 1)

            gate_unit(0, ("F", 0), 0, (0,))
            gate_unit(0, ("F", 1), 1, (0,))
            gate_unit(0, ("F", 0), 0, (1,))
            merge(("w13", 2), [("lora", "F", 2), ("lora3", "F", 2)])
            gate_unit(0, ("F", 1), 1, (1,))
            with dve.Fori(0, HC1 // 2 - 1) as i:
                for j in range(2):
                    merge(("w13", "L", j), [("lora", "L", j), ("lora3", "L", j)], i)
                    gate_unit(i, ("L", j), 2 * i + 2 + j)
            dve.wait_ge(gb1_in, 16)
            floor_gate(gb1[:, :], gb1t[:, :]).then_inc(gb1_ready, 1)
            dve.wait_ge(gb1_ready, 1)

            def merge2(c):
                s = raw_loaded(dve, ("w2", c // 2))
                b = filled(dve, ("lora2", c))
                r = raw[:, s, D * (c % 2):D * (c % 2) + D]
                V.scalar_tensor_tensor(out=r, in0=ps[:, b, :], scalar=2.0, in1=r, op0=ALU.mult, op1=ALU.add)\
                    .then_inc(read_b[b], 1)
                evacuated(dve, ("lora2", c))
                V.tensor_tensor(r, r, gb1[:, :], ALU.mult).then_inc(w2_scaled, 1)

            for c in range(2):
                merge2(c)
            gate_unit(0, ("E", 0), HC1 - 1)
            for c in range(2, HC1):
                merge2(c)
            for q in range(2):
                for t in range(4):
                    add_x(("down", q, t), 4 * q + t, x[:, 4 * q + t, :])

        @block.gpsimd
        def _(pool):
            chain = Chain(pool, pool_c)
            link = chain.link
            tok = [slice(0, HALF), slice(HALF, T)]

            def tscopy(dst, src):
                return nc.gpsimd.tensor_scalar(dst, src, 1.0, 0.0, ALU.mult, ALU.add)

            def split(name, n, hi, lo, turn=0, loaded=False, last=True, at=0):
                s = piece_slot(name)
                if not loaded:
                    base, per = pieces.at[name]
                    wait_before(raw_in[s], 16 * (base // 2 + 1) + (8 * per * turn if per else 0))
                r = raw[:, s, at:at + n]
                link(tscopy(hi, r))
                ins = nc.gpsimd.tensor_tensor(lo, r, hi.bitcast(F32), ALU.subtract)
                if last:
                    ins.then_inc(piece_done, 1)

            count = nc.gpsimd.alloc_register("count_waited_for")

            def wait_before(sem_, value):
                if isinstance(value, int):
                    pool.wait_ge(sem_, value)
                else:
                    nc.gpsimd.reg_add(count, value, 0)
                    pool.wait_ge(consts, 1)
                    pool.wait_ge(sem_, count)

            def rstd(L, hf):
                pool.wait_ge(ln_var, 2 * L + hf + 1)
                nc.gpsimd.tensor_tensor(rs[:, hf, :], ve[:, :], mh[:, :], ALU.pow).then_inc(ln_rstd, 1)

            def ln_lo_(L, hf):
                for c in range(0, KC, 2):
                    n = 8 * L + 4 * hf + c
                    pool.wait_ge(ln_hi, n + 1)
                    nc.gpsimd.tensor_tensor(hT[1][:, c, tok[hf]], turned_chunk(c), hT[0][:, c, tok[hf]].bitcast(F32),
                                            ALU.subtract).then_inc(ln_lo_g, 1)

            wq = [w.rearrange("p c n -> p (c n)") for w in Wqkv]

            def wqkv_lo(k):
                pool.wait_ge(wq_hi, k + 1)
                cols_ = slice(1024 * k, 1024 * k + 1024)
                nc.gpsimd.tensor_tensor(wq[1][:, cols_], raw[:, piece_slot(("wqkv", k)), :], wq[0][:, cols_].bitcast(F32),
                                        ALU.subtract).then_inc(piece_done, 1)

            rstd(0, 0)
            wqkv_lo(0)
            wqkv_lo(1)
            ln_lo_(0, 0)
            rstd(0, 1)
            ln_lo_(0, 1)
            pool.wait_ge(trig_in, 32)
            for n in range(11):
                if n < 10:
                    pool.wait_ge(rope_sw, n + 1)
                    nc.gpsimd.tensor_tensor(rsw[:, n % 2, :], rsw[:, n % 2, :], sinb[:, tok[n // 5]], ALU.mult)\
                        .then_inc(rope_sin, 1)
                if n:
                    pool.wait_ge(part_m, n)
                    nc.gpsimd.tensor_tensor(parts[(n - 1) % 3][:, 2, :], rq[(n - 1) % 3][:, :], parts[(n - 1) % 3][:, 1, :],
                                            ALU.subtract).then_inc(part_l, 1)

            pool.wait_ge(lraw_in, 16)
            link(tscopy(lpart[:, 0, :], lraw[:, :]))
            link(nc.gpsimd.tensor_tensor(lraw[:, :], lraw[:, :], lpart[:, 0, :], ALU.subtract))
            link(tscopy(lpart[:, 1, :], lraw[:, :]))
            nc.gpsimd.tensor_tensor(lpart[:, 2, :], lraw[:, :], lpart[:, 1, :], ALU.subtract).then_inc(lpart_ready, 1)
            evacuated(pool, ("vT", 0))
            evacuated(pool, ("vT", 1))
            pool.wait_ge(v_ones, 1)

            def head_v(n):
                if not (isinstance(n, int) and n == 0):
                    wait_before(pv_done, n * NTU)
                nc.gpsimd.tensor_copy(vr[:, :, 0:DH], vtok[:, :, bass.ds(n * DH, DH)]).then_inc(vr_ready, 1)

            with pool.Fori(0, NKV - 1) as n:
                head_v(n)
            head_v(NKV - 1)
            for j in range(KC):
                k, half = divmod(j, 2)
                if j == 0:
                    pool.wait_ge(ga_ready, 1)
                    pool.wait_ge(part_l, 10)
                if half == 0:
                    raw_loaded(pool, ("wo", k))
                r = raw[:, piece_slot(("wo", k)), D * half:D * half + D]
                link(nc.gpsimd.tensor_tensor(r, r, gabc[:, :], ALU.mult))
                split(("wo", k), D, Wo[0][:, j, :], Wo[1][:, j, :], loaded=True, last=half == 1, at=D * half)

            split("fc1", 1024, Wf1[0].rearrange("p a b c -> p (a b c)"), Wf1[1].rearrange("p a b c -> p (a b c)"))
            pool.wait_ge(s_read, ctx_at(NKV - 1) + 2)
            split("gate", KC * NE, Wg[0].rearrange("p a b -> p (a b)"), Wg[1].rearrange("p a b -> p (a b)"))
            split("expert", 2 * LAT, Wex[0].rearrange("p a b -> p (a b)"), Wex[1].rearrange("p a b -> p (a b)"))
            rstd(1, 0)
            ln_lo_(1, 0)
            rstd(1, 1)
            ln_lo_(1, 1)

            def up_pieces(turn, j):
                c = 2 * turn + j
                s = piece_slot(("up", j))
                if isinstance(turn, int) and turn == 0:
                    filled(pool, ("fc1", 1, 1))
                else:
                    filled(pool, ("up", j, 1), turn - 1)
                split(("up", j), D, Wup[j][0].rearrange("p a b -> p (a b)"), Wup[j][1].rearrange("p a b -> p (a b)"),
                      turn)
                pool.wait_ge(dn_hi, c + 1)
                nc.gpsimd.tensor_tensor(Wd0[1][:, bass.ds(c, 1), :].rearrange("p o n -> p (o n)"),
                                        raw[:, piece_slot(("down", j)), 0:D],
                                        Wd0[0][:, bass.ds(c, 1), :].rearrange("p o n -> p (o n)").bitcast(F32),
                                        ALU.subtract).then_inc(piece_done, 1)

            for j in range(2):
                up_pieces(0, j)
            with pool.Fori(0, HC0 // 2 - 1) as i:
                chain.enter(i, 2)
                for j in range(2):
                    up_pieces(i + 1, j)
            chain.leave(HC0 // 2 - 1)
            for j in range(2):
                filled(pool, ("up", j, 1), HC0 // 2 - 1)
            split("fc2", 1024, Wf2[0].rearrange("p a b -> p (a b)"), Wf2[1].rearrange("p a b -> p (a b)"))
            split("wdown", D, Wdn[0].rearrange("p a b -> p (a b)"), Wdn[1].rearrange("p a b -> p (a b)"))
            split("hin", D, Whi[0].rearrange("p a b -> p (a b)"), Whi[1].rearrange("p a b -> p (a b)"))
            pool.wait_ge(gg_ready, 1)
            pool.wait_ge(ln_xn, 16)
            for t in range(NT):
                nc.gpsimd.tensor_tensor(x[:, t, :], x[:, t, :], bb[:, :], ALU.add).then_inc(bb_added, 1)
                pool.wait_ge(y_var, t + 1)
                nc.gpsimd.tensor_tensor(yrs[:, t % 2, :], yve[:, t % 2, :], mh[:, 0:1], ALU.pow).then_inc(y_rstd, 1)
                if t == 5:
                    rstd(2, 0)
                if t == 6:
                    ln_lo_(2, 0)
            rstd(2, 1)

            def rest(t):
                pool.wait_ge(rn_ready, t + 1)
                nc.gpsimd.tensor_tensor(x[:, t, :], x[:, t, :], Bbc[:, :], ALU.add).then_inc(xb_ready, 1)

            def w13_lo(slot, name, k):
                pool.wait_ge(w_hi, k + 1)
                nc.gpsimd.tensor_tensor(W13[slot][1].rearrange("p a b c -> p (a b c)"), raw[:, piece_slot(name), :],
                                        W13[slot][0].rearrange("p a b c -> p (a b c)").bitcast(F32),
                                        ALU.subtract).then_inc(piece_done, 1)

            split("fcd", D, Wfd[0].rearrange("p a b c -> p (a b c)"), Wfd[1].rearrange("p a b c -> p (a b c)"))
            raw_loaded(pool, "hout")
            s = piece_slot("hout")
            for k in range(2):
                r = raw[:, s, P * k:P * k + P]
                link(nc.gpsimd.tensor_scalar(r, r, cols[:, C_NW + k:C_NW + k + 1], 0.0, ALU.mult, ALU.add))
            split("hout", 2 * P, Who[0].rearrange("p a b -> p (a b)"), Who[1].rearrange("p a b -> p (a b)"), loaded=True)
            for kind, y, hf in MIXER_POOL:
                if kind == "ln":
                    ln_lo_(2, 1)
                elif kind == "in":
                    for m in range(2):
                        n = 4 * y + 2 * hf + m
                        pool.wait_ge(xs_hi, n + 1)
                        nc.gpsimd.tensor_tensor(xsr[1][:, m, tok[hf]], xs[:, m, tok[hf]],
                                                xsr[0][:, m, tok[hf]].bitcast(F32), ALU.subtract).then_inc(xs_lo, 1)
                    if y == 0:
                        for t in ((4, 5) if hf else range(4)):
                            rest(t)
                    elif hf == 0:
                        for t in range(6, 8):
                            rest(t)
                        raw_loaded(pool, "wup")
                        r = raw[:, piece_slot("wup"), 0:D]
                        link(nc.gpsimd.tensor_tensor(r, r, t36[:, :], ALU.mult))
                        split("wup", D, Wuo[0], Wuo[1], loaded=True)
                elif kind == "out":
                    evacuated(pool, ("ssq", y, hf))
                    nc.gpsimd.tensor_tensor(hrs[:, :], hms[:, :], mh[:, :], ALU.pow).then_inc(mr_ready, 1)
                elif kind == "up":
                    if hf:
                        w13_lo(0, ("w13", 0), 0)
                        ln_lo_(3, 0)
                        w13_lo(1, ("w13", 1), 1)
                    rstd(3, hf)
            ln_lo_(3, 1)

            w13_lo(0, ("w13", 2), 2)
            with pool.Fori(0, HC1 // 2 - 1) as i:
                w13_lo(1, ("w13", "L", 0), 2 * i + 3)
                w13_lo(0, ("w13", "L", 1), 2 * i + 4)
            for c in range(HC1):
                pool.wait_ge(w_hi, HC1 + c + 1)
                ins = nc.gpsimd.tensor_tensor(W2[c][1], raw[:, piece_slot(("w2", c // 2)), D * (c % 2):D * (c % 2) + D],
                                              W2[c][0].bitcast(F32), ALU.subtract)
                if c % 2 or c == HC1 - 1:
                    ins.then_inc(piece_done, 1)


def _rope(np):
    f = np.float32
    inv = f(1.0) / np.power(f(500000.0), np.arange(0, DH, 2, dtype=f) / f(DH)).astype(f)
    wavelen = f(2.0 * np.pi) / inv
    lo, hi = 1024 / 4.0, 1024 / 1.0
    scaled = np.where(wavelen > hi, inv / f(32.0), inv)
    smooth = (f(1024) / wavelen - f(1.0)) / f(3.0)
    smoothed = (f(1.0) - smooth) * scaled / f(32.0) + smooth * scaled
    scaled = np.where(~(wavelen < hi) & ~(wavelen > lo), smoothed, scaled).astype(f)
    angle = (np.arange(T, dtype=f)[:, None] * scaled[None, :]).astype(f).astype(np.float64)
    cos, sin = np.cos(angle).T, np.sin(angle).T
    return (np.tile(np.concatenate([cos, cos]), (NKV, 1)).astype(f),
            np.tile(np.concatenate([-sin, sin]), (NKV, 1)).astype(f))


def _layout(np, i):
    g = lambda name: np.asarray(i[name])
    c = np.ascontiguousarray
    d = {}

    def chunks(w):
        return c(w.reshape(-1, P, w.shape[1]).transpose(1, 0, 2)).reshape(P, -1)

    d["x"] = g("L0_attn_x").reshape(T, D)
    wq = g("L0_attn_Wq").T.reshape(D, NKV, G, DH).transpose(0, 2, 1, 3).reshape(D, D)
    d["wqkv"] = chunks(np.concatenate([wq, g("L0_attn_Wk").T, g("L0_attn_Wv").T], axis=1))
    d["wo"] = chunks(g("L0_attn_Wo").T)
    d["cos"], d["sin"] = _rope(np)
    d["ident"] = np.eye(P, dtype=np.float32)
    mask = np.where(np.arange(P)[:, None] >= np.arange(P)[None, :], 0.0, NEG).astype(np.float32)
    d["mask"] = c(np.concatenate([mask, mask.T], axis=1))
    m0, m1 = g("L0_wmod"), g("L1_wmod")
    d["wm0"] = chunks(m0[:, :1024])
    rest = np.concatenate([m0[:, 1024:], m1], axis=1)
    d["wmr"] = np.stack([chunks(rest[:, MODW * k:MODW * (k + 1)]) for k in range(8)])

    def col(v, n):
        return np.asarray(v).reshape(n, P).T

    gate1 = np.broadcast_to(g("L1_attn_gate1").reshape(1, 1), (P, 1))
    d["cols"] = c(np.concatenate([
        col(g("L0_c"), KC), col(g("L1_c"), KC), gate1, col(g("L1_attn_b_down"), 1),
        col(g("L1_attn_hy_conv_w")[:DIN, 0, 6], 2), col(g("L1_attn_hy_conv_b")[:DIN], 2),
        col(np.repeat(g("L1_attn_hy_D"), 64), 2), col(g("L1_attn_hy_norm_w"), 2)], axis=1))

    def outchunks(w):
        k, n = w.shape
        return c(w.reshape(k // P, P, n // P, P).transpose(2, 1, 0, 3)).reshape(n // P, P, k)

    d["fc1"] = c(outchunks(g("L0_ffn_fc1_w")).transpose(1, 0, 2)).reshape(P, -1)
    d["gate"] = chunks(g("L0_ffn_gate_w"))
    d["expert"] = chunks(g("L0_ffn_expert_w"))
    d["fc2"] = chunks(g("L0_ffn_fc2_w"))
    d["up"] = outchunks(g("L0_ffn_up_w"))
    d["down"] = g("L0_ffn_down_w").reshape(HC0, P, D)
    d["gamma"], d["beta"], d["bup"] = g("L0_ffn_ln_gamma"), g("L0_ffn_ln_beta"), g("L1_attn_b_up")
    d["wdown"] = chunks(g("L1_attn_w_down").T)
    d["hin"] = c(g("L1_attn_hy_in_w")[:2 * DIN].T)
    d["fcd"] = chunks(np.repeat(g("L1_attn_hy_fcD_w").T, 64, axis=1))
    d["hout"] = chunks(g("L1_attn_hy_out_w").T)
    d["wup"] = c(g("L1_attn_w_up").T)
    pad = HC1 * P - HID1

    def padrows(w):
        return np.concatenate([w, np.zeros((pad, w.shape[1]), w.dtype)], axis=0)

    w1, w3 = (outchunks(padrows(g(n)).T) for n in ("L1_ffn_w1", "L1_ffn_w3"))
    d["w13"] = c(np.concatenate([w1, w3], axis=2))
    w2 = padrows(g("L1_ffn_w2").T).reshape(HC1, P, D)
    w2 = np.concatenate([w2, np.zeros((W2_PIECES * 2 - HC1, P, D), w2.dtype)], axis=0)
    d["w2"] = c(w2.reshape(W2_PIECES, 2, P, D).transpose(0, 2, 1, 3)).reshape(W2_PIECES, P, 2 * D)
    d["lora"] = c(np.concatenate([
        g("L1_ffn_lora_A1"), g("L1_ffn_lora_A3"), padrows(g("L1_ffn_lora_A2").T).T,
        padrows(g("L1_ffn_lora_B1")).T, padrows(g("L1_ffn_lora_B3")).T, g("L1_ffn_lora_B2").T],
        axis=1)).reshape(P, -1)
    return d


def kernel(**inputs):
    import numpy as _np
    import concourse.bacc as _bacc
    from concourse import mybir as _mybir
    from concourse.bass_utils import run_bass_kernel_spmd as _run

    nc = _bacc.Bacc("TRN2", target_bir_lowering=False, num_devices=1)
    arrays, args = {}, {}
    for name, v in _layout(_np, inputs).items():
        arrays[f"in_{name}"] = _np.ascontiguousarray(v)
        args[name] = nc.dram_tensor(f"in_{name}", v.shape, _mybir.dt.from_np(v.dtype), kind="ExternalInput").ap()
    out = nc.dram_tensor("out_x", (T, D), _mybir.dt.float32, kind="ExternalOutput").ap()
    adaln_two_blocks(nc, args, out)
    r = _run(nc, [arrays], core_ids=[0])
    return _np.asarray(r.results[0]["out_x"]).reshape(1, T, D)
```
